# Optimizing a Trainium2 kernel written in Bass

```python
import numpy as np
import jax
import jax.numpy as jnp

def _softmax(x, axis=-1):
    return jax.nn.softmax(x, axis=axis)

def _gelu(x):
    return jax.nn.gelu(x, approximate=True)

def _silu(x):
    return jax.nn.silu(x)

def _sigmoid(x):
    return jax.nn.sigmoid(x)

def _layernorm(x, axis=-1, eps=1e-05):
    m = jnp.mean(x, axis=axis, keepdims=True)
    v = jnp.var(x, axis=axis, keepdims=True)
    return (x - m) / jnp.sqrt(v + eps)

def _scatter_add(tgt, idx, src, axis=0):
    return tgt.at[idx].add(src)

def _segment_sum(src, seg, n):
    return jax.ops.segment_sum(src, seg, n)
kernel_name = 'mk_vit_tower_cls_d1_tok_img768_r4_82a422'

def setup_inputs(seed: int=0):
    np.random.seed(seed)
    _w = jnp.asarray

    def _rec_inputs():
        import jax
        import jax.numpy as jnp
        _rk = jax.random.key(seed)
        x = -0.000147625 + 0.999875 * jax.random.normal(jax.random.fold_in(_rk, 1), (64, 12, 224, 224), jnp.float32)
        cls_tok = 0.02 * jax.random.normal(jax.random.fold_in(_rk, 5), (1, 1, 192), jnp.float32)
        return (x, cls_tok)
    x, cls_tok = _rec_inputs()

    def _L0_tok_setup():
        import jax, jax.numpy as jnp
        import numpy as np
        IMG = 224
        PATCH = 16
        EMBED = 192
        C = 12
        B = 64
        key = jax.random.key(seed)
        k1, k2 = jax.random.split(key)
        x = jax.random.normal(k1, (B, C, IMG, IMG), dtype=jnp.float32)
        channel_weights = jax.random.normal(k2, (C, EMBED), dtype=jnp.float32)
        return {'x': x, 'channel_weights': channel_weights}
    _L0_tok_all = _L0_tok_setup()
    _L0_tok_in = {k: v for k, v in _L0_tok_all.items() if k in ('channel_weights',)}
    del _L0_tok_all

    def _L0_attn_setup():
        import jax, jax.numpy as jnp
        import numpy as np
        N_HEAD = 12
        N_EMBD = 192
        key = jax.random.key(seed)
        k1, k2, k3 = jax.random.split(key, 3)
        B, T, C = (4, 512, N_EMBD)
        x = jax.random.normal(k1, (B, T, C), dtype=jnp.float32)
        w_attn = jax.random.normal(k2, (C, 3 * C), dtype=jnp.float32) * C ** (-0.5)
        b_attn = jnp.zeros((3 * C,), dtype=jnp.float32)
        w_proj = jax.random.normal(k3, (C, C), dtype=jnp.float32) * C ** (-0.5)
        b_proj = jnp.zeros((C,), dtype=jnp.float32)
        return {'x': x, 'w_attn': w_attn, 'b_attn': b_attn, 'w_proj': w_proj, 'b_proj': b_proj}
    _L0_attn_all = _L0_attn_setup()
    _L0_attn_in = {k: v for k, v in _L0_attn_all.items() if k in ('w_attn', 'b_attn', 'w_proj', 'b_proj')}
    del _L0_attn_all

    def _L0_ffn_setup():
        import jax, jax.numpy as jnp
        import numpy as np
        DIM = 192
        NUM_HEADS = 12
        HEAD_DIM = DIM // NUM_HEADS
        SCALE = HEAD_DIM ** (-0.5)
        NUM_EXPERTS = 8
        RANK = 16
        ALPHA = 32
        TOPK = 2
        SCALING = ALPHA / RANK
        B, S = (8, 256)
        key = jax.random.key(seed)
        ks = jax.random.split(key, 12)
        d, e, r = (DIM, NUM_EXPERTS, RANK)
        inp = {'x': jax.random.normal(ks[0], (B, S, d), jnp.float32), 'Wg': jax.random.normal(ks[1], (e, d), jnp.float32) * 0.02, 'bg': jax.random.normal(ks[2], (e,), jnp.float32) * 0.02, 'Wqkv': jax.random.normal(ks[3], (3 * d, d), jnp.float32) * 0.02, 'bqkv': jax.random.normal(ks[4], (3 * d,), jnp.float32) * 0.02, 'Wproj': jax.random.normal(ks[5], (d, d), jnp.float32) * 0.02, 'bproj': jax.random.normal(ks[6], (d,), jnp.float32) * 0.02, 'A': jax.random.normal(ks[7], (e, r, d), jnp.float32) * 0.05, 'ba': jax.random.normal(ks[8], (e, r), jnp.float32) * 0.02, 'Bm': jax.random.normal(ks[9], (e, 3 * d, r), jnp.float32) * 0.05, 'bb': jax.random.normal(ks[10], (e, 3 * d), jnp.float32) * 0.02}
        return inp
    _L0_ffn_all = _L0_ffn_setup()
    _L0_ffn_in = {k: v for k, v in _L0_ffn_all.items() if k in ('Wg', 'bg', 'Wqkv', 'bqkv', 'Wproj', 'bproj', 'A', 'ba', 'Bm', 'bb')}
    del _L0_ffn_all
    return {'x': x, 'cls_tok': cls_tok, 'L0_tok_channel_weights': _L0_tok_in['channel_weights'], 'L0_attn_w_attn': _L0_attn_in['w_attn'], 'L0_attn_b_attn': _L0_attn_in['b_attn'], 'L0_attn_w_proj': _L0_attn_in['w_proj'], 'L0_attn_b_proj': _L0_attn_in['b_proj'], 'L0_ffn_Wg': _L0_ffn_in['Wg'], 'L0_ffn_bg': _L0_ffn_in['bg'], 'L0_ffn_Wqkv': _L0_ffn_in['Wqkv'], 'L0_ffn_bqkv': _L0_ffn_in['bqkv'], 'L0_ffn_Wproj': _L0_ffn_in['Wproj'], 'L0_ffn_bproj': _L0_ffn_in['bproj'], 'L0_ffn_A': _L0_ffn_in['A'], 'L0_ffn_ba': _L0_ffn_in['ba'], 'L0_ffn_Bm': _L0_ffn_in['Bm'], 'L0_ffn_bb': _L0_ffn_in['bb']}

def reference(x, cls_tok, L0_tok_channel_weights, L0_attn_w_attn, L0_attn_b_attn, L0_attn_w_proj, L0_attn_b_proj, L0_ffn_Wg, L0_ffn_bg, L0_ffn_Wqkv, L0_ffn_bqkv, L0_ffn_Wproj, L0_ffn_bproj, L0_ffn_A, L0_ffn_ba, L0_ffn_Bm, L0_ffn_bb):
    import jax
    import jax.numpy as jnp

    def _L0_tok_ref(x, channel_weights):
        import jax, jax.numpy as jnp
        import numpy as np
        IMG = 224
        PATCH = 16
        EMBED = 192
        C = 12
        B = 64
        Bb, Cc, H, W = x.shape
        K = PATCH
        n = H // K
        pooled = x.reshape(Bb, Cc, n, K, n, K).sum(axis=(3, 5))
        out = jnp.einsum('bcij,ce->bije', pooled, channel_weights)
        return out.reshape(Bb, n * n, EMBED)

    def _L0_attn_ref(x, w_attn, b_attn, w_proj, b_proj):
        import jax, jax.numpy as jnp
        import numpy as np
        N_HEAD = 12
        N_EMBD = 192
        B, T, C = x.shape
        H = N_HEAD
        D = C // H
        qkv = x @ w_attn + b_attn
        q, k, v = jnp.split(qkv, 3, axis=-1)
        q = q.reshape(B, T, H, D).transpose(0, 2, 1, 3)
        k = k.reshape(B, T, H, D).transpose(0, 2, 1, 3)
        v = v.reshape(B, T, H, D).transpose(0, 2, 1, 3)
        scores = jnp.einsum('bhqd,bhkd->bhqk', q, k) * C ** (-0.5)
        causal = jnp.triu(jnp.ones((T, T), dtype=bool), k=1)
        scores = jnp.where(causal, -jnp.inf, scores)
        attn = jax.nn.softmax(scores, axis=-1)
        out = jnp.einsum('bhqk,bhkd->bhqd', attn, v)
        out = out.transpose(0, 2, 1, 3).reshape(B, T, C)
        return out @ w_proj + b_proj

    def _L0_ffn_ref(x, Wg, bg, Wqkv, bqkv, Wproj, bproj, A, ba, Bm, bb):
        import jax, jax.numpy as jnp
        import numpy as np
        DIM = 192
        NUM_HEADS = 12
        HEAD_DIM = DIM // NUM_HEADS
        SCALE = HEAD_DIM ** (-0.5)
        NUM_EXPERTS = 8
        RANK = 16
        ALPHA = 32
        TOPK = 2
        SCALING = ALPHA / RANK
        B, S = (8, 256)
        b, s, d = x.shape
        t = b * s
        xf = x.reshape(t, d)
        probs = jax.nn.softmax(xf @ Wg.T + bg, axis=-1)
        top_w, top_idx = jax.lax.top_k(probs, TOPK)
        combine = jnp.zeros((t, NUM_EXPERTS), x.dtype).at[jnp.arange(t)[:, None], top_idx].add(top_w)
        h = jnp.einsum('td,erd->ter', xf, A) + ba
        hw = h * combine[:, :, None]
        delta = jnp.einsum('ter,eor->to', hw, Bm) + combine @ bb
        delta = delta * SCALING
        qkv = xf @ Wqkv.T + bqkv + delta
        qkv = qkv.reshape(b, s, 3, NUM_HEADS, HEAD_DIM)
        qkv = jnp.transpose(qkv, (2, 0, 3, 1, 4))
        q, k, v = (qkv[0], qkv[1], qkv[2])
        attn = jax.nn.softmax(jnp.einsum('bhsd,bhtd->bhst', q, k) * SCALE, axis=-1)
        out = jnp.einsum('bhst,bhtd->bhsd', attn, v)
        out = jnp.transpose(out, (0, 2, 1, 3)).reshape(b, s, d)
        return out @ Wproj.T + bproj
    h = _L0_tok_ref(x, L0_tok_channel_weights)
    h = jnp.concatenate([jnp.broadcast_to(cls_tok, (h.shape[0], 1, h.shape[2])), h], axis=1)
    h = h + _L0_attn_ref(_layernorm(h, axis=-1), L0_attn_w_attn, L0_attn_b_attn, L0_attn_w_proj, L0_attn_b_proj)
    h = h + _L0_ffn_ref(_layernorm(h, axis=-1), L0_ffn_Wg, L0_ffn_bg, L0_ffn_Wqkv, L0_ffn_bqkv, L0_ffn_Wproj, L0_ffn_bproj, L0_ffn_A, L0_ffn_ba, L0_ffn_Bm, L0_ffn_bb)
    return h

_drawn_inputs = setup_inputs


def setup_inputs(seed=0):
    import zlib

    import numpy as np

    out = dict(_drawn_inputs(seed))
    spreads = {'L0_attn_b_attn': (0.0, 0.8), 'L0_attn_b_proj': (0.0, 0.8)}
    factors = {'cls_tok': 8.0,
     'L0_attn_w_attn': 8.0,
     'L0_attn_w_proj': 8.0,
     'L0_ffn_Wg': 8.0,
     'L0_ffn_bg': 8.0,
     'L0_ffn_Wqkv': 8.0,
     'L0_ffn_bqkv': 8.0,
     'L0_ffn_Wproj': 8.0,
     'L0_ffn_bproj': 200.0,
     'L0_ffn_A': 8.0,
     'L0_ffn_ba': 8.0,
     'L0_ffn_Bm': 8.0,
     'L0_ffn_bb': 8.0}
    for name, (base, spread) in spreads.items():
        noise = np.random.default_rng([zlib.crc32(name.encode()), seed]).standard_normal(out[name].shape)
        drawn = base * np.exp(spread * noise) if base else spread * noise
        out[name] = jnp.asarray(drawn.astype(out[name].dtype))
    for name, factor in factors.items():
        out[name] = (out[name] * factor).astype(out[name].dtype)
    return out
```

```python
from contextlib import ExitStack

import concourse.bass as bass
from concourse import mybir

F32 = mybir.dt.float32
F32R = mybir.dt.float32r
BF16 = mybir.dt.bfloat16
I32 = mybir.dt.int32
U32 = mybir.dt.uint32
ALU = mybir.AluOpType
ACT = mybir.ActivationFunctionType
AX = mybir.AxisListType

PE_STEPS = ["pooled", "st2_0", "gram", "st2_1", "var", "st2_2", "spread", "st2_3", "qk1", "v1", "mx1_0",
            "st2_4", "mx1_1", "st2_5", "mx1_2", "mx1_3", "av2", "mx1_4", "xt", "out2", "mt1",
            "route", "st1_0", "st1_1", "hwt", "st1_2", "qk2", "v2", "st1_3", "mx2_0", "mx2_1",
            "av1", "mx2_2", "mx2_3", "out1", "mx2_4", "mx2_5", "mt2"]
ACT_STEPS = ["pooled", "st2_0", "st2_1", "st2_2", "st2_3", "q1r", "q1", "v1", "st2_4", "st2_5",
             "ln2", "inv2", "xt0", "xtb", "mt1", "st1_0", "rexp", "st1_1", "hwt", "c2t", "st1_2", "q2r", "q2", "v2",
             "st1_3", "ln1", "inv1", "h1", "mt2"]
DVE_STEPS = ["prod", "vare", "rstok", "ptn", "k1", "mx1_0", "mx1_1", "mx1_2", "mx1_3", "sh2", "t2", "n2", "o2", "mx1_4",
             "fin2",
             "rmax", "rsub", "rsum", "rinv", "rprob", "rtop0", "rtop1", "ridx0", "ridx1", "ridxf",
             "rone0", "rone1", "rtwo0", "rtwo1", "rcomb", "hw",
             "pool0", "pool1", "pool2",
             "k2", "mx2_0", "mx2_1", "sh1", "t1", "n1", "o1", "mx2_2", "mx2_3",
             "bs0", "bs1", "ba0", "ba1", "var1", "xh0", "xh1", "mx2_4", "mx2_5"]
POOL_STEPS = ["rstd", "kr1_0", "kr1_1", "kz1_0", "kz1_1", "h1b",
              "kr2_0", "kr2_1", "kz2_0", "kz2_1", "rs", "big0", "big1", "big2"]

READERS = {
    "pooled": [("act", "pooled")], "gram": [("dve", "prod")], "var": [("dve", "vare")], "spread": [("dve", "ptn")],
    "qk1": [("act", "q1"), ("dve", "k1")], "v1": [("act", "v1")],
    "xt": [("act", "xtb")], "route": [("dve", "hw")], "hwt": [("act", "c2t")],
    "qk2": [("act", "q2"), ("dve", "k2")], "v2": [("act", "v2")],
    "mt1": [("act", "mt1")], "mt2": [("act", "mt2")],
    "av1": [("dve", "o1")], "av2": [("dve", "o2")],
    "out1": [("act", "h1")], "out2": [("dve", "fin2")],
}
for _n in range(6):
    READERS[f"st2_{_n}"] = [("act", f"st2_{_n}")]
    READERS[f"mx2_{_n}"] = [("dve", f"mx2_{_n}")]
for _n in range(5):
    READERS[f"mx1_{_n}"] = [("dve", f"mx1_{_n}")]
for _n in range(4):
    READERS[f"st1_{_n}"] = [("act", f"st1_{_n}")]

STEPS = {"pe": PE_STEPS, "act": ACT_STEPS, "dve": DVE_STEPS, "pool": POOL_STEPS}


def at(it, engine, step, back=0):
    steps = STEPS[engine]
    return it * len(steps) + (len(steps) * (1 - back) + steps.index(step) + 1)


def build(nc, x, cls_tok, cw, w_attn, b_attn, w_proj, b_proj, Wg, bg, Wqkv, bqkv, Wproj, bproj,
          A, ba, Bm, bb, out):
    B, C, IMG, _ = x.shape
    D = cw.shape[1]
    H = 12
    DH = D // H
    P = 16
    NP = IMG // P
    T = NP * NP + 1
    TP = 256
    T0, T1 = 128, T - 128
    E, RANK = A.shape[0], A.shape[1]
    G = 6
    GR = G * DH
    KR = GR + G
    SL = 256
    NQ = C + 2
    CT = 4
    XP = CT * NP * 2
    XT = C // CT
    XF = (P // 2) * IMG
    EPS = 1e-5
    N_IT = B + 2
    SCALING = 2.0
    SC1 = float(D) ** -0.5
    SC2 = float(DH) ** -0.5
    NEG = -1e30

    with ExitStack() as ctx:
        def sb(name, shape, dt=F32):
            return ctx.enter_context(nc.sbuf_tensor(name, shape, dt))

        def sem(name):
            return ctx.enter_context(nc.semaphore(name))

        slots = [ctx.enter_context(nc.psum_tensor(f"slot{i}", [128, 4 * SL], F32)) for i in range(4)]
        slot = {s: slots[i % 4] for i, s in enumerate(PE_STEPS)}

        def tiles(step, parts=128):
            return slot[step][0:parts, :].rearrange("p (t c) -> p t c", c=SL)

        ident = sb("ident", [128, 128])
        ident_b = sb("ident_b", [128, 128], BF16)
        causal = sb("causal", [128, 128], BF16)
        minus_half = sb("minus_half", [128, 1])
        causal_t = sb("causal_t", [128, 128], BF16)
        head_mask = sb("head_mask", [GR, G])
        patch_c = sb("patch_c", [XP, CT, NP])
        patch_mask = sb("patch_mask", [XP, NP])
        chan_sel = sb("chan_sel", [XP, XT, NQ])
        row_sel = sb("row_sel", [2, NQ], BF16)
        row_val = sb("row_val", [2, T], BF16)
        var_ones = sb("var_ones", [C + 1, 1])
        iota_i = sb("iota_i", [128, E], I32)
        iota_f = sb("iota_f", [128, E])
        h0_w = sb("h0_w", [NQ, D])
        cen = sb("cen", [C + 1, D])
        cen_sum = sb("cen_sum", [C + 1, 1])
        cen_t = sb("cen_t", [128, 2, NQ])
        gram_w = sb("gram_w", [C + 1, C + 1])
        wa = sb("wa", [128, 2, 3 * D])
        w1 = sb("w1", [NQ, 3 * D])
        wp1 = sb("wp1", [128, 3, D])
        wp2 = sb("wp2", [128, 3, D])
        nat_q = sb("nat_q", [GR, 6, D])
        nat_b = sb("nat_b", [GR, 6, E * RANK])
        nat_p = sb("nat_p", [GR, 2, 3, 4, 32])
        nat_a = sb("nat_a", [128, D])
        nat_g = sb("nat_g", [E, D])
        wx = sb("wx", [128, 3 * D])
        wb = sb("wb", [104, 3 * D])
        wh = sb("wh", [128, 3 * D])
        rx = sb("rx", [128, 128 + E])
        rb = sb("rb", [65, 128 + E])
        xs = sb("xs", [XP, XT, XF])
        part = sb("part", [XP, XT, NP])
        big = sb("big", [XP, XT, NP * NP])
        pt = sb("pt", [NQ, TP])
        prod = sb("prod", [C + 1, TP])
        tok_var = sb("tok_var", [128, 2])
        rstd_tok = sb("rstd_tok", [128, 2, NQ])
        ptn = sb("ptn", [NQ, TP])
        q_t = [sb(f"q_t{n}", [KR, 2, T]) for n in (1, 2)]
        q_r = [sb(f"q_r{n}", [GR, 2, T + 1], F32R) for n in (1, 2)]
        k_t = [sb(f"k_t{n}", [GR, 2, T]) for n in (1, 2)]
        kz = [sb(f"kz{n}", [128, H, T]) for n in (1, 2)]
        kr = [sb(f"kr{n}", [GR, H, T + 1], F32R) for n in (1, 2)]
        va = [sb(f"va{n}", [128, 2, H, 32]) for n in (1, 2)]
        mx = [sb(f"mx{n}", [128, 2, H]) for n in (1, 2)]
        p0 = [sb(f"p0_{n}", [128, H, T]) for n in (1, 2)]
        p1 = [sb("p1_1", [T1, H, T1]), sb("p1_2", [T1, H, T])]
        den = sb("den", [128, 3, T])
        lnd = sb("lnd", [128, 3, T])
        inv = sb("inv", [128, 3, T])
        o_t = [sb(f"o_t{n}", [128, 3, TP]) for n in (1, 2)]
        h1 = sb("h1", [128, 2, D])
        h1b = sb("h1b", [128, 2, D])
        bst = sb("bst", [128, 2, 6])
        bag = sb("bag", [128, 2, 2])
        rstd = sb("rstd", [128, 2, 1])
        xh = sb("xh", [128, 2, D])
        xt0 = sb("xt0", [128, TP])
        xtb = sb("xtb", [104, TP])
        hwt = sb("hwt", [128, TP])
        rm = sb("rm", [128, 2])
        rl = sb("rl", [128, 2, E])
        re = sb("re", [128, 2, E])
        rs = sb("rs", [128, 2])
        ri = sb("ri", [128, 2])
        rp = sb("rp", [128, 2, E])
        rt = sb("rt", [128, 2, 8])
        rx_u = sb("rx_u", [128, 2, 8], U32)
        rx_f = sb("rx_f", [128, 2, 8])
        one_h = sb("one_h", [128, 2, E])
        two_h = sb("two_h", [128, 2, E])
        c2 = sb("c2", [128, 2, E])
        hw = sb("hw", [128, 2, E, RANK])
        y = sb("y", [128, 2, D])

        pe_done, act_done, dve_done, pool_done = (sem(s) for s in ("pe_done", "act_done", "dve_done", "pool_done"))
        done = {"pe": pe_done, "act": act_done, "dve": dve_done, "pool": pool_done}
        cleared = sem("cleared")
        loaded = sem("loaded")
        x_in = [sem(f"x_in{t}") for t in range(XT)]
        out_stored = sem("out_stored")
        const_ready = sem("const_ready")
        prep_dve = sem("prep_dve")
        prep_pe = sem("prep_pe")
        prep_act = sem("prep_act")
        prep_pool = sem("prep_pool")
        ready = sem("ready")

        N_LOADS = 0
        loads = []

        def load(dst, src):
            loads.append((dst, src))

        load(h0_w[0:C, :], cw)
        load(h0_w[C:C + 1, :], cls_tok.rearrange("a b d -> (a b) d"))
        load(h0_w[C + 1:C + 2, :], b_proj.rearrange("(a d) -> a d", a=1))
        load(cen[0:C, :], cw)
        load(cen[C:C + 1, :], cls_tok.rearrange("a b d -> (a b) d"))
        load(wa[:, 0, :], w_attn[0:128, :])
        load(wa[0:D - 128, 1, :], w_attn[128:D, :])
        load(w1[C + 1:C + 2, :], b_attn.rearrange("(a d) -> a d", a=1))
        wp_src = w_proj.rearrange("(t j d) n -> j d t n", j=4, d=DH)
        for j in range(4):
            load(wp1[32 * j:32 * j + DH, :, :], wp_src[j])
        load(nat_q[:, :, :], Wqkv.rearrange("(m p) d -> p m d", p=GR))
        bm_src = Bm.rearrange("e (m p) r -> m p e r", p=GR)
        pr_src = Wproj.rearrange("(m p) (t j d) -> m p t j d", p=GR, j=4, d=DH)
        for m in range(6):
            load(nat_b[:, m, :].rearrange("p (e r) -> p e r", e=E), bm_src[m])
        for m in range(2):
            for t in range(3):
                load(nat_p[:, m, t, :, 0:DH], pr_src[m, :, t])
            load(nat_p[:, m, 0, 0, DH:DH + 1], bproj.rearrange("(m p a) -> m p a", p=GR, a=1)[m])
        load(nat_a[:, :], A.rearrange("e r d -> (e r) d"))
        load(nat_g[:, :], Wg)
        load(wb[64:65, :], bqkv.rearrange("(a d) -> a d", a=1))
        load(wb[96:96 + E, :], bb)
        load(rb[64:65, 0:128], ba.rearrange("(a e) r -> a (e r)", a=1))
        load(rb[64:65, 128:128 + E], bg.rearrange("(a e) -> a e", a=1))

        def x_tile(image, t):
            return x[bass.ds(image, 1), CT * t:CT * (t + 1)].rearrange(
                "b c (i h r) w -> (b c i h) (r w)", h=2, r=P // 2)

        N_READY = 4
        paused = {n: sem(f"{n}_paused") for n in ("pool", "pe", "dve")}

        def hold(e, name):
            e.sem_inc(paused[name], 1)

        block = ctx.enter_context(nc.Block())

        @block.sync
        def _(sp):
            for t in range(XT):
                sp.dma_start(xs[:, t, :], x_tile(0, t)).then_inc(x_in[t], 16)
            sp.wait_ge(cleared, 1)
            for dst, src in loads:
                sp.dma_start(dst, src).then_inc(loaded, 16)
            for t in range(XT):
                sp.wait_ge(prep_dve, 1 + t)
                sp.dma_start(xs[:, t, :], x_tile(1, t)).then_inc(x_in[t], 16)
            sp.sem_inc(out_stored, 32)
            with sp.Fori(0, N_IT) as it:
                image = sp.snap((it + 2) % B)
                o_img = sp.snap((it + (B - 2)) % B)
                sp.wait_ge(dve_done, at(it, "dve", "fin2"))
                sp.dma_start(out[bass.ds(o_img, 1), 0:T0].rearrange("b t d -> (b t) d"),
                             y[:, 0, :]).then_inc(out_stored, 16)
                sp.dma_start(out[bass.ds(o_img, 1), T0:T].rearrange("b t d -> (b t) d"),
                             y[0:T1, 1, :]).then_inc(out_stored, 16)
                for t in range(XT):
                    sp.wait_ge(dve_done, at(it, "dve", f"pool{t}"))
                    sp.dma_start(xs[:, t, :], x_tile(image, t)).then_inc(x_in[t], 16)
            sp.wait_ge(out_stored, 32 * (N_IT + 1))
            for t in range(XT):
                sp.wait_ge(x_in[t], 16 * (N_IT + 2))

        @block.gpsimd
        def _(pool):
            n = [0]

            def step(ins):
                n[0] += 1
                ins.then_inc(prep_pool, 1)
                pool.wait_ge(prep_pool, n[0])

            for tile in (wp1, nat_p, wb):
                pool.memset(tile[:], 0.0).then_inc(prep_pool, 1)
            n[0] += 3
            pool.wait_ge(prep_pool, 3)
            pool.sem_inc(cleared, 1)
            for tile, v in ((ident, 0.0), (causal, 0.0), (causal_t, 0.0), (minus_half, -0.5), (head_mask, 1.0), (patch_c, 1.0), (chan_sel, 1.0),
                            (row_sel, 0.0), (row_val, 1.0), (var_ones, 1.0), (rstd_tok, 1.0), (prod, 0.0),
                            (kz[0], 0.0), (kz[1], 0.0), (q_t[1], 0.0), (va[0], 1.0), (va[1], 1.0),
                            (h1, 0.0), (h1b, 0.0), (xh, 0.0), (pt, 0.0), (ptn, 0.0), (o_t[0], 0.0),
                            (o_t[1], 0.0), (xt0, 0.0), (xtb, 0.0), (hwt, 0.0)):
                pool.memset(tile[:], v).then_inc(prep_pool, 1)
                n[0] += 1
            for i in range(2):
                pool.memset(kr[i][:, :, T:T + 1].bitcast(F32), 0.0).then_inc(prep_pool, 1)
                n[0] += 1
            pool.iota(iota_i[:], pattern=[[1, E]], base=0, channel_multiplier=0).then_inc(prep_pool, 1)
            n[0] += 1
            pool.wait_ge(prep_pool, n[0])

            def select(tile, op, fill, base, pattern, cm):
                step(pool.affine_select(out=tile, in_=tile, compare_op=op, fill=fill, base=base,
                                        pattern=pattern, channel_multiplier=cm))

            select(ident[:], ALU.not_equal, 1.0, 0, [[-1, 128]], 1)
            select(causal[:], ALU.is_ge, NEG, 0, [[-1, 128]], 1)
            select(causal_t[:], ALU.is_ge, NEG, 0, [[1, 128]], -1)
            select(head_mask[:], ALU.is_ge, 0.0, 0, [[-DH, G]], 1)
            select(head_mask[:], ALU.is_ge, 0.0, DH - 1, [[DH, G]], -1)
            select(patch_c[:], ALU.is_ge, 0.0, 0, [[-2 * NP, CT], [-2, NP]], 1)
            select(patch_c[:], ALU.is_ge, 0.0, 1, [[2 * NP, CT], [2, NP]], -1)
            select(chan_sel[:], ALU.is_ge, 0.0, 0, [[XP, XT], [-2 * NP, NQ]], 1)
            select(chan_sel[:], ALU.is_ge, 0.0, 2 * NP - 1, [[-XP, XT], [2 * NP, NQ]], -1)
            select(row_sel[:], ALU.not_equal, 1.0, C, [[-1, NQ]], 1)
            select(row_val[:], ALU.is_ge, 0.0, 0, [[-1, T]], 1000)
            for i in range(2):
                for g in range(2):
                    select(kz[i][GR:128, G * g:G * g + G, :], ALU.not_equal, 1.0, 0, [[-1, G], [0, T]], 1)
            step(pool.memset(xtb[64:65, :], 1.0))
            step(pool.tensor_copy(ident_b[:], ident[:]))
            step(pool.tensor_copy(iota_f[:], iota_i[:]))
            pool.sem_inc(const_ready, 1)
            pool.wait_ge(prep_dve, 4)
            for t in range(XT):
                step(pool.tensor_tensor(
                    big[:, t, :].rearrange("p (i j) -> p i j", i=NP),
                    part[:, t, :].unsqueeze(1).broadcast_to([XP, NP, NP]),
                    patch_mask[:, :].unsqueeze(2).broadcast_to([XP, NP, NP]), ALU.mult))
            pool.sem_inc(pool_done, len(POOL_STEPS))
            pool.sem_inc(ready, 1)
            pool.wait_ge(ready, N_READY)

            with pool.Fori(0, N_IT) as it:
                def scatter(i, k_step):
                    pool.wait_ge(dve_done, at(it, "dve", k_step))
                    for dst in (kr[i], kz[i]):
                        for g in range(2):
                            pool.tensor_tensor(
                                dst[0:GR, G * g:G * g + G, 0:T],
                                k_t[i][:, g, :].unsqueeze(1).broadcast_to([GR, G, T]),
                                head_mask[:, :].unsqueeze(2).broadcast_to([GR, G, T]),
                                ALU.mult).then_inc(pool_done, 1)

                pool.wait_ge(dve_done, at(it, "dve", "vare"))
                hold(pool, "pool")
                pool.tensor_tensor(tok_var[:], tok_var[:], minus_half[:, :].broadcast_to([128, 2]), ALU.pow).then_inc(pool_done, 1)
                scatter(0, "k1")
                pool.wait_ge(dve_done, at(it, "dve", "fin2"))
                pool.wait_ge(act_done, at(it, "act", "h1", 1))
                hold(pool, "pool")
                pool.tensor_copy(h1b[:], h1[:]).then_inc(pool_done, 1)
                scatter(1, "k2")
                pool.wait_ge(dve_done, at(it, "dve", "var1"))
                hold(pool, "pool")
                pool.tensor_tensor(rstd[:], rstd[:], minus_half[:, :].unsqueeze(1).broadcast_to([128, 2, 1]), ALU.pow).then_inc(pool_done, 1)
                pool.wait_ge(pe_done, at(it, "pe", "pooled"))
                for t in range(XT):
                    pool.wait_ge(dve_done, at(it, "dve", f"pool{t}"))
                    pool.tensor_tensor(
                        big[:, t, :].rearrange("p (i j) -> p i j", i=NP),
                        part[:, t, :].unsqueeze(1).broadcast_to([XP, NP, NP]),
                        patch_mask[:, :].unsqueeze(2).broadcast_to([XP, NP, NP]),
                        ALU.mult).then_inc(pool_done, 1)

        @block.tensor
        def _(pe):
            pe.wait_ge(const_ready, 1)
            pe.wait_ge(loaded, 16 * len(loads))
            pe.wait_ge(prep_dve, 7)
            for c, (a, b) in enumerate(((0, 128), (128, D))):
                ins = pe.transpose(slots[0][0:b - a, SL * c:SL * c + C + 1], cen[:, a:b], ident[0:C + 1, 0:C + 1])
            ins.then_inc(prep_pe, 1)
            for m in range(6):
                if m >= 1:
                    pe.wait_ge(prep_act, 3 * m)
                pe.transpose(slots[1][:, 0:GR], nat_q[:, m, 0:128], ident[0:GR, 0:GR])
                pe.transpose(slots[2][0:D - 128, 0:GR], nat_q[:, m, 128:D], ident[0:GR, 0:GR])
                pe.transpose(slots[3][:, 0:GR], nat_b[:, m, :], ident[0:GR, 0:GR]).then_inc(prep_pe, 1)
            for m in range(2):
                for t in range(3):
                    pe.wait_ge(prep_act, 18 + 3 * m + t)
                    pe.transpose(slots[1][:, 0:GR], nat_p[:, m, t].rearrange("p j d -> p (j d)"),
                                 ident[0:GR, 0:GR]).then_inc(prep_pe, 1)
            pe.wait_ge(prep_act, 24)
            pe.transpose(slots[1][:, 0:128], nat_a[:, 0:128], ident[:])
            pe.transpose(slots[1][:, 128:128 + E], nat_g[:, 0:128], ident[0:E, 0:E])
            pe.transpose(slots[2][0:D - 128, 0:128], nat_a[:, 128:D], ident[:])
            pe.transpose(slots[2][0:D - 128, 128:128 + E], nat_g[:, 128:D], ident[0:E, 0:E]).then_inc(prep_pe, 1)
            pe.wait_ge(prep_dve, 9)
            pe.wait_ge(prep_act, 26)
            for half in range(2):
                cols = slice(3 * D // 2 * half, 3 * D // 2 * (half + 1))
                for c, n in enumerate((128, D - 128)):
                    pe.matmul(slots[3][0:C + 1, 2 * SL * half:2 * SL * half + 3 * D // 2],
                              cen_t[0:n, c, 0:C + 1], wa[0:n, c, cols], start=(c == 0), stop=(c == 1))
            for c, n in enumerate((128, D - 128)):
                ins = pe.matmul(slots[1][0:C + 1, 0:C + 1], cen_t[0:n, c, 0:C + 1], cen_t[0:n, c, 0:C + 1],
                                start=(c == 0), stop=(c == 1))
            ins.then_inc(prep_pe, 1)
            pe.sem_inc(pe_done, len(PE_STEPS))
            pe.sem_inc(ready, 1)
            pe.wait_ge(ready, N_READY)

            with pe.Fori(0, N_IT) as it:
                def claim(step):
                    i = PE_STEPS.index(step)
                    p = i - 4 if i >= 4 else max(k for k in range(len(PE_STEPS)) if k % 4 == i % 4)
                    for engine, reader in READERS[PE_STEPS[p]]:
                        pe.wait_ge(done[engine], at(it, engine, reader, int(p > i)))

                def shifted(n, step, heads, keys, queries):
                    claim(step)
                    k0, k1 = keys
                    for i, h in enumerate(heads):
                        if k0 and n == 0:
                            dst = slot[step][0:k1 - k0, 512 * (i // G) + 80 * (i % G):512 * (i // G) + 80 * (i % G) + T - queries]
                        else:
                            dst = slot[step][0:k1 - k0, SL * i:SL * i + T]
                        ins = pe.matmul(dst, kz[n][0:KR, h, k0:k1], q_t[n][:, h // G, queries:T], start=True, stop=(n == 1))
                        if n == 0:
                            w = k1 - k0
                            ins = pe.matmul(dst[:, 0:w], ident_b[0:w, 0:w], causal_t[0:w, 0:w], start=False, stop=True)
                    ins.then_inc(pe_done, 1)

                def raw(n, step, tile, heads):
                    q0, q1, nk = ((0, T0, T0) if n == 0 else (0, T0, T + 1)) if tile == 0 else (T0, T, T + 1)
                    if n == 0 and tile == 0:
                        for b in range(len(heads) // 4):
                            bank = slot[step][:, 512 * b:512 * b + 512].rearrange("p (h k) -> p h k", h=4)
                            pe.matmul(bank, ident_b[:], causal[:].unsqueeze(1).broadcast_to([128, 4, 128]),
                                      start=True, stop=False)
                            for k in range(2):
                                h = heads[4 * b + 2 * k]
                                ins = pe.matmul(bank[:, 2 * k:2 * k + 2, :], q_r[n][:, h // G, q0:q1],
                                                kr[n][:, h:h + 2, 0:nk], start=False, stop=(k == 1))
                        ins.then_inc(pe_done, 1)
                        return
                    rows = q1 - q0
                    for k in range(0, len(heads), 2):
                        h = heads[k]
                        pair = slot[step][0:rows, SL * k:SL * k + 2 * SL].rearrange("p (h k) -> p h k", h=2)
                        ins = pe.matmul(pair[:, :, 0:nk], q_r[n][:, h // G, q0:q1], kr[n][:, h:h + 2, 0:nk],
                                        start=True, stop=(n == 1))
                        if n == 0:
                            ins = pe.matmul(pair[:, :, T0:T], ident_b[0:rows, 0:rows],
                                            causal[0:rows, 0:T1].unsqueeze(1).broadcast_to([rows, 2, T1]),
                                            start=False, stop=True)
                    ins.then_inc(pe_done, 1)

                def turn_maxima(n, step):
                    claim(step)
                    for g in range(2):
                        pe.transpose(slot[step][0:G, SL * g:SL * g + T0], mx[n][:, 0, G * g:G * g + G], ident[:])
                        ins = pe.transpose(slot[step][0:G, SL * g + T0:SL * g + T], mx[n][0:T1, 1, G * g:G * g + G],
                                           ident[0:T1, 0:T1])
                    ins.then_inc(pe_done, 1)

                def values(n, step):
                    claim(step)
                    q1 = T0 if n == 0 else 0
                    for t in range(3):
                        for j in range(4):
                            pe.matmul(slot[step][32 * j:32 * j + 32, SL * t:SL * t + T], va[n][:, 0, 4 * t + j, :],
                                      p0[n][:, 4 * t + j, :], start=True, stop=False)
                        for j in range(4):
                            ins = pe.matmul(slot[step][32 * j:32 * j + 32, SL * t + q1:SL * t + T],
                                            va[n][0:T1, 1, 4 * t + j, :], p1[n][:, 4 * t + j, :], start=False, stop=True)
                    ins.then_inc(pe_done, 1)

                claim("pooled")
                pe.wait_ge(pool_done, at(it, "pool", "big2", 1))
                hold(pe, "pe")
                pe.matmul(slot["pooled"][0:NQ, 0:T], row_sel[:], row_val[:], start=True, stop=False)
                for t in range(XT):
                    ins = pe.matmul(slot["pooled"][0:NQ, 1:T], chan_sel[:, t, :], big[:, t, :],
                                    start=False, stop=(t == XT - 1))
                ins.then_inc(pe_done, 1)
                pe.wait_ge(act_done, at(it, "act", "mt2", 1))
                pe.wait_ge(pool_done, at(it, "pool", "kz2_1", 1))
                shifted(1, "st2_0", [0, 1, 2, 3], (0, T0), 0)
                claim("gram")
                pe.wait_ge(act_done, at(it, "act", "pooled"))
                hold(pe, "pe")
                pe.matmul(slot["gram"][0:C + 1, 0:T], gram_w[:], pt[0:C + 1, 0:T], start=True, stop=True).then_inc(pe_done, 1)
                shifted(1, "st2_1", [4, 5, 6, 7], (0, T0), 0)
                claim("var")
                pe.wait_ge(dve_done, at(it, "dve", "prod"))
                hold(pe, "pe")
                for t in range(2):
                    ins = pe.matmul(slot["var"][:, t:t + 1], prod[:, 128 * t:128 * t + 128], var_ones[:],
                                    start=True, stop=True)
                ins.then_inc(pe_done, 1)
                shifted(1, "st2_2", [8, 9, 10, 11], (0, T0), 0)
                claim("spread")
                pe.wait_ge(dve_done, at(it, "dve", "rstok"))
                for t, (a, b) in enumerate(((0, T0), (T0, T))):
                    ins = pe.matmul(slot["spread"][0:NQ, a:b], rstd_tok[0:b - a, t, :], ident[0:b - a, 0:b - a],
                                    start=True, stop=True)
                ins.then_inc(pe_done, 1)
                shifted(1, "st2_3", [0, 1, 2, 3], (T0, T), 0)
                claim("qk1")
                pe.wait_ge(dve_done, at(it, "dve", "ptn"))
                for m in range(4):
                    ins = pe.matmul(slot["qk1"][0:GR, SL * m:SL * m + T], w1[:, GR * m:GR * m + GR], ptn[:, 0:T],
                                    start=True, stop=True)
                ins.then_inc(pe_done, 1)
                claim("v1")
                for t in range(2):
                    ins = pe.matmul(slot["v1"][:, SL * t:SL * t + D], ptn[:, 128 * t:128 * t + 128], w1[:, 2 * D:3 * D],
                                    start=True, stop=True)
                ins.then_inc(pe_done, 1)
                claim("mx1_0")
                pe.wait_ge(act_done, at(it, "act", "q1r"))
                pe.wait_ge(pool_done, at(it, "pool", "kr1_1"))
                raw(0, "mx1_0", 0, list(range(0, 8)))
                shifted(1, "st2_4", [4, 5, 6, 7], (T0, T), 0)
                claim("mx1_1")
                raw(0, "mx1_1", 0, list(range(8, 12)))
                shifted(1, "st2_5", [8, 9, 10, 11], (T0, T), 0)
                claim("mx1_2")
                raw(0, "mx1_2", 1, [0, 1, 2, 3])
                claim("mx1_3")
                raw(0, "mx1_3", 1, [4, 5, 6, 7])
                pe.wait_ge(act_done, at(it, "act", "st2_5"))
                values(1, "av2")
                claim("mx1_4")
                raw(0, "mx1_4", 1, [8, 9, 10, 11])
                claim("xt")
                pe.wait_ge(dve_done, at(it, "dve", "xh1", 1))
                for t in range(2):
                    pe.transpose(slot["xt"][:, 128 * t:128 * t + 128], xh[:, t, 0:128], ident[:])
                for t in range(2):
                    ins = pe.transpose(slot["xt"][0:D - 128, SL + 128 * t:SL + 128 * t + 128], xh[:, t, 128:D], ident[:])
                ins.then_inc(pe_done, 1)
                claim("out2")
                pe.wait_ge(dve_done, at(it, "dve", "o2"))
                for tt in range(2):
                    for t in range(3):
                        ins = pe.matmul(slot["out2"][:, SL * tt:SL * tt + D], o_t[1][:, t, 128 * tt:128 * tt + 128],
                                        wp2[:, t, :], start=(t == 0), stop=(t == 2))
                ins.then_inc(pe_done, 1)
                pe.wait_ge(dve_done, at(it, "dve", "mx1_4"))
                turn_maxima(0, "mt1")
                claim("route")
                pe.wait_ge(act_done, at(it, "act", "xtb"))
                for tt in range(2):
                    tok = slice(128 * tt, 128 * tt + 128)
                    pe.matmul(slot["route"][:, SL * tt:SL * tt + 128 + E], xt0[:, tok], rx[:], start=True, stop=False)
                    ins = pe.matmul(slot["route"][:, SL * tt:SL * tt + 128 + E], xtb[0:65, tok], rb[:],
                                    start=False, stop=True)
                ins.then_inc(pe_done, 1)
                pe.wait_ge(act_done, at(it, "act", "mt1"))
                pe.wait_ge(pool_done, at(it, "pool", "kz1_1"))
                shifted(0, "st1_0", [0, 1, 2, 3], (0, T0), 0)
                shifted(0, "st1_1", [4, 5, 6, 7], (0, T0), 0)
                claim("hwt")
                pe.wait_ge(dve_done, at(it, "dve", "hw"))
                for tt in range(2):
                    pe.transpose(slot["hwt"][:, 128 * tt:128 * tt + 128], hw[:, tt].rearrange("p e r -> p (e r)"), ident[:])
                for tt in range(2):
                    ins = pe.transpose(slot["hwt"][0:E, SL + 128 * tt:SL + 128 * tt + 128], c2[:, tt, :], ident[:])
                ins.then_inc(pe_done, 1)
                shifted(0, "st1_2", [8, 9, 10, 11], (0, T0), 0)
                chunks = ((xt0, wx, 128), (xtb, wb, 104), (hwt, wh, 128))
                claim("qk2")
                pe.wait_ge(act_done, at(it, "act", "c2t"))
                for m in range(4):
                    for c, (act_rows, w, k) in enumerate(chunks):
                        ins = pe.matmul(slot["qk2"][0:GR, SL * m:SL * m + T], w[0:k, GR * m:GR * m + GR],
                                        act_rows[0:k, 0:T], start=(c == 0), stop=(c == 2))
                ins.then_inc(pe_done, 1)
                claim("v2")
                for tt in range(2):
                    for c, (act_rows, w, k) in enumerate(chunks):
                        ins = pe.matmul(slot["v2"][:, SL * tt:SL * tt + D], act_rows[0:k, 128 * tt:128 * tt + 128],
                                        w[0:k, 2 * D:3 * D], start=(c == 0), stop=(c == 2))
                ins.then_inc(pe_done, 1)
                shifted(0, "st1_3", list(range(H)), (T0, T), T0)
                claim("mx2_0")
                pe.wait_ge(act_done, at(it, "act", "q2r"))
                pe.wait_ge(pool_done, at(it, "pool", "kr2_1"))
                raw(1, "mx2_0", 0, [0, 1, 2, 3])
                claim("mx2_1")
                raw(1, "mx2_1", 0, [4, 5, 6, 7])
                pe.wait_ge(act_done, at(it, "act", "st1_3"))
                values(0, "av1")
                claim("mx2_2")
                raw(1, "mx2_2", 0, [8, 9, 10, 11])
                claim("mx2_3")
                raw(1, "mx2_3", 1, [0, 1, 2, 3])
                claim("out1")
                pe.wait_ge(dve_done, at(it, "dve", "o1"))
                for tt in range(2):
                    tok = slice(128 * tt, 128 * tt + 128)
                    pe.matmul(slot["out1"][:, SL * tt:SL * tt + D], pt[:, tok], h0_w[:], start=True, stop=False)
                    for t in range(3):
                        ins = pe.matmul(slot["out1"][:, SL * tt:SL * tt + D], o_t[0][:, t, tok], wp1[:, t, :],
                                        start=False, stop=(t == 2))
                ins.then_inc(pe_done, 1)
                claim("mx2_4")
                raw(1, "mx2_4", 1, [4, 5, 6, 7])
                claim("mx2_5")
                raw(1, "mx2_5", 1, [8, 9, 10, 11])
                pe.wait_ge(dve_done, at(it, "dve", "mx2_5"))
                turn_maxima(1, "mt2")

        @block.scalar
        def _(act):
            for m in range(6):
                cols = slice(GR * m, GR * m + GR)
                act.wait_ge(prep_pe, m + 2)
                act.activation(wx[:, cols], slots[1][:, 0:GR], ACT.Copy).then_inc(prep_act, 1)
                act.activation(wb[0:D - 128, cols], slots[2][0:D - 128, 0:GR], ACT.Copy).then_inc(prep_act, 1)
                act.activation(wh[:, cols], slots[3][:, 0:GR], ACT.Copy, scale=SCALING).then_inc(prep_act, 1)
            for m in range(2):
                for t in range(3):
                    act.wait_ge(prep_pe, 8 + 3 * m + t)
                    act.activation(wp2[:, t, GR * m:GR * m + GR], slots[1][:, 0:GR], ACT.Copy).then_inc(prep_act, 1)
            act.wait_ge(prep_pe, 14)
            act.activation(rx[:], slots[1][:, 0:128 + E], ACT.Copy).then_inc(prep_act, 1)
            act.activation(rb[0:D - 128, :], slots[2][0:D - 128, 0:128 + E], ACT.Copy).then_inc(prep_act, 1)
            act.wait_ge(prep_pe, 15)
            act.activation(w1[0:C + 1, :].rearrange("p (h n) -> p h n", h=2),
                           slots[3][0:C + 1, :].rearrange("p (h n) -> p h n", h=2)[:, :, 0:3 * D // 2],
                           ACT.Copy).then_inc(prep_act, 1)
            act.activation(gram_w[:], slots[1][0:C + 1, 0:C + 1], ACT.Copy, scale=1.0 / D).then_inc(prep_act, 1)
            act.wait_ge(prep_act, 28)
            act.sem_inc(act_done, len(ACT_STEPS))
            act.sem_inc(ready, 1)
            act.wait_ge(ready, N_READY)

            with act.Fori(0, N_IT) as it:
                def copy(dst, src, scale=1.0):
                    act.activation(dst, src, ACT.Copy, scale=scale).then_inc(act_done, 1)

                def after(step):
                    act.wait_ge(pe_done, at(it, "pe", step))

                def exps2(c):
                    after(f"st2_{c}")
                    rows, dst = (128, p0[1]) if c < 3 else (T1, p1[1])
                    h = 4 * (c % 3)
                    act.activation(dst[0:rows, h:h + 4, :], tiles(f"st2_{c}", rows)[:, :, 0:T], ACT.Exp,
                                   scale=SC2).then_inc(act_done, 1)

                def inverse(n):
                    act.wait_ge(dve_done, at(it, "dve", f"sh{n}"))
                    act.activation(lnd[:], den[:], ACT.Ln).then_inc(act_done, 1)
                    act.wait_ge(act_done, at(it, "act", f"ln{n}"))
                    act.activation(inv[:], lnd[:], ACT.Exp, scale=-1.0).then_inc(act_done, 1)

                def exps1(c):
                    after(f"st1_{c}")
                    act.activation(p0[0][:, 4 * c:4 * c + 4, :], tiles(f"st1_{c}")[:, :, 0:T], ACT.Exp,
                                   scale=SC1).then_inc(act_done, 1)

                after("pooled")
                copy(pt[:, 0:T], slot["pooled"][0:NQ, 0:T])
                exps2(0)
                exps2(1)
                exps2(2)
                exps2(3)
                after("qk1")
                copy(q_r[0][:, :, 0:T], tiles("qk1", GR)[:, 0:2, 0:T])
                copy(q_t[0][0:GR, :, :], tiles("qk1", GR)[:, 0:2, 0:T])
                after("v1")
                copy(va[0][:, :, :, 0:DH], tiles("v1")[:, 0:2, 0:D].rearrange("p t (h d) -> p t h d", h=H))
                exps2(4)
                exps2(5)
                inverse(2)
                after("xt")
                copy(xt0[:], slot["xt"][:, 0:SL])
                copy(xtb[0:D - 128, :], slot["xt"][0:D - 128, SL:2 * SL])
                after("mt1")
                copy(q_t[0][GR:KR, :, :], tiles("mt1", G)[:, 0:2, 0:T], -1.0)
                exps1(0)
                act.wait_ge(dve_done, at(it, "dve", "rsub"))
                act.activation(re[:], rl[:], ACT.Exp).then_inc(act_done, 1)
                exps1(1)
                after("hwt")
                copy(hwt[:], slot["hwt"][:, 0:SL])
                copy(xtb[96:96 + E, :], slot["hwt"][0:E, SL:2 * SL])
                exps1(2)
                after("qk2")
                copy(q_r[1][:, :, 0:T], tiles("qk2", GR)[:, 0:2, 0:T])
                copy(q_t[1][0:GR, :, :], tiles("qk2", GR)[:, 0:2, 0:T])
                after("v2")
                copy(va[1][:, :, :, 0:DH], tiles("v2")[:, 0:2, 0:D].rearrange("p t (h d) -> p t h d", h=H))
                after("st1_3")
                act.activation(
                    p1[0][:].rearrange("p (b h) q -> p b h q", b=2),
                    slot["st1_3"][0:T1, :].rearrange("p (b n) -> p b n", b=2)[:, :, 0:80 * G].rearrange(
                        "p b (h n) -> p b h n", h=G)[:, :, :, 0:T1],
                    ACT.Exp, scale=SC1).then_inc(act_done, 1)
                inverse(1)
                after("out1")
                act.wait_ge(pool_done, at(it, "pool", "h1b"))
                copy(h1[:], tiles("out1")[:, 0:2, 0:D])
                after("mt2")
                copy(q_t[1][GR:KR, :, :], tiles("mt2", G)[:, 0:2, 0:T], -1.0)

        @block.vector
        def _(dve):
            def pooling(t):
                return dve.tensor_reduce(part[:, t, :], xs[:, t, :].rearrange("p (r j w) -> p j r w", r=P // 2, w=P),
                                         AX.XY, ALU.add)

            for t in range(XT):
                dve.wait_ge(x_in[t], 16)
                pooling(t).then_inc(prep_dve, 1)
            dve.wait_ge(const_ready, 1)
            dve.tensor_reduce(patch_mask[:], patch_c[:].rearrange("p c i -> p i c"), AX.X, ALU.add).then_inc(prep_dve, 1)
            dve.wait_ge(loaded, 16 * len(loads))
            dve.tensor_reduce(cen_sum[:], cen[:], AX.X, ALU.add).then_inc(prep_dve, 1)
            dve.wait_ge(prep_dve, 5)
            dve.tensor_scalar(cen_sum[:], cen_sum[:], 1.0 / D, None, ALU.mult).then_inc(prep_dve, 1)
            dve.wait_ge(prep_dve, 6)
            dve.tensor_scalar(cen[:], cen[:], cen_sum[:, 0:1], None, ALU.subtract).then_inc(prep_dve, 1)
            dve.wait_ge(prep_pe, 1)
            dve.tensor_copy(cen_t[:, 0, 0:C + 1], slots[0][:, 0:C + 1]).then_inc(prep_dve, 1)
            dve.tensor_copy(cen_t[0:D - 128, 1, 0:C + 1], slots[0][0:D - 128, SL:SL + C + 1]).then_inc(prep_dve, 1)
            dve.tensor_scalar(wb[96:96 + E, :], wb[96:96 + E, :], SCALING, None, ALU.mult).then_inc(prep_dve, 1)
            dve.wait_ge(prep_dve, 10)
            dve.sem_inc(dve_done, len(DVE_STEPS))
            dve.sem_inc(ready, 1)
            dve.wait_ge(ready, N_READY)

            with dve.Fori(0, N_IT) as it:
                def after(step):
                    dve.wait_ge(pe_done, at(it, "pe", step))

                def own(step):
                    dve.wait_ge(dve_done, at(it, "dve", step))

                def inc(ins):
                    ins.then_inc(dve_done, 1)

                def maxima1(c):
                    after(f"mx1_{c}")
                    if c < 2:
                        heads = 8 if c == 0 else 4
                        src = slot[f"mx1_{c}"][:, 0:128 * heads].rearrange("p (h k) -> p h k", h=heads)
                        inc(dve.tensor_reduce(mx[0][:, 0, 8 * c:8 * c + heads], src, AX.X, ALU.max))
                    else:
                        h = 4 * (c - 2)
                        inc(dve.tensor_reduce(mx[0][0:T1, 1, h:h + 4], tiles(f"mx1_{c}", T1)[:, :, 0:T], AX.X, ALU.max))

                def maxima2(c):
                    after(f"mx2_{c}")
                    rows, h = (128 if c < 3 else T1), 4 * (c % 3)
                    inc(dve.tensor_reduce(mx[1][0:rows, c // 3, h:h + 4], tiles(f"mx2_{c}", rows)[:, :, 0:T], AX.X, ALU.max))

                def normalise(n, step):
                    after(step)
                    hold(dve, "dve")
                    inc(dve.stream_shuffle(den[:], tiles(step)[:, 0:3, 0:T], [16 + i % 16 for i in range(32)]))
                    dve.wait_ge(act_done, at(it, "act", f"inv{n + 1}"))
                    inc(dve.tensor_tensor(den[:], den[:], inv[:], ALU.mult))
                    own(f"t{n + 1}")
                    inc(dve.scalar_tensor_tensor(inv[:], den[:], 2.0, inv[:], ALU.subtract, ALU.mult))
                    own(f"n{n + 1}")
                    inc(dve.scalar_tensor_tensor(o_t[n][:, :, 0:T], tiles(step)[:, 0:3, 0:T], -1.0, inv[:],
                                                 ALU.mult, ALU.mult))

                after("gram")
                dve.wait_ge(act_done, at(it, "act", "pooled"))
                inc(dve.tensor_tensor(prod[:, 0:T], slot["gram"][0:C + 1, 0:T], pt[0:C + 1, 0:T], ALU.mult))
                after("var")
                inc(dve.tensor_scalar(tok_var[:], slot["var"][:, 0:2], EPS, None, ALU.add))
                dve.wait_ge(pool_done, at(it, "pool", "rstd"))
                inc(dve.tensor_copy(rstd_tok[:, :, 0:C + 1], tok_var[:, :].unsqueeze(2).broadcast_to([128, 2, C + 1])))
                after("spread")
                inc(dve.tensor_tensor(ptn[:, 0:T], pt[:, 0:T], slot["spread"][0:NQ, 0:T], ALU.mult))
                after("qk1")
                inc(dve.tensor_copy(k_t[0][:], tiles("qk1", GR)[:, 2:4, 0:T]))
                maxima1(0)
                maxima1(1)
                maxima1(2)
                maxima1(3)
                normalise(1, "av2")
                maxima1(4)
                after("out2")
                dve.wait_ge(out_stored, 32 * it + 32)
                inc(dve.tensor_tensor(y[:], tiles("out2")[:, 0:2, 0:D], h1b[:], ALU.add))
                after("route")
                logits = tiles("route")[:, 0:2, 128:128 + E]
                inc(dve.tensor_reduce(rm[:], logits, AX.X, ALU.max))
                own("rmax")
                inc(dve.tensor_tensor(rl[:], logits, rm[:, :].unsqueeze(2).broadcast_to([128, 2, E]), ALU.subtract))
                dve.wait_ge(act_done, at(it, "act", "rexp"))
                inc(dve.tensor_reduce(rs[:], re[:], AX.X, ALU.add))
                own("rsum")
                inc(dve.reciprocal(ri[:], rs[:]))
                own("rinv")
                inc(dve.tensor_tensor(rp[:], re[:], ri[:, :].unsqueeze(2).broadcast_to([128, 2, E]), ALU.mult))
                own("rprob")
                hold(dve, "dve")
                for tt in range(2):
                    inc(dve.max(rt[:, tt, :], rp[:, tt, :]))
                own("rtop1")
                hold(dve, "dve")
                for tt in range(2):
                    inc(dve.max_index(rx_u[:, tt, :], rt[:, tt, :], rp[:, tt, :]))
                own("ridx1")
                inc(dve.tensor_copy(rx_f[:], rx_u[:]))
                own("ridxf")
                for k, dst in enumerate((one_h, two_h)):
                    for tt in range(2):
                        inc(dve.tensor_scalar(dst[:, tt, :], iota_f[:], rx_f[:, tt, k:k + 1], rt[:, tt, k:k + 1],
                                              ALU.is_equal, ALU.mult))
                own("rtwo1")
                inc(dve.tensor_tensor(c2[:], one_h[:], two_h[:], ALU.add))
                own("rcomb")
                inc(dve.tensor_tensor(hw[:], tiles("route")[:, 0:2, 0:128].rearrange("p t (e r) -> p t e r", e=E),
                                      c2[:, :, :].unsqueeze(3).broadcast_to([128, 2, E, RANK]), ALU.mult))
                for t in range(XT):
                    dve.wait_ge(x_in[t], 16 * it + 32)
                    dve.wait_ge(pool_done, at(it, "pool", f"big{t}", 1))
                    inc(pooling(t))
                after("qk2")
                inc(dve.tensor_copy(k_t[1][:], tiles("qk2", GR)[:, 2:4, 0:T]))
                maxima2(0)
                maxima2(1)
                normalise(0, "av1")
                maxima2(2)
                maxima2(3)
                dve.wait_ge(act_done, at(it, "act", "h1"))
                for tt in range(2):
                    inc(dve.bn_stats(bst[:, tt, :], h1[:, tt, :]))
                own("bs1")
                hold(dve, "dve")
                for tt in range(2):
                    inc(dve.bn_aggr(bag[:, tt, :], bst[:, tt, :]))
                own("ba1")
                own("ba1")
                inc(dve.tensor_scalar(rstd[:], bag[:, :, 1:2], EPS, None, ALU.add))
                dve.wait_ge(pool_done, at(it, "pool", "rs"))
                for tt in range(2):
                    inc(dve.tensor_scalar(xh[:, tt, :], h1[:, tt, :], bag[:, tt, 0:1], rstd[:, tt, :],
                                          ALU.subtract, ALU.mult))
                maxima2(4)
                maxima2(5)


_INS = ['x', 'cls_tok', 'L0_tok_channel_weights', 'L0_attn_w_attn', 'L0_attn_b_attn', 'L0_attn_w_proj',
        'L0_attn_b_proj', 'L0_ffn_Wg', 'L0_ffn_bg', 'L0_ffn_Wqkv', 'L0_ffn_bqkv', 'L0_ffn_Wproj',
        'L0_ffn_bproj', 'L0_ffn_A', 'L0_ffn_ba', 'L0_ffn_Bm', 'L0_ffn_bb']
_OUTS = [((64, 197, 192), 'float32')]


def kernel(**inputs):
    import numpy as _np
    import concourse.bacc as _bacc
    from concourse import mybir as _mybir
    from concourse.bass_utils import run_bass_kernel_spmd as _run

    nc = _bacc.Bacc("TRN2", target_bir_lowering=False, num_devices=1)
    arrays, args = {}, []
    for name in _INS:
        a = _np.ascontiguousarray(inputs[name])
        arrays[f"in_{name}_dram"] = a
        args.append(nc.dram_tensor(f"in_{name}_dram", a.shape, _mybir.dt.from_np(a.dtype), kind="ExternalInput").ap())
    for i, (shape, dtype) in enumerate(_OUTS):
        dt = _mybir.dt.from_np(_np.dtype(dtype))
        args.append(nc.dram_tensor(f"out_{i}_dram", shape, dt, kind="ExternalOutput").ap())
    build(nc, *args)
    r = _run(nc, [arrays], core_ids=[0])
    got = tuple(r.results[0][f"out_{i}_dram"] for i in range(len(_OUTS)))
    return got[0]
```

```python
from contextlib import ExitStack

import concourse.bass as bass
from concourse import mybir

F32 = mybir.dt.float32
F32R = mybir.dt.float32r
BF16 = mybir.dt.bfloat16
I32 = mybir.dt.int32
U32 = mybir.dt.uint32
ALU = mybir.AluOpType
ACT = mybir.ActivationFunctionType
AX = mybir.AxisListType

PE_STEPS = {
    "mt2": 2, "out1": 1, "st2_1": 2, "st2_0": 2, "pooled": 0, "st2_2": 2, "gram": 0, "st2_5": 2, "var": 0,
    "xt": 1, "spread": 0, "st2_3": 2, "qk1": 0, "route": 1, "st2_4": 2, "v1": 0, "av2": 2, "hwt": 1, "qk2": 1,
    "mx1_4": 0, "mx1_0": 0, "mx1_3": 0, "mx1_1": 0, "mx1_2": 0, "out2": 2, "mt1": 0, "v2": 1, "st1_1": 0,
    "st1_2": 0, "st1_3": 0, "mx2_0": 1, "st1_0": 0, "mx2_4": 1, "mx2_5": 1, "mx2_3": 1, "av1": 0, "mx2_2": 1,
    "mx2_1": 1,
}
ACT_STEPS = {
    "shift2": 2, "hidden": 1, "probs2_1": 2, "pooled_rows": 0, "probs2_2": 2, "probs2_5": 2, "probs2_0": 2,
    "xt_low": 1, "probs2_3": 2, "xt_high": 1, "high1": 0, "rexp": 1, "probs2_4": 2, "middle1": 0, "hwt_rows":
    1, "weight_rows": 1, "log2": 2, "values1": 0, "inverse2": 2, "high2": 1, "middle2": 1, "shift1": 0,
    "probs1_1": 0, "probs1_2": 0, "probs1_3": 0, "probs1_0": 0, "values2": 1, "log1": 0, "inverse1": 0,
}
DVE_STEPS = {
    "max_low2": 2, "heads1": 1, "pooling2": 0, "pooling1": 0, "pooling0": 0, "stats": 1, "moments": 1,
    "token_var": 1, "normal": 1, "prod": 0, "variance": 0, "deviation_cols": 0, "scaled": 0, "rmax": 1,
    "rsub": 1, "rest1": 0, "rsum": 1, "rinv": 1, "rprob": 1, "rtop": 1, "ridx": 1, "ridxf": 1, "rpick": 1,
    "rcomb": 1, "weighted": 1, "den2": 2, "newton_a2": 2, "newton_b2": 2, "heads2": 2, "rest2": 1, "max1_4":
    0, "max1_0": 0, "max1_3": 0, "max1_1": 0, "max1_2": 0, "max_high1": 0, "max_low1": 0, "result": 2,
    "max2_0": 1, "max2_4": 1, "max2_5": 1, "max2_3": 1, "den1": 0, "max2_2": 1, "max2_1": 1, "newton_a1": 0,
    "max_high2": 1, "newton_b1": 0,
}
POOL_STEPS = {
    "pooled_kept": 1, "hidden_kept": 2, "halves1": 0, "halves2": 0, "halves0": 0, "rows1": 0, "rows2": 0,
    "rows0": 0, "deviation2": 1, "deviation1": 0, "low1": 0, "low2": 1,
}
SP_STEPS = {
    "load1": 0, "load0": 0, "load2": 0, "keep_high1": 0, "keep_low1": 0, "keep_middle1": 0, "stack_high1": 0,
    "stack_middle1": 0, "stack_low1": 0, "keep_high2": 1, "keep_middle2": 1, "stack_high2": 1, "keep_low2": 1,
    "stack_middle2": 1, "store": 2, "stack_low2": 1,
}
STEPS = {"pe": PE_STEPS, "act": ACT_STEPS, "dve": DVE_STEPS, "pool": POOL_STEPS, "sp": SP_STEPS}
ENGINE = {step: engine for engine, steps in STEPS.items() for step in steps}
BEHIND = {step: n for steps in STEPS.values() for step, n in steps.items()}
LAST = max(BEHIND.values())
HEAD_START = LAST + 2

WIDE = [s for s in PE_STEPS if s[:2] in ("qk", "mx", "st", "av")]
NARROW = [s for s in PE_STEPS if s not in WIDE]
N_WIDE, N_NARROW = 3, 2

READERS = {
    "pooled": ["pooled_rows"], "gram": ["prod"], "var": ["variance"], "spread": ["scaled"],
    "qk1": ["high1", "rest1"], "v1": ["values1"], "qk2": ["high2", "rest2"], "v2": ["values2"],
    "xt": ["xt_low", "xt_high"], "route": ["weighted"], "hwt": ["hwt_rows", "weight_rows"],
    "mt1": ["shift1"], "mt2": ["shift2"], "av1": ["heads1"], "av2": ["heads2"],
    "out1": ["hidden"], "out2": ["result"],
}
for _s in PE_STEPS:
    if _s[:2] == "mx":
        READERS[_s] = ["max" + _s[2:]]
    if _s[:2] == "st":
        READERS[_s] = ["probs" + _s[2:]]

N_DMAS = {"store": 2, "load0": 1, "load1": 1, "load2": 1}
for _n in "12":
    for _p, _c in (("high", 5), ("middle", 3), ("low", 2)):
        N_DMAS[f"keep_{_p}{_n}"] = 1
        N_DMAS[f"stack_{_p}{_n}"] = _c


def count(it, step, back):
    steps = list(STEPS[ENGINE[step]])
    return it * len(steps) + (len(steps) * (HEAD_START - back) + steps.index(step) + 1)


def at(it, user, *steps, age=0):
    places = [(BEHIND[s] - BEHIND[user] - age, list(STEPS[ENGINE[s]]).index(s), s) for s in steps]
    last = max(places)[2]
    return count(it, last, BEHIND[user] + age - BEHIND[last])


def landed_at(it, user, step, age=0):
    back = BEHIND[user] + age - BEHIND[step]
    return it * (16 * N_DMAS[step]) + 16 * N_DMAS[step] * (HEAD_START + 1 - back)


def build(nc, x, cls_tok, cw, w_attn, b_attn, w_proj, b_proj, Wg, bg, Wqkv, bqkv, Wproj, bproj,
          A, ba, Bm, bb, out):
    B, C, IMG, _ = x.shape
    D = cw.shape[1]
    H = 12
    DH = D // H
    P = 16
    NP = IMG // P
    T = NP * NP + 1
    TP = 256
    T0, T1 = 128, T - 128
    E, RANK = A.shape[0], A.shape[1]
    G = 6
    GR = G * DH
    KR = GR + 2 * G
    SL = 256
    NQ = C + 2
    CT = 4
    XP = CT * NP * 2
    XT = C // CT
    XF = (P // 2) * IMG
    EPS = 1e-5
    N_IT = B + LAST
    SCALING = 2.0
    SC1 = float(D) ** -0.5
    SC2 = float(DH) ** -0.5
    NEG = -1e30

    with ExitStack() as ctx:
        def sb(name, shape, dt=F32):
            return ctx.enter_context(nc.sbuf_tensor(name, shape, dt))

        def sem(name):
            return ctx.enter_context(nc.semaphore(name))

        wide = [ctx.enter_context(nc.psum_tensor(f"wide{i}", [128, 4 * SL], F32)) for i in range(N_WIDE)]
        narrow = [ctx.enter_context(nc.psum_tensor(f"narrow{i}", [128, 2 * SL], F32)) for i in range(N_NARROW)]
        slots = [narrow[0]] + wide
        slot = {s: wide[i % N_WIDE] for i, s in enumerate(WIDE)}
        slot.update({s: narrow[i % N_NARROW] for i, s in enumerate(NARROW)})

        def tiles(step, parts=128):
            return slot[step][0:parts, :].rearrange("p (t c) -> p t c", c=SL)

        ident = sb("ident", [128, 128])
        ident_b = sb("ident_b", [128, 128], BF16)
        causal = sb("causal", [128, 128], BF16)
        minus_half = sb("minus_half", [128, 1])
        causal_t = sb("causal_t", [128, 128], BF16)
        patch_c = sb("patch_c", [XP, CT, NP])
        patch_mask = sb("patch_mask", [XP, NP])
        chan_sel = sb("chan_sel", [XP, XT, NQ])
        row_sel = sb("row_sel", [2, NQ], BF16)
        row_val = sb("row_val", [2, T], BF16)
        var_ones = sb("var_ones", [C + 1, 1])
        iota_i = sb("iota_i", [128, E], I32)
        iota_f = sb("iota_f", [128, E])
        h0_w = sb("h0_w", [NQ, D])
        cen = sb("cen", [C + 1, D])
        cen_sum = sb("cen_sum", [C + 1, 1])
        cen_t = sb("cen_t", [128, 2, NQ])
        gram_w = sb("gram_w", [C + 1, C + 1])
        wa = sb("wa", [128, 2, 3 * D])
        w1 = sb("w1", [NQ, 3 * D])
        wp1 = sb("wp1", [128, 3, D])
        wp2 = sb("wp2", [128, 3, D])
        nat_q = sb("nat_q", [GR, 6, D])
        nat_b = sb("nat_b", [GR, 6, E * RANK])
        nat_p = sb("nat_p", [GR, 2, 3, 4, 32])
        nat_a = sb("nat_a", [128, D])
        nat_g = sb("nat_g", [E, D])
        wx = sb("wx", [128, 3 * D])
        wb = sb("wb", [104, 3 * D])
        wh = sb("wh", [128, 3 * D])
        rx = sb("rx", [128, 128 + E])
        rb = sb("rb", [65, 128 + E])
        xs = sb("xs", [XP, XT, XF])
        part = sb("part", [XP, XT, NP])
        xa = sb("xa", [XP, XT, XF // 2])
        big = sb("big", [XP, XT, NP * NP])
        pt = sb("pt", [NQ, TP])
        ptk = sb("ptk", [NQ, TP])
        prod = sb("prod", [C + 1, TP])
        tok_var = sb("tok_var", [128, 2])
        rstd_tok = sb("rstd_tok", [128, 2, NQ])
        ptn = sb("ptn", [NQ, TP])
        pieces = [sb(f"pieces{n}", [GR, 3, 4, T], BF16) for n in (1, 2)]
        rest = [sb(f"rest{n}", [GR, 4, T]) for n in (1, 2)]
        stack = [sb(f"stack{n}", [KR, G, 4, T], BF16) for n in (1, 2)]
        kept = [nc.dram_tensor(f"kept{n}", (3, GR, 4 * T), BF16, kind="Internal").ap() for n in (1, 2)]
        mxp = [sb(f"mxp{n}", [128, 2, 2, 2, G], BF16) for n in (1, 2)]
        va = [sb(f"va{n}", [128, 2, H, 32]) for n in (1, 2)]
        mx = [sb(f"mx{n}", [128, 2, H]) for n in (1, 2)]
        p0 = [sb(f"p0_{n}", [128, H, T]) for n in (1, 2)]
        p1 = [sb("p1_1", [T1, H, T1]), sb("p1_2", [T1, H, T])]
        den = [sb(f"den{n}", [128, 3, T]) for n in (1, 2)]
        lnd = [sb(f"lnd{n}", [128, 3, T]) for n in (1, 2)]
        inv = [sb(f"inv{n}", [128, 3, T]) for n in (1, 2)]
        o_t = [sb(f"o_t{n}", [128, 3, TP]) for n in (1, 2)]
        h1 = sb("h1", [128, 2, D])
        h1k = sb("h1k", [128, 2, D])
        bst = sb("bst", [128, 2, 6])
        bag = sb("bag", [128, 2, 2])
        rstd = sb("rstd", [128, 2, 1])
        xh = sb("xh", [128, 2, D])
        xt0 = sb("xt0", [128, TP])
        xtb = sb("xtb", [104, TP])
        hwt = sb("hwt", [128, TP])
        rm = sb("rm", [128, 2])
        rl = sb("rl", [128, 2, E])
        re = sb("re", [128, 2, E])
        rs = sb("rs", [128, 2])
        ri = sb("ri", [128, 2])
        rp = sb("rp", [128, 2, E])
        rt = sb("rt", [128, 2, 8])
        rx_u = sb("rx_u", [128, 2, 8], U32)
        rx_f = sb("rx_f", [128, 2, 8])
        picked = sb("picked", [128, 2, 2, E])
        c2 = sb("c2", [128, 2, E])
        hw = sb("hw", [128, 2, E, RANK])
        y = sb("y", [128, 2, D])

        pe_done, act_done, dve_done, pool_done = (sem(s) for s in ("pe_done", "act_done", "dve_done", "pool_done"))
        done = {"pe": pe_done, "act": act_done, "dve": dve_done, "pool": pool_done}
        cleared = sem("cleared")
        loaded = sem("loaded")
        landed = {s: sem(f"{s}_landed") for s in SP_STEPS}
        first_kept = sem("first_kept")
        const_ready = sem("const_ready")
        prep_dve = sem("prep_dve")
        prep_pe = sem("prep_pe")
        prep_act = sem("prep_act")
        prep_pool = sem("prep_pool")
        ready = sem("ready")

        loads = []

        def load(dst, src):
            loads.append((dst, src))

        load(h0_w[0:C, :], cw)
        load(h0_w[C:C + 1, :], cls_tok.rearrange("a b d -> (a b) d"))
        load(h0_w[C + 1:C + 2, :], b_proj.rearrange("(a d) -> a d", a=1))
        load(cen[0:C, :], cw)
        load(cen[C:C + 1, :], cls_tok.rearrange("a b d -> (a b) d"))
        load(wa[:, 0, :], w_attn[0:128, :])
        load(wa[0:D - 128, 1, :], w_attn[128:D, :])
        load(w1[C + 1:C + 2, :], b_attn.rearrange("(a d) -> a d", a=1))
        wp_src = w_proj.rearrange("(t j d) n -> j d t n", j=4, d=DH)
        for j in range(4):
            load(wp1[32 * j:32 * j + DH, :, :], wp_src[j])
        load(nat_q[:, :, :], Wqkv.rearrange("(m p) d -> p m d", p=GR))
        bm_src = Bm.rearrange("e (m p) r -> m p e r", p=GR)
        pr_src = Wproj.rearrange("(m p) (t j d) -> m p t j d", p=GR, j=4, d=DH)
        for m in range(6):
            load(nat_b[:, m, :].rearrange("p (e r) -> p e r", e=E), bm_src[m])
        for m in range(2):
            for t in range(3):
                load(nat_p[:, m, t, :, 0:DH], pr_src[m, :, t])
            load(nat_p[:, m, 0, 0, DH:DH + 1], bproj.rearrange("(m p a) -> m p a", p=GR, a=1)[m])
        load(nat_a[:, :], A.rearrange("e r d -> (e r) d"))
        load(nat_g[:, :], Wg)
        load(wb[64:65, :], bqkv.rearrange("(a d) -> a d", a=1))
        load(wb[96:96 + E, :], bb)
        load(rb[64:65, 0:128], ba.rearrange("(a e) r -> a (e r)", a=1))
        load(rb[64:65, 128:128 + E], bg.rearrange("(a e) -> a e", a=1))

        clears = [(t, 0.0) for t in (h1, h1k, xh, o_t[0], o_t[1], xt0, hwt, y, part, big, xs, xa, mx[0], mx[1], mxp[0],
                                     mxp[1], rm, rl, rp, rt, rx_f, picked, c2, hw, bag, rx_u)]
        clears += [(t, 1.0) for t in (p0[0], p0[1], p1[0], p1[1], den[0], den[1], lnd[0], lnd[1], inv[0], inv[1],
                                      rs, ri, re, tok_var, rstd, bst, *wide, *narrow)]

        def x_tile(image, t):
            return x[bass.ds(image, 1), CT * t:CT * (t + 1)].rearrange(
                "b c (i h r) w -> (b c i h) (r w)", h=2, r=P // 2)

        N_READY = 5
        PREP_DVE = 7 + len(clears)
        paused = {n: sem(f"{n}_paused") for n in ("pool", "pe", "dve", "sp")}

        def hold(e, name):
            e.sem_inc(paused[name], 1)

        block = ctx.enter_context(nc.Block())

        @block.sync
        def _(sp):
            sp.wait_ge(cleared, 1)
            for dst, src in loads:
                sp.dma_start(dst, src).then_inc(loaded, 16)
            sp.wait_ge(const_ready, 1)
            for n in range(2):
                for piece in range(3):
                    sp.dma_start(kept[n][piece], pieces[n][:, piece].rearrange("p m t -> p (m t)")).then_inc(first_kept, 16)
            sp.wait_ge(first_kept, 6 * 16)
            for s in SP_STEPS:
                sp.sem_inc(landed[s], 16 * N_DMAS[s] * HEAD_START)
            sp.sem_inc(ready, 1)
            sp.wait_ge(ready, N_READY)

            places = (((0, 0, 4), (2, 0, 2), (3, 2, 4), (4, 0, 2), (5, 2, 4)),
                      ((1, 0, 4), (2, 2, 4), (3, 0, 2)),
                      ((4, 2, 4), (5, 0, 2)))

            def stack_piece(n, piece, signal):
                for block, m0, m1 in places[piece]:
                    sp.dma_start(stack[n][DH * block:DH * block + DH, :, m0:m1, :].rearrange("d j m t -> d j (m t)"),
                                 kept[n][piece, :, m0 * T:m1 * T].rearrange("(j d) x -> d j x", d=DH)).then_inc(signal, 16)

            with sp.Fori(0, N_IT) as it:
                loading = sp.snap((it + (B - BEHIND["load0"])) % B)
                storing = sp.snap((it + (B - BEHIND["store"])) % B)
                sp.wait_ge(pool_done, at(it, "load1", "halves1", age=1))
                hold(sp, "sp")
                sp.dma_start(xs[:, 1, :], x_tile(loading, 1)).then_inc(landed["load1"], 16)
                sp.wait_ge(pool_done, at(it, "load0", "halves0", age=1))
                hold(sp, "sp")
                sp.dma_start(xs[:, 0, :], x_tile(loading, 0)).then_inc(landed["load0"], 16)
                sp.wait_ge(pool_done, at(it, "load2", "halves2", age=1))
                hold(sp, "sp")
                sp.dma_start(xs[:, 2, :], x_tile(loading, 2)).then_inc(landed["load2"], 16)
                sp.wait_ge(act_done, at(it, "keep_high1", "high1"))
                hold(sp, "sp")
                sp.wait_ge(landed["stack_high1"], landed_at(it, "keep_high1", "stack_high1", age=1))
                hold(sp, "sp")
                sp.dma_start(kept[0][0], pieces[0][:, 0].rearrange("p m t -> p (m t)")).then_inc(landed["keep_high1"], 16)
                sp.wait_ge(pool_done, at(it, "keep_low1", "low1"))
                hold(sp, "sp")
                sp.wait_ge(landed["stack_low1"], landed_at(it, "keep_low1", "stack_low1", age=1))
                hold(sp, "sp")
                sp.dma_start(kept[0][2], pieces[0][:, 2].rearrange("p m t -> p (m t)")).then_inc(landed["keep_low1"], 16)
                sp.wait_ge(act_done, at(it, "keep_middle1", "middle1"))
                hold(sp, "sp")
                sp.wait_ge(landed["stack_middle1"], landed_at(it, "keep_middle1", "stack_middle1", age=1))
                hold(sp, "sp")
                sp.dma_start(kept[0][1], pieces[0][:, 1].rearrange("p m t -> p (m t)")).then_inc(landed["keep_middle1"], 16)
                sp.wait_ge(landed["keep_high1"], landed_at(it, "stack_high1", "keep_high1"))
                hold(sp, "sp")
                sp.wait_ge(pe_done, at(it, "stack_high1", "mx1_0", "mx1_1", "mx1_2", "mx1_3", "mx1_4", "st1_0", "st1_1", "st1_2", "st1_3", age=1))
                hold(sp, "sp")
                stack_piece(0, 0, landed["stack_high1"])
                sp.wait_ge(landed["keep_middle1"], landed_at(it, "stack_middle1", "keep_middle1"))
                hold(sp, "sp")
                stack_piece(0, 1, landed["stack_middle1"])
                sp.wait_ge(landed["keep_low1"], landed_at(it, "stack_low1", "keep_low1"))
                hold(sp, "sp")
                stack_piece(0, 2, landed["stack_low1"])
                sp.wait_ge(act_done, at(it, "keep_high2", "high2"))
                hold(sp, "sp")
                sp.wait_ge(landed["stack_high2"], landed_at(it, "keep_high2", "stack_high2", age=1))
                hold(sp, "sp")
                sp.dma_start(kept[1][0], pieces[1][:, 0].rearrange("p m t -> p (m t)")).then_inc(landed["keep_high2"], 16)
                sp.wait_ge(act_done, at(it, "keep_middle2", "middle2"))
                hold(sp, "sp")
                sp.wait_ge(landed["stack_middle2"], landed_at(it, "keep_middle2", "stack_middle2", age=1))
                hold(sp, "sp")
                sp.dma_start(kept[1][1], pieces[1][:, 1].rearrange("p m t -> p (m t)")).then_inc(landed["keep_middle2"], 16)
                sp.wait_ge(landed["keep_high2"], landed_at(it, "stack_high2", "keep_high2"))
                hold(sp, "sp")
                sp.wait_ge(pe_done, at(it, "stack_high2", "mx2_0", "mx2_1", "mx2_2", "mx2_3", "mx2_4", "mx2_5", "st2_0", "st2_1", "st2_2", "st2_3", "st2_4", "st2_5", age=1))
                hold(sp, "sp")
                stack_piece(1, 0, landed["stack_high2"])
                sp.wait_ge(pool_done, at(it, "keep_low2", "low2"))
                hold(sp, "sp")
                sp.wait_ge(landed["stack_low2"], landed_at(it, "keep_low2", "stack_low2", age=1))
                hold(sp, "sp")
                sp.dma_start(kept[1][2], pieces[1][:, 2].rearrange("p m t -> p (m t)")).then_inc(landed["keep_low2"], 16)
                sp.wait_ge(landed["keep_middle2"], landed_at(it, "stack_middle2", "keep_middle2"))
                hold(sp, "sp")
                stack_piece(1, 1, landed["stack_middle2"])
                sp.wait_ge(dve_done, at(it, "store", "result"))
                hold(sp, "sp")
                sp.dma_start(out[bass.ds(storing, 1), 0:T0].rearrange("b t d -> (b t) d"),
                             y[:, 0, :]).then_inc(landed["store"], 16)
                sp.dma_start(out[bass.ds(storing, 1), T0:T].rearrange("b t d -> (b t) d"),
                             y[0:T1, 1, :]).then_inc(landed["store"], 16)
                sp.wait_ge(landed["keep_low2"], landed_at(it, "stack_low2", "keep_low2"))
                hold(sp, "sp")
                stack_piece(1, 2, landed["stack_low2"])
            for s in SP_STEPS:
                sp.wait_ge(landed[s], 16 * N_DMAS[s] * (HEAD_START + N_IT))

        @block.gpsimd
        def _(pool):
            n = [0]

            def step(ins):
                n[0] += 1
                ins.then_inc(prep_pool, 1)
                pool.wait_ge(prep_pool, n[0])

            for tile in (wp1, nat_p, wb):
                pool.memset(tile[:], 0.0).then_inc(prep_pool, 1)
            n[0] += 3
            pool.wait_ge(prep_pool, 3)
            pool.sem_inc(cleared, 1)
            for tile, v in ((ident, 0.0), (causal, 0.0), (causal_t, 0.0), (minus_half, -0.5), (patch_c, 1.0),
                            (chan_sel, 1.0), (row_sel, 0.0), (row_val, 1.0), (var_ones, 1.0), (rstd_tok, 1.0),
                            (prod, 0.0), (pt, 0.0), (ptk, 0.0), (ptn, 0.0), (va[0], 1.0), (va[1], 1.0),
                            (stack[0], 0.0), (stack[1], 0.0), (pieces[0], 0.0), (pieces[1], 0.0),
                            (rest[0], 0.0), (rest[1], 0.0), (xtb, 0.0)):
                pool.memset(tile[:], v).then_inc(prep_pool, 1)
                n[0] += 1
            pool.iota(iota_i[:], pattern=[[1, E]], base=0, channel_multiplier=0).then_inc(prep_pool, 1)
            n[0] += 1
            pool.wait_ge(prep_pool, n[0])

            def select(tile, op, fill, base, pattern, cm):
                step(pool.affine_select(out=tile, in_=tile, compare_op=op, fill=fill, base=base,
                                        pattern=pattern, channel_multiplier=cm))

            select(ident[:], ALU.not_equal, 1.0, 0, [[-1, 128]], 1)
            select(causal[:], ALU.is_ge, NEG, 0, [[-1, 128]], 1)
            select(causal_t[:], ALU.is_ge, NEG, 0, [[1, 128]], -1)
            select(patch_c[:], ALU.is_ge, 0.0, 0, [[-2 * NP, CT], [-2, NP]], 1)
            select(patch_c[:], ALU.is_ge, 0.0, 1, [[2 * NP, CT], [2, NP]], -1)
            select(chan_sel[:], ALU.is_ge, 0.0, 0, [[XP, XT], [-2 * NP, NQ]], 1)
            select(chan_sel[:], ALU.is_ge, 0.0, 2 * NP - 1, [[-XP, XT], [2 * NP, NQ]], -1)
            select(row_sel[:], ALU.not_equal, 1.0, C, [[-1, NQ]], 1)
            select(row_val[:], ALU.is_ge, 0.0, 0, [[-1, T]], 1000)
            for i in range(2):
                for piece in range(2):
                    select(stack[i][GR:KR, :, 2:4, :], ALU.not_equal, 1.0, -G * piece, [[-1, G], [0, 2], [0, T]], 1)
            step(pool.memset(xtb[64:65, :], 1.0))
            step(pool.tensor_copy(ident_b[:], ident[:]))
            step(pool.tensor_copy(iota_f[:], iota_i[:]))
            pool.sem_inc(const_ready, 1)
            pool.wait_ge(prep_dve, PREP_DVE)
            pool.sem_inc(pool_done, HEAD_START * len(POOL_STEPS))
            pool.sem_inc(ready, 1)
            pool.wait_ge(ready, N_READY)

            with pool.Fori(0, N_IT) as it:
                pool.wait_ge(act_done, at(it, "pooled_kept", "pooled_rows"))
                pool.wait_ge(pe_done, at(it, "pooled_kept", "out1", age=1))
                hold(pool, "pool")
                pool.tensor_copy(ptk[:, 0:T], pt[:, 0:T]).then_inc(pool_done, 1)
                pool.wait_ge(act_done, at(it, "hidden_kept", "hidden"))
                pool.wait_ge(dve_done, at(it, "hidden_kept", "result", age=1))
                hold(pool, "pool")
                pool.tensor_copy(h1k[:], h1[:]).then_inc(pool_done, 1)
                pool.wait_ge(landed["load1"], landed_at(it, "halves1", "load1"))
                pool.wait_ge(dve_done, at(it, "halves1", "pooling1", age=1))
                pool.tensor_tensor(xa[:, 1, :], xs[:, 1, 0:XF // 2], xs[:, 1, XF // 2:XF], ALU.add).then_inc(pool_done, 1)
                pool.wait_ge(landed["load2"], landed_at(it, "halves2", "load2"))
                pool.wait_ge(dve_done, at(it, "halves2", "pooling2", age=1))
                pool.tensor_tensor(xa[:, 2, :], xs[:, 2, 0:XF // 2], xs[:, 2, XF // 2:XF], ALU.add).then_inc(pool_done, 1)
                pool.wait_ge(landed["load0"], landed_at(it, "halves0", "load0"))
                pool.wait_ge(dve_done, at(it, "halves0", "pooling0", age=1))
                pool.tensor_tensor(xa[:, 0, :], xs[:, 0, 0:XF // 2], xs[:, 0, XF // 2:XF], ALU.add).then_inc(pool_done, 1)
                pool.wait_ge(dve_done, at(it, "rows1", "pooling1"))
                pool.wait_ge(pe_done, at(it, "rows1", "pooled", age=1))
                pool.tensor_tensor(
                    big[:, 1, :].rearrange("p (i j) -> p i j", i=NP),
                    part[:, 1, :].unsqueeze(1).broadcast_to([XP, NP, NP]),
                    patch_mask[:, :].unsqueeze(2).broadcast_to([XP, NP, NP]), ALU.mult).then_inc(pool_done, 1)
                pool.wait_ge(dve_done, at(it, "rows2", "pooling2"))
                pool.tensor_tensor(
                    big[:, 2, :].rearrange("p (i j) -> p i j", i=NP),
                    part[:, 2, :].unsqueeze(1).broadcast_to([XP, NP, NP]),
                    patch_mask[:, :].unsqueeze(2).broadcast_to([XP, NP, NP]), ALU.mult).then_inc(pool_done, 1)
                pool.wait_ge(dve_done, at(it, "rows0", "pooling0"))
                pool.tensor_tensor(
                    big[:, 0, :].rearrange("p (i j) -> p i j", i=NP),
                    part[:, 0, :].unsqueeze(1).broadcast_to([XP, NP, NP]),
                    patch_mask[:, :].unsqueeze(2).broadcast_to([XP, NP, NP]), ALU.mult).then_inc(pool_done, 1)
                pool.wait_ge(dve_done, at(it, "deviation2", "token_var"))
                hold(pool, "pool")
                pool.tensor_tensor(rstd[:], rstd[:], minus_half[:, :].unsqueeze(1).broadcast_to([128, 2, 1]), ALU.pow).then_inc(pool_done, 1)
                pool.wait_ge(dve_done, at(it, "deviation1", "variance"))
                hold(pool, "pool")
                pool.tensor_tensor(tok_var[:], tok_var[:], minus_half[:, :].broadcast_to([128, 2]), ALU.pow).then_inc(pool_done, 1)
                pool.wait_ge(act_done, at(it, "low1", "middle1"))
                pool.wait_ge(landed["keep_low1"], landed_at(it, "low1", "keep_low1", age=1))
                pool.tensor_tensor(pieces[0][:, 2], rest[0][:], pieces[0][:, 1], ALU.subtract).then_inc(pool_done, 1)
                pool.wait_ge(act_done, at(it, "low2", "middle2"))
                pool.wait_ge(landed["keep_low2"], landed_at(it, "low2", "keep_low2", age=1))
                pool.tensor_tensor(pieces[1][:, 2], rest[1][:], pieces[1][:, 1], ALU.subtract).then_inc(pool_done, 1)

        @block.tensor
        def _(pe):
            pe.wait_ge(const_ready, 1)
            pe.wait_ge(loaded, 16 * len(loads))
            pe.wait_ge(prep_dve, PREP_DVE - 3)
            for c, (a, b) in enumerate(((0, 128), (128, D))):
                ins = pe.transpose(slots[0][0:b - a, SL * c:SL * c + C + 1], cen[:, a:b], ident[0:C + 1, 0:C + 1])
            ins.then_inc(prep_pe, 1)
            for m in range(6):
                if m >= 1:
                    pe.wait_ge(prep_act, 3 * m)
                pe.transpose(slots[1][:, 0:GR], nat_q[:, m, 0:128], ident[0:GR, 0:GR])
                pe.transpose(slots[2][0:D - 128, 0:GR], nat_q[:, m, 128:D], ident[0:GR, 0:GR])
                pe.transpose(slots[3][:, 0:GR], nat_b[:, m, :], ident[0:GR, 0:GR]).then_inc(prep_pe, 1)
            for m in range(2):
                for t in range(3):
                    pe.wait_ge(prep_act, 18 + 3 * m + t)
                    pe.transpose(slots[1][:, 0:GR], nat_p[:, m, t].rearrange("p j d -> p (j d)"),
                                 ident[0:GR, 0:GR]).then_inc(prep_pe, 1)
            pe.wait_ge(prep_act, 24)
            pe.transpose(slots[1][:, 0:128], nat_a[:, 0:128], ident[:])
            pe.transpose(slots[1][:, 128:128 + E], nat_g[:, 0:128], ident[0:E, 0:E])
            pe.transpose(slots[2][0:D - 128, 0:128], nat_a[:, 128:D], ident[:])
            pe.transpose(slots[2][0:D - 128, 128:128 + E], nat_g[:, 128:D], ident[0:E, 0:E]).then_inc(prep_pe, 1)
            pe.wait_ge(prep_dve, PREP_DVE - 1)
            pe.wait_ge(prep_act, 26)
            for half in range(2):
                cols = slice(3 * D // 2 * half, 3 * D // 2 * (half + 1))
                for c, n in enumerate((128, D - 128)):
                    pe.matmul(slots[3][0:C + 1, 2 * SL * half:2 * SL * half + 3 * D // 2],
                              cen_t[0:n, c, 0:C + 1], wa[0:n, c, cols], start=(c == 0), stop=(c == 1))
            for c, n in enumerate((128, D - 128)):
                ins = pe.matmul(slots[1][0:C + 1, 0:C + 1], cen_t[0:n, c, 0:C + 1], cen_t[0:n, c, 0:C + 1],
                                start=(c == 0), stop=(c == 1))
            ins.then_inc(prep_pe, 1)
            pe.sem_inc(pe_done, HEAD_START * len(PE_STEPS))
            pe.sem_inc(ready, 1)
            pe.wait_ge(ready, N_READY)

            with pe.Fori(0, N_IT) as it:
                def claim(step):
                    steps, slots_ = (WIDE, N_WIDE) if step in WIDE else (NARROW, N_NARROW)
                    i = steps.index(step)
                    p = i - slots_ if i >= slots_ else max(k for k in range(len(steps)) if k % slots_ == i % slots_)
                    previous = steps[p]
                    for reader in READERS[previous]:
                        pe.wait_ge(done[ENGINE[reader]], count(it, reader, int(p > i) + BEHIND[previous] - BEHIND[reader]))

                def shifted(n, step, heads, keys, queries):
                    k0, k1 = keys
                    w = k1 - k0
                    for i, h in enumerate(heads):
                        if n == 0 and k0:
                            dst = slot[step][0:w, 512 * (i // G) + 80 * (i % G):512 * (i // G) + 80 * (i % G) + T - queries]
                        else:
                            dst = slot[step][0:w, SL * i:SL * i + T]
                        ins = pe.matmul(dst, stack[n][:, h % G, 2 + h // G, k0:k1], stack[n][:, h % G, h // G, queries:T],
                                        start=True, stop=(n == 1))
                        if n == 0:
                            ins = pe.matmul(dst[:, 0:w], ident_b[0:w, 0:w], causal_t[0:w, 0:w], start=False, stop=True)
                    ins.then_inc(pe_done, 1)

                def raw(n, step, tile, heads):
                    q0, q1 = (0, T0) if tile == 0 else (T0, T)
                    rows = q1 - q0
                    nk, pitch = (T0, T0) if n == 0 and tile == 0 else (T, SL)
                    masked = n == 0
                    per_bank = 2 * SL // pitch
                    for b in range(len(heads) // per_bank):
                        bank = slot[step][0:rows, 2 * SL * b:2 * SL * b + 2 * SL].rearrange("p (h k) -> p h k", k=pitch)
                        first = masked and tile == 0
                        if first:
                            pe.matmul(bank, ident_b[:], causal[:].unsqueeze(1).broadcast_to([128, per_bank, 128]),
                                      start=True, stop=False)
                        for k in range(per_bank):
                            h = heads[per_bank * b + k]
                            ins = pe.matmul(bank[:, k, 0:nk], stack[n][0:GR, h % G, h // G, q0:q1],
                                            stack[n][0:GR, h % G, 2 + h // G, 0:nk],
                                            start=not first, stop=(not masked or (first and k == per_bank - 1)))
                            if masked and not first:
                                ins = pe.matmul(bank[:, k, T0:T], ident_b[0:rows, 0:rows], causal[0:rows, 0:T1],
                                                start=False, stop=True)
                    ins.then_inc(pe_done, 1)

                def turn_maxima(n, step):
                    for g in range(2):
                        for t, (a, b) in enumerate(((0, T0), (T0, T))):
                            ins = pe.matmul(slot[step][0:KR - GR, SL * g + a:SL * g + b],
                                            mxp[n][0:b - a, t, g].rearrange("p c j -> p (c j)"), ident_b[0:b - a, 0:b - a],
                                            start=True, stop=True)
                    ins.then_inc(pe_done, 1)

                def values(n, step):
                    q1 = T0 if n == 0 else 0
                    for t in range(3):
                        for j in range(4):
                            pe.matmul(slot[step][32 * j:32 * j + 32, SL * t:SL * t + T], va[n][:, 0, 4 * t + j, :],
                                      p0[n][:, 4 * t + j, :], start=True, stop=False)
                        for j in range(4):
                            ins = pe.matmul(slot[step][32 * j:32 * j + 32, SL * t + q1:SL * t + T],
                                            va[n][0:T1, 1, 4 * t + j, :], p1[n][:, 4 * t + j, :], start=False, stop=True)
                    ins.then_inc(pe_done, 1)

                chunks = ((xt0, wx, 128), (xtb, wb, 104), (hwt, wh, 128))
                claim("mt2")
                pe.wait_ge(dve_done, at(it, "mt2", "max_low2"))
                hold(pe, "pe")
                turn_maxima(1, "mt2")
                claim("out1")
                pe.wait_ge(pool_done, at(it, "out1", "pooled_kept"))
                pe.wait_ge(dve_done, at(it, "out1", "heads1"))
                hold(pe, "pe")
                for tt in range(2):
                    tok = slice(128 * tt, 128 * tt + 128)
                    pe.matmul(slot["out1"][:, SL * tt:SL * tt + D], ptk[:, tok], h0_w[:], start=True, stop=False)
                    for t in range(3):
                        ins = pe.matmul(slot["out1"][:, SL * tt:SL * tt + D], o_t[0][:, t, tok], wp1[:, t, :],
                                        start=False, stop=(t == 2))
                ins.then_inc(pe_done, 1)
                claim("st2_1")
                pe.wait_ge(act_done, at(it, "st2_1", "shift2"))
                shifted(1, "st2_1", range(4, 8), (0, T0), 0)
                claim("st2_0")
                shifted(1, "st2_0", range(0, 4), (0, T0), 0)
                claim("pooled")
                pe.wait_ge(pool_done, at(it, "pooled", "rows0", "rows1", "rows2"))
                hold(pe, "pe")
                pe.matmul(slot["pooled"][0:NQ, 0:T], row_sel[:], row_val[:], start=True, stop=False)
                for t in range(XT):
                    ins = pe.matmul(slot["pooled"][0:NQ, 1:T], chan_sel[:, t, :], big[:, t, :],
                                    start=False, stop=(t == XT - 1))
                ins.then_inc(pe_done, 1)
                claim("st2_2")
                shifted(1, "st2_2", range(8, 12), (0, T0), 0)
                claim("gram")
                pe.wait_ge(act_done, at(it, "gram", "pooled_rows"))
                hold(pe, "pe")
                pe.matmul(slot["gram"][0:C + 1, 0:T], gram_w[:], pt[0:C + 1, 0:T], start=True, stop=True).then_inc(pe_done, 1)
                claim("st2_5")
                shifted(1, "st2_5", range(8, 12), (T0, T), 0)
                claim("var")
                pe.wait_ge(dve_done, at(it, "var", "prod"))
                hold(pe, "pe")
                for t in range(2):
                    ins = pe.matmul(slot["var"][:, t:t + 1], prod[:, 128 * t:128 * t + 128], var_ones[:], start=True, stop=True)
                ins.then_inc(pe_done, 1)
                claim("xt")
                pe.wait_ge(dve_done, at(it, "xt", "normal"))
                for t in range(2):
                    pe.transpose(slot["xt"][:, 128 * t:128 * t + 128], xh[:, t, 0:128], ident[:])
                for t in range(2):
                    ins = pe.transpose(slot["xt"][0:D - 128, SL + 128 * t:SL + 128 * t + 128], xh[:, t, 128:D], ident[:])
                ins.then_inc(pe_done, 1)
                claim("spread")
                pe.wait_ge(dve_done, at(it, "spread", "deviation_cols"))
                for t, (a, b) in enumerate(((0, T0), (T0, T))):
                    ins = pe.matmul(slot["spread"][0:NQ, a:b], rstd_tok[0:b - a, t, :], ident[0:b - a, 0:b - a],
                                    start=True, stop=True)
                ins.then_inc(pe_done, 1)
                claim("st2_3")
                shifted(1, "st2_3", range(0, 4), (T0, T), 0)
                claim("qk1")
                pe.wait_ge(dve_done, at(it, "qk1", "scaled"))
                hold(pe, "pe")
                for m in range(4):
                    ins = pe.matmul(slot["qk1"][0:GR, SL * m:SL * m + T], w1[:, GR * m:GR * m + GR], ptn[:, 0:T],
                                    start=True, stop=True)
                ins.then_inc(pe_done, 1)
                claim("route")
                pe.wait_ge(act_done, at(it, "route", "xt_low", "xt_high"))
                for tt in range(2):
                    tok = slice(128 * tt, 128 * tt + 128)
                    pe.matmul(slot["route"][:, SL * tt:SL * tt + 128 + E], xt0[:, tok], rx[:], start=True, stop=False)
                    ins = pe.matmul(slot["route"][:, SL * tt:SL * tt + 128 + E], xtb[0:65, tok], rb[:], start=False, stop=True)
                ins.then_inc(pe_done, 1)
                claim("st2_4")
                shifted(1, "st2_4", range(4, 8), (T0, T), 0)
                claim("v1")
                hold(pe, "pe")
                for t in range(2):
                    ins = pe.matmul(slot["v1"][:, SL * t:SL * t + D], ptn[:, 128 * t:128 * t + 128], w1[:, 2 * D:3 * D],
                                    start=True, stop=True)
                ins.then_inc(pe_done, 1)
                claim("av2")
                pe.wait_ge(act_done, at(it, "av2", "probs2_0", "probs2_1", "probs2_2", "probs2_3", "probs2_4", "probs2_5", "values2"))
                hold(pe, "pe")
                values(1, "av2")
                claim("hwt")
                pe.wait_ge(dve_done, at(it, "hwt", "weighted"))
                for tt in range(2):
                    pe.transpose(slot["hwt"][:, 128 * tt:128 * tt + 128], hw[:, tt].rearrange("p e r -> p (e r)"), ident[:])
                for tt in range(2):
                    ins = pe.transpose(slot["hwt"][0:E, SL + 128 * tt:SL + 128 * tt + 128], c2[:, tt, :], ident[:])
                ins.then_inc(pe_done, 1)
                claim("qk2")
                pe.wait_ge(act_done, at(it, "qk2", "xt_low", "xt_high", "hwt_rows", "weight_rows"))
                for m in range(4):
                    for c, (act_rows, w, k) in enumerate(chunks):
                        ins = pe.matmul(slot["qk2"][0:GR, SL * m:SL * m + T], w[0:k, GR * m:GR * m + GR], act_rows[0:k, 0:T],
                                        start=(c == 0), stop=(c == 2))
                ins.then_inc(pe_done, 1)
                claim("mx1_4")
                pe.wait_ge(landed["stack_high1"], landed_at(it, "mx1_4", "stack_high1"))
                pe.wait_ge(landed["stack_middle1"], landed_at(it, "mx1_4", "stack_middle1"))
                pe.wait_ge(landed["stack_low1"], landed_at(it, "mx1_4", "stack_low1"))
                raw(0, "mx1_4", 1, range(8, 12))
                claim("mx1_0")
                raw(0, "mx1_0", 0, range(0, 8))
                claim("mx1_3")
                raw(0, "mx1_3", 1, range(4, 8))
                claim("mx1_1")
                raw(0, "mx1_1", 0, range(8, 12))
                claim("mx1_2")
                raw(0, "mx1_2", 1, range(0, 4))
                claim("out2")
                pe.wait_ge(dve_done, at(it, "out2", "heads2"))
                for tt in range(2):
                    for t in range(3):
                        ins = pe.matmul(slot["out2"][:, SL * tt:SL * tt + D], o_t[1][:, t, 128 * tt:128 * tt + 128],
                                        wp2[:, t, :], start=(t == 0), stop=(t == 2))
                ins.then_inc(pe_done, 1)
                claim("mt1")
                pe.wait_ge(dve_done, at(it, "mt1", "max_low1"))
                hold(pe, "pe")
                turn_maxima(0, "mt1")
                claim("v2")
                for tt in range(2):
                    for c, (act_rows, w, k) in enumerate(chunks):
                        ins = pe.matmul(slot["v2"][:, SL * tt:SL * tt + D], act_rows[0:k, 128 * tt:128 * tt + 128],
                                        w[0:k, 2 * D:3 * D], start=(c == 0), stop=(c == 2))
                ins.then_inc(pe_done, 1)
                claim("st1_1")
                pe.wait_ge(act_done, at(it, "st1_1", "shift1"))
                shifted(0, "st1_1", range(4, 8), (0, T0), 0)
                claim("st1_2")
                shifted(0, "st1_2", range(8, 12), (0, T0), 0)
                claim("st1_3")
                shifted(0, "st1_3", range(H), (T0, T), T0)
                claim("mx2_0")
                pe.wait_ge(landed["stack_high2"], landed_at(it, "mx2_0", "stack_high2"))
                pe.wait_ge(landed["stack_middle2"], landed_at(it, "mx2_0", "stack_middle2"))
                pe.wait_ge(landed["stack_low2"], landed_at(it, "mx2_0", "stack_low2"))
                raw(1, "mx2_0", 0, range(0, 4))
                claim("st1_0")
                shifted(0, "st1_0", range(0, 4), (0, T0), 0)
                claim("mx2_4")
                raw(1, "mx2_4", 1, range(4, 8))
                claim("mx2_5")
                raw(1, "mx2_5", 1, range(8, 12))
                claim("mx2_3")
                raw(1, "mx2_3", 1, range(0, 4))
                claim("av1")
                pe.wait_ge(act_done, at(it, "av1", "probs1_0", "probs1_1", "probs1_2", "probs1_3", "values1"))
                hold(pe, "pe")
                values(0, "av1")
                claim("mx2_2")
                raw(1, "mx2_2", 0, range(8, 12))
                claim("mx2_1")
                raw(1, "mx2_1", 0, range(4, 8))

        @block.scalar
        def _(act):
            for m in range(6):
                cols = slice(GR * m, GR * m + GR)
                act.wait_ge(prep_pe, m + 2)
                act.activation(wx[:, cols], slots[1][:, 0:GR], ACT.Copy).then_inc(prep_act, 1)
                act.activation(wb[0:D - 128, cols], slots[2][0:D - 128, 0:GR], ACT.Copy).then_inc(prep_act, 1)
                act.activation(wh[:, cols], slots[3][:, 0:GR], ACT.Copy, scale=SCALING).then_inc(prep_act, 1)
            for m in range(2):
                for t in range(3):
                    act.wait_ge(prep_pe, 8 + 3 * m + t)
                    act.activation(wp2[:, t, GR * m:GR * m + GR], slots[1][:, 0:GR], ACT.Copy).then_inc(prep_act, 1)
            act.wait_ge(prep_pe, 14)
            act.activation(rx[:], slots[1][:, 0:128 + E], ACT.Copy).then_inc(prep_act, 1)
            act.activation(rb[0:D - 128, :], slots[2][0:D - 128, 0:128 + E], ACT.Copy).then_inc(prep_act, 1)
            act.wait_ge(prep_pe, 15)
            act.activation(w1[0:C + 1, :].rearrange("p (h n) -> p h n", h=2),
                           slots[3][0:C + 1, :].rearrange("p (h n) -> p h n", h=2)[:, :, 0:3 * D // 2],
                           ACT.Copy).then_inc(prep_act, 1)
            act.activation(gram_w[:], slots[1][0:C + 1, 0:C + 1], ACT.Copy, scale=1.0 / D).then_inc(prep_act, 1)
            act.wait_ge(prep_act, 28)
            act.sem_inc(act_done, HEAD_START * len(ACT_STEPS))
            act.sem_inc(ready, 1)
            act.wait_ge(ready, N_READY)

            act.preload_act_table_set("natural_log_exp_and_others")
            with act.Fori(0, N_IT) as it:
                def copy(dst, src, scale=1.0):
                    act.activation(dst, src, ACT.Copy, scale=scale).then_inc(act_done, 1)

                act.wait_ge(pe_done, at(it, "shift2", "mt2"))
                act.wait_ge(pe_done, at(it, "shift2", "st2_0", "st2_1", "st2_2", "st2_3", "st2_4", "st2_5", age=1))
                copy(stack[1][GR:KR, :, 0:2, :],
                     tiles("mt2", KR - GR)[:, 0:2, 0:T].unsqueeze(1).broadcast_to([KR - GR, G, 2, T]))
                act.wait_ge(pe_done, at(it, "hidden", "out1"))
                act.wait_ge(pool_done, at(it, "hidden", "hidden_kept", age=1))
                act.wait_ge(dve_done, at(it, "hidden", "stats", "normal", age=1))
                copy(h1[:], tiles("out1")[:, :, 0:D])
                act.wait_ge(pe_done, at(it, "probs2_1", "st2_1"))
                act.wait_ge(pe_done, at(it, "probs2_1", "av2", age=1))
                act.activation(p0[1][:, 4:8, :], tiles("st2_1")[:, :, 0:T], ACT.Exp, scale=SC2).then_inc(act_done, 1)
                act.wait_ge(pe_done, at(it, "pooled_rows", "pooled"))
                act.wait_ge(dve_done, at(it, "pooled_rows", "prod", "scaled", age=1))
                act.wait_ge(pool_done, at(it, "pooled_rows", "pooled_kept", age=1))
                copy(pt[:, 0:T], slot["pooled"][0:NQ, 0:T])
                act.wait_ge(pe_done, at(it, "probs2_2", "st2_2"))
                act.activation(p0[1][:, 8:12, :], tiles("st2_2")[:, :, 0:T], ACT.Exp, scale=SC2).then_inc(act_done, 1)
                act.wait_ge(pe_done, at(it, "probs2_5", "st2_5"))
                act.activation(p1[1][:, 8:12, :], tiles("st2_5", T1)[:, :, 0:T], ACT.Exp, scale=SC2).then_inc(act_done, 1)
                act.wait_ge(pe_done, at(it, "probs2_0", "st2_0"))
                act.activation(p0[1][:, 0:4, :], tiles("st2_0")[:, :, 0:T], ACT.Exp, scale=SC2).then_inc(act_done, 1)
                act.wait_ge(pe_done, at(it, "xt_low", "xt"))
                act.wait_ge(pe_done, at(it, "xt_low", "route", "qk2", "v2", age=1))
                copy(xt0[:], slot["xt"][:, 0:SL])
                act.wait_ge(pe_done, at(it, "probs2_3", "st2_3"))
                act.activation(p1[1][:, 0:4, :], tiles("st2_3", T1)[:, :, 0:T], ACT.Exp, scale=SC2).then_inc(act_done, 1)
                copy(xtb[0:D - 128, :], slot["xt"][0:D - 128, SL:2 * SL])
                act.wait_ge(pe_done, at(it, "high1", "qk1"))
                act.wait_ge(dve_done, at(it, "high1", "rest1", age=1))
                act.wait_ge(landed["keep_high1"], landed_at(it, "high1", "keep_high1", age=1))
                copy(pieces[0][:, 0], tiles("qk1", GR)[:, :, 0:T])
                act.wait_ge(dve_done, at(it, "rexp", "rsub"))
                act.wait_ge(dve_done, at(it, "rexp", "rsum", "rprob", age=1))
                act.activation(re[:], rl[:], ACT.Exp).then_inc(act_done, 1)
                act.wait_ge(pe_done, at(it, "probs2_4", "st2_4"))
                act.activation(p1[1][:, 4:8, :], tiles("st2_4", T1)[:, :, 0:T], ACT.Exp, scale=SC2).then_inc(act_done, 1)
                act.wait_ge(dve_done, at(it, "middle1", "rest1"))
                act.wait_ge(pool_done, at(it, "middle1", "low1", age=1))
                act.wait_ge(landed["keep_middle1"], landed_at(it, "middle1", "keep_middle1", age=1))
                copy(pieces[0][:, 1], rest[0][:])
                act.wait_ge(pe_done, at(it, "hwt_rows", "hwt"))
                act.wait_ge(pe_done, at(it, "hwt_rows", "qk2", "v2", age=1))
                copy(hwt[:], slot["hwt"][:, 0:SL])
                copy(xtb[96:96 + E, :], slot["hwt"][0:E, SL:2 * SL])
                act.wait_ge(dve_done, at(it, "log2", "den2"))
                act.activation(lnd[1][:], den[1][:], ACT.Ln).then_inc(act_done, 1)
                act.wait_ge(pe_done, at(it, "values1", "v1"))
                act.wait_ge(pe_done, at(it, "values1", "av1", age=1))
                copy(va[0][:, :, :, 0:DH], tiles("v1")[:, 0:2, 0:D].rearrange("p t (h d) -> p t h d", h=H))
                act.wait_ge(act_done, at(it, "inverse2", "log2"))
                act.activation(inv[1][:], lnd[1][:], ACT.Exp, scale=-1.0).then_inc(act_done, 1)
                act.wait_ge(pe_done, at(it, "high2", "qk2"))
                act.wait_ge(dve_done, at(it, "high2", "rest2", age=1))
                act.wait_ge(landed["keep_high2"], landed_at(it, "high2", "keep_high2", age=1))
                copy(pieces[1][:, 0], tiles("qk2", GR)[:, :, 0:T])
                act.wait_ge(dve_done, at(it, "middle2", "rest2"))
                act.wait_ge(pool_done, at(it, "middle2", "low2", age=1))
                act.wait_ge(landed["keep_middle2"], landed_at(it, "middle2", "keep_middle2", age=1))
                copy(pieces[1][:, 1], rest[1][:])
                act.wait_ge(pe_done, at(it, "shift1", "mt1"))
                act.wait_ge(pe_done, at(it, "shift1", "st1_0", "st1_1", "st1_2", "st1_3", age=1))
                copy(stack[0][GR:KR, :, 0:2, :],
                     tiles("mt1", KR - GR)[:, 0:2, 0:T].unsqueeze(1).broadcast_to([KR - GR, G, 2, T]))
                act.wait_ge(pe_done, at(it, "probs1_1", "st1_1"))
                act.activation(p0[0][:, 4:8, :], tiles("st1_1")[:, :, 0:T], ACT.Exp, scale=SC1).then_inc(act_done, 1)
                act.wait_ge(pe_done, at(it, "probs1_2", "st1_2"))
                act.activation(p0[0][:, 8:12, :], tiles("st1_2")[:, :, 0:T], ACT.Exp, scale=SC1).then_inc(act_done, 1)
                act.wait_ge(pe_done, at(it, "probs1_3", "st1_3"))
                act.activation(
                    p1[0][:].rearrange("p (b h) q -> p b h q", b=2),
                    slot["st1_3"][0:T1, :].rearrange("p (b n) -> p b n", b=2)[:, :, 0:80 * G].rearrange(
                        "p b (h n) -> p b h n", h=G)[:, :, :, 0:T1],
                    ACT.Exp, scale=SC1).then_inc(act_done, 1)
                act.wait_ge(pe_done, at(it, "probs1_0", "st1_0"))
                act.activation(p0[0][:, 0:4, :], tiles("st1_0")[:, :, 0:T], ACT.Exp, scale=SC1).then_inc(act_done, 1)
                act.wait_ge(pe_done, at(it, "values2", "v2"))
                act.wait_ge(pe_done, at(it, "values2", "av2", age=1))
                copy(va[1][:, :, :, 0:DH], tiles("v2")[:, 0:2, 0:D].rearrange("p t (h d) -> p t h d", h=H))
                act.wait_ge(dve_done, at(it, "log1", "den1"))
                act.activation(lnd[0][:], den[0][:], ACT.Ln).then_inc(act_done, 1)
                act.wait_ge(act_done, at(it, "inverse1", "log1"))
                act.activation(inv[0][:], lnd[0][:], ACT.Exp, scale=-1.0).then_inc(act_done, 1)

        @block.vector
        def _(dve):
            def pooling(t):
                return dve.tensor_reduce(part[:, t, :], xa[:, t, :].rearrange("p (r j w) -> p j r w", r=P // 4, w=P),
                                         AX.XY, ALU.add)

            for tile, v in clears:
                dve.memset(tile[:], v).then_inc(prep_dve, 1)
            dve.wait_ge(const_ready, 1)
            dve.tensor_reduce(patch_mask[:], patch_c[:].rearrange("p c i -> p i c"), AX.X, ALU.add).then_inc(prep_dve, 1)
            dve.wait_ge(loaded, 16 * len(loads))
            dve.tensor_reduce(cen_sum[:], cen[:], AX.X, ALU.add).then_inc(prep_dve, 1)
            dve.wait_ge(prep_dve, PREP_DVE - 5)
            dve.tensor_scalar(cen_sum[:], cen_sum[:], 1.0 / D, None, ALU.mult).then_inc(prep_dve, 1)
            dve.wait_ge(prep_dve, PREP_DVE - 4)
            dve.tensor_scalar(cen[:], cen[:], cen_sum[:, 0:1], None, ALU.subtract).then_inc(prep_dve, 1)
            dve.wait_ge(prep_pe, 1)
            dve.tensor_copy(cen_t[:, 0, 0:C + 1], slots[0][:, 0:C + 1]).then_inc(prep_dve, 1)
            dve.tensor_copy(cen_t[0:D - 128, 1, 0:C + 1], slots[0][0:D - 128, SL:SL + C + 1]).then_inc(prep_dve, 1)
            dve.tensor_scalar(wb[96:96 + E, :], wb[96:96 + E, :], SCALING, None, ALU.mult).then_inc(prep_dve, 1)
            dve.wait_ge(prep_dve, PREP_DVE)
            dve.sem_inc(dve_done, HEAD_START * len(DVE_STEPS))
            dve.sem_inc(ready, 1)
            dve.wait_ge(ready, N_READY)

            with dve.Fori(0, N_IT) as it:
                dve.wait_ge(dve_done, at(it, "max_low2", "max_high2"))
                dve.scalar_tensor_tensor(mxp[1][:, :, :, 1], mx[1][:].rearrange("p t (g j) -> p t g j", g=2), -1.0,
                                         mxp[1][:, :, :, 0], ALU.mult, ALU.subtract).then_inc(dve_done, 1)
                dve.wait_ge(dve_done, at(it, "heads1", "newton_b1"))
                dve.wait_ge(pe_done, at(it, "heads1", "out1", age=1))
                dve.scalar_tensor_tensor(o_t[0][:, :, 0:T], tiles("av1")[:, 0:3, 0:T], -1.0, inv[0][:],
                                         ALU.mult, ALU.mult).then_inc(dve_done, 1)
                dve.wait_ge(pool_done, at(it, "pooling2", "halves2"))
                dve.wait_ge(pool_done, at(it, "pooling2", "rows2", age=1))
                pooling(2).then_inc(dve_done, 1)
                dve.wait_ge(pool_done, at(it, "pooling1", "halves1"))
                dve.wait_ge(pool_done, at(it, "pooling1", "rows1", age=1))
                pooling(1).then_inc(dve_done, 1)
                dve.wait_ge(pool_done, at(it, "pooling0", "halves0"))
                dve.wait_ge(pool_done, at(it, "pooling0", "rows0", age=1))
                pooling(0).then_inc(dve_done, 1)
                dve.wait_ge(act_done, at(it, "stats", "hidden"))
                for tt in range(2):
                    ins = dve.bn_stats(bst[:, tt, :], h1[:, tt, :])
                ins.then_inc(dve_done, 1)
                dve.wait_ge(dve_done, at(it, "moments", "stats"))
                hold(dve, "dve")
                for tt in range(2):
                    ins = dve.bn_aggr(bag[:, tt, :], bst[:, tt, :])
                ins.then_inc(dve_done, 1)
                dve.wait_ge(dve_done, at(it, "token_var", "moments"))
                dve.tensor_scalar(rstd[:], bag[:, :, 1:2], EPS, None, ALU.add).then_inc(dve_done, 1)
                dve.wait_ge(pool_done, at(it, "normal", "deviation2"))
                dve.wait_ge(pe_done, at(it, "normal", "xt", age=1))
                for tt in range(2):
                    ins = dve.tensor_scalar(xh[:, tt, :], h1[:, tt, :], bag[:, tt, 0:1], rstd[:, tt, :], ALU.subtract, ALU.mult)
                ins.then_inc(dve_done, 1)
                dve.wait_ge(pe_done, at(it, "prod", "gram"))
                dve.wait_ge(act_done, at(it, "prod", "pooled_rows"))
                dve.wait_ge(pe_done, at(it, "prod", "var", age=1))
                dve.tensor_tensor(prod[:, 0:T], slot["gram"][0:C + 1, 0:T], pt[0:C + 1, 0:T], ALU.mult).then_inc(dve_done, 1)
                dve.wait_ge(pe_done, at(it, "variance", "var"))
                dve.wait_ge(pool_done, at(it, "variance", "deviation1", age=1))
                dve.tensor_scalar(tok_var[:], slot["var"][:, 0:2], EPS, None, ALU.add).then_inc(dve_done, 1)
                dve.wait_ge(pool_done, at(it, "deviation_cols", "deviation1"))
                dve.wait_ge(pe_done, at(it, "deviation_cols", "spread", age=1))
                dve.tensor_copy(rstd_tok[:, :, 0:C + 1], tok_var[:, :].unsqueeze(2).broadcast_to([128, 2, C + 1])).then_inc(dve_done, 1)
                dve.wait_ge(pe_done, at(it, "scaled", "spread"))
                dve.wait_ge(pe_done, at(it, "scaled", "qk1", "v1", age=1))
                dve.tensor_tensor(ptn[:, 0:T], pt[:, 0:T], slot["spread"][0:NQ, 0:T], ALU.mult).then_inc(dve_done, 1)
                dve.wait_ge(pe_done, at(it, "rmax", "route"))
                dve.tensor_reduce(rm[:], tiles("route")[:, :, 128:128 + E], AX.X, ALU.max).then_inc(dve_done, 1)
                dve.wait_ge(dve_done, at(it, "rsub", "rmax"))
                dve.wait_ge(act_done, at(it, "rsub", "rexp", age=1))
                dve.tensor_tensor(rl[:], tiles("route")[:, :, 128:128 + E], rm[:, :].unsqueeze(2).broadcast_to([128, 2, E]),
                                  ALU.subtract).then_inc(dve_done, 1)
                dve.wait_ge(act_done, at(it, "rest1", "high1"))
                dve.wait_ge(act_done, at(it, "rest1", "middle1", age=1))
                dve.wait_ge(pool_done, at(it, "rest1", "low1", age=1))
                dve.tensor_tensor(rest[0][:], tiles("qk1", GR)[:, :, 0:T], pieces[0][:, 0], ALU.subtract).then_inc(dve_done, 1)
                dve.wait_ge(act_done, at(it, "rsum", "rexp"))
                dve.tensor_reduce(rs[:], re[:], AX.X, ALU.add).then_inc(dve_done, 1)
                dve.wait_ge(dve_done, at(it, "rinv", "rsum"))
                dve.reciprocal(ri[:], rs[:]).then_inc(dve_done, 1)
                dve.wait_ge(dve_done, at(it, "rprob", "rinv"))
                dve.tensor_tensor(rp[:], re[:], ri[:, :].unsqueeze(2).broadcast_to([128, 2, E]), ALU.mult).then_inc(dve_done, 1)
                dve.wait_ge(dve_done, at(it, "rtop", "rprob"))
                hold(dve, "dve")
                for tt in range(2):
                    ins = dve.max(rt[:, tt, :], rp[:, tt, :])
                ins.then_inc(dve_done, 1)
                dve.wait_ge(dve_done, at(it, "ridx", "rtop"))
                hold(dve, "dve")
                for tt in range(2):
                    ins = dve.max_index(rx_u[:, tt, :], rt[:, tt, :], rp[:, tt, :])
                ins.then_inc(dve_done, 1)
                dve.wait_ge(dve_done, at(it, "ridxf", "ridx"))
                dve.tensor_copy(rx_f[:], rx_u[:]).then_inc(dve_done, 1)
                dve.wait_ge(dve_done, at(it, "rpick", "ridxf"))
                for k in range(2):
                    for tt in range(2):
                        ins = dve.tensor_scalar(picked[:, k, tt, :], iota_f[:], rx_f[:, tt, k:k + 1], rt[:, tt, k:k + 1],
                                                ALU.is_equal, ALU.mult)
                ins.then_inc(dve_done, 1)
                dve.wait_ge(dve_done, at(it, "rcomb", "rpick"))
                dve.wait_ge(pe_done, at(it, "rcomb", "hwt", age=1))
                dve.tensor_tensor(c2[:], picked[:, 0], picked[:, 1], ALU.add).then_inc(dve_done, 1)
                dve.wait_ge(dve_done, at(it, "weighted", "rcomb"))
                dve.tensor_tensor(hw[:], tiles("route")[:, :, 0:128].rearrange("p t (e r) -> p t e r", e=E),
                                  c2[:, :, :].unsqueeze(3).broadcast_to([128, 2, E, RANK]), ALU.mult).then_inc(dve_done, 1)
                dve.wait_ge(pe_done, at(it, "den2", "av2"))
                hold(dve, "dve")
                dve.stream_shuffle(den[1][:], tiles("av2")[:, 0:3, 0:T], [DH + i % DH for i in range(32)]).then_inc(dve_done, 1)
                dve.wait_ge(act_done, at(it, "newton_a2", "inverse2"))
                dve.tensor_tensor(den[1][:], den[1][:], inv[1][:], ALU.mult).then_inc(dve_done, 1)
                dve.wait_ge(dve_done, at(it, "newton_b2", "newton_a2"))
                dve.scalar_tensor_tensor(inv[1][:], den[1][:], 2.0, inv[1][:], ALU.subtract, ALU.mult).then_inc(dve_done, 1)
                dve.wait_ge(dve_done, at(it, "heads2", "newton_b2"))
                dve.wait_ge(pe_done, at(it, "heads2", "out2", age=1))
                dve.scalar_tensor_tensor(o_t[1][:, :, 0:T], tiles("av2")[:, 0:3, 0:T], -1.0, inv[1][:],
                                         ALU.mult, ALU.mult).then_inc(dve_done, 1)
                dve.wait_ge(act_done, at(it, "rest2", "high2"))
                dve.wait_ge(act_done, at(it, "rest2", "middle2", age=1))
                dve.wait_ge(pool_done, at(it, "rest2", "low2", age=1))
                dve.tensor_tensor(rest[1][:], tiles("qk2", GR)[:, :, 0:T], pieces[1][:, 0], ALU.subtract).then_inc(dve_done, 1)
                dve.wait_ge(pe_done, at(it, "max1_4", "mx1_4"))
                dve.tensor_reduce(mx[0][0:T1, 1, 8:12], tiles("mx1_4", T1)[:, :, 0:T], AX.X, ALU.max).then_inc(dve_done, 1)
                dve.wait_ge(pe_done, at(it, "max1_0", "mx1_0"))
                dve.tensor_reduce(mx[0][:, 0, 0:8], slot["mx1_0"][:, 0:8 * T0].rearrange("p (h k) -> p h k", h=8),
                                  AX.X, ALU.max).then_inc(dve_done, 1)
                dve.wait_ge(pe_done, at(it, "max1_3", "mx1_3"))
                dve.tensor_reduce(mx[0][0:T1, 1, 4:8], tiles("mx1_3", T1)[:, :, 0:T], AX.X, ALU.max).then_inc(dve_done, 1)
                dve.wait_ge(pe_done, at(it, "max1_1", "mx1_1"))
                dve.tensor_reduce(mx[0][:, 0, 8:12], slot["mx1_1"][:, 0:4 * T0].rearrange("p (h k) -> p h k", h=4),
                                  AX.X, ALU.max).then_inc(dve_done, 1)
                dve.wait_ge(pe_done, at(it, "max1_2", "mx1_2"))
                dve.tensor_reduce(mx[0][0:T1, 1, 0:4], tiles("mx1_2", T1)[:, :, 0:T], AX.X, ALU.max).then_inc(dve_done, 1)
                dve.wait_ge(dve_done, at(it, "max_high1", "max1_0", "max1_1", "max1_2", "max1_3", "max1_4"))
                dve.wait_ge(pe_done, at(it, "max_high1", "mt1", age=1))
                hold(dve, "dve")
                dve.tensor_scalar(mxp[0][:, :, :, 0], mx[0][:].rearrange("p t (g j) -> p t g j", g=2), -1.0, None, ALU.mult).then_inc(dve_done, 1)
                dve.wait_ge(dve_done, at(it, "max_low1", "max_high1"))
                dve.scalar_tensor_tensor(mxp[0][:, :, :, 1], mx[0][:].rearrange("p t (g j) -> p t g j", g=2), -1.0,
                                         mxp[0][:, :, :, 0], ALU.mult, ALU.subtract).then_inc(dve_done, 1)
                dve.wait_ge(pe_done, at(it, "result", "out2"))
                dve.wait_ge(pool_done, at(it, "result", "hidden_kept"))
                dve.wait_ge(landed["store"], landed_at(it, "result", "store", age=1))
                dve.tensor_tensor(y[:], tiles("out2")[:, :, 0:D], h1k[:], ALU.add).then_inc(dve_done, 1)
                dve.wait_ge(pe_done, at(it, "max2_0", "mx2_0"))
                dve.tensor_reduce(mx[1][:, 0, 0:4], tiles("mx2_0")[:, :, 0:T], AX.X, ALU.max).then_inc(dve_done, 1)
                dve.wait_ge(pe_done, at(it, "max2_4", "mx2_4"))
                dve.tensor_reduce(mx[1][0:T1, 1, 4:8], tiles("mx2_4", T1)[:, :, 0:T], AX.X, ALU.max).then_inc(dve_done, 1)
                dve.wait_ge(pe_done, at(it, "max2_5", "mx2_5"))
                dve.tensor_reduce(mx[1][0:T1, 1, 8:12], tiles("mx2_5", T1)[:, :, 0:T], AX.X, ALU.max).then_inc(dve_done, 1)
                dve.wait_ge(pe_done, at(it, "max2_3", "mx2_3"))
                dve.tensor_reduce(mx[1][0:T1, 1, 0:4], tiles("mx2_3", T1)[:, :, 0:T], AX.X, ALU.max).then_inc(dve_done, 1)
                dve.wait_ge(pe_done, at(it, "den1", "av1"))
                hold(dve, "dve")
                dve.stream_shuffle(den[0][:], tiles("av1")[:, 0:3, 0:T], [DH + i % DH for i in range(32)]).then_inc(dve_done, 1)
                dve.wait_ge(pe_done, at(it, "max2_2", "mx2_2"))
                dve.tensor_reduce(mx[1][:, 0, 8:12], tiles("mx2_2")[:, :, 0:T], AX.X, ALU.max).then_inc(dve_done, 1)
                dve.wait_ge(pe_done, at(it, "max2_1", "mx2_1"))
                dve.tensor_reduce(mx[1][:, 0, 4:8], tiles("mx2_1")[:, :, 0:T], AX.X, ALU.max).then_inc(dve_done, 1)
                dve.wait_ge(act_done, at(it, "newton_a1", "inverse1"))
                dve.tensor_tensor(den[0][:], den[0][:], inv[0][:], ALU.mult).then_inc(dve_done, 1)
                dve.wait_ge(dve_done, at(it, "max_high2", "max2_0", "max2_1", "max2_2", "max2_3", "max2_4", "max2_5"))
                dve.wait_ge(pe_done, at(it, "max_high2", "mt2", age=1))
                hold(dve, "dve")
                dve.tensor_scalar(mxp[1][:, :, :, 0], mx[1][:].rearrange("p t (g j) -> p t g j", g=2), -1.0, None, ALU.mult).then_inc(dve_done, 1)
                dve.wait_ge(dve_done, at(it, "newton_b1", "newton_a1"))
                dve.scalar_tensor_tensor(inv[0][:], den[0][:], 2.0, inv[0][:], ALU.subtract, ALU.mult).then_inc(dve_done, 1)


_INS = ['x', 'cls_tok', 'L0_tok_channel_weights', 'L0_attn_w_attn', 'L0_attn_b_attn', 'L0_attn_w_proj',
        'L0_attn_b_proj', 'L0_ffn_Wg', 'L0_ffn_bg', 'L0_ffn_Wqkv', 'L0_ffn_bqkv', 'L0_ffn_Wproj',
        'L0_ffn_bproj', 'L0_ffn_A', 'L0_ffn_ba', 'L0_ffn_Bm', 'L0_ffn_bb']
_OUTS = [((64, 197, 192), 'float32')]


def kernel(**inputs):
    import numpy as _np
    import concourse.bacc as _bacc
    from concourse import mybir as _mybir
    from concourse.bass_utils import run_bass_kernel_spmd as _run

    nc = _bacc.Bacc("TRN2", target_bir_lowering=False, num_devices=1)
    arrays, args = {}, []
    for name in _INS:
        a = _np.ascontiguousarray(inputs[name])
        arrays[f"in_{name}_dram"] = a
        args.append(nc.dram_tensor(f"in_{name}_dram", a.shape, _mybir.dt.from_np(a.dtype), kind="ExternalInput").ap())
    for i, (shape, dtype) in enumerate(_OUTS):
        dt = _mybir.dt.from_np(_np.dtype(dtype))
        args.append(nc.dram_tensor(f"out_{i}_dram", shape, dt, kind="ExternalOutput").ap())
    build(nc, *args)
    r = _run(nc, [arrays], core_ids=[0])
    got = tuple(r.results[0][f"out_{i}_dram"] for i in range(len(_OUTS)))
    return got[0]
```

```python
from contextlib import ExitStack

import concourse.bass as bass
from concourse import mybir

F32 = mybir.dt.float32
F32R = mybir.dt.float32r
BF16 = mybir.dt.bfloat16
I32 = mybir.dt.int32
U32 = mybir.dt.uint32
ALU = mybir.AluOpType
ACT = mybir.ActivationFunctionType
AX = mybir.AxisListType

PE_STEPS = {
    "mx1_2": 1, "mx1_1": 1, "mx1_4": 1, "mx1_3": 1, "mx1_0": 1, "out2": 3, "mt1": 1, "v1": 1, "st1_2": 1,
    "st1_3": 1, "st1_0": 1, "st1_1": 1, "mx2_3": 2, "mx2_4": 2, "av1": 1, "mx2_2": 2, "mx2_0": 2, "pooled": 0,
    "v2": 2, "gram": 0, "mx2_1": 2, "mx2_5": 2, "var": 0, "out1": 1, "spread": 0, "mt2": 2, "qk1": 0, "xt": 1,
    "st2_0": 2, "st2_2": 2, "route": 1, "st2_1": 2, "st2_3": 2, "st2_5": 2, "st2_4": 2, "hwt": 1, "av2": 2,
    "qk2": 1,
}
ACT_STEPS = {
    "shift1_1": 1, "shift1_0": 1, "probs1_2": 1, "values1": 1, "probs1_3": 1, "probs1_0": 1, "probs1_1": 1,
    "log1": 1, "inverse1": 1, "pooled_rows": 0, "values2": 2, "hidden": 1, "shift2_0": 2, "shift2_1": 2,
    "high1": 0, "xt_high": 1, "xt_low": 1, "middle1": 0, "probs2_0": 2, "rexp": 1, "probs2_2": 2,
    "probs2_1": 2, "probs2_3": 2, "probs2_5": 2, "probs2_4": 2, "hwt_rows": 1, "weight_rows": 1, "log2": 2,
    "inverse2": 2, "high2": 1, "middle2": 1,
}
DVE_STEPS = {
    "max1_2": 1, "max1_1": 1, "max1_4": 1, "max1_3": 1, "max1_0": 1, "max_high1": 1, "max_low1": 1,
    "result": 3, "pooling1": 0, "pooling0": 0, "pooling2": 0, "max2_3": 2, "max2_4": 2, "den1": 1,
    "max2_2": 2, "max2_0": 2, "newton_a1": 1, "newton_b1": 1, "prod": 0, "heads1": 1, "variance": 0,
    "max2_5": 2, "deviation_cols": 0, "max2_1": 2, "max_high2": 2, "max_low2": 2, "scaled": 0, "stats": 1,
    "moments": 1, "token_var": 1, "normal": 1, "rest1": 0, "rmax": 1, "rsub": 1, "rsum": 1, "rinv": 1,
    "rprob": 1, "rtop": 1, "ridx": 1, "ridxf": 1, "rpick": 1, "rcomb": 1, "weighted": 1, "den2": 2,
    "newton_a2": 2, "newton_b2": 2, "heads2": 2, "rest2": 1,
}
POOL_STEPS = {
    "halves1": 0, "low1": 1, "low2": 2, "halves2": 0, "halves0": 0, "hidden_kept": 2, "rows2": 0, "rows1": 0,
    "pooled_kept": 1, "rows0": 0, "deviation1": 0, "deviation2": 1,
}
SP_STEPS = {
    "load1": 0, "keep_high1": 1, "keep_low1": 1, "load2": 0, "stack_high1": 1, "keep_middle1": 1, "load0": 0,
    "stack_low1": 1, "stack_middle1": 1, "keep_high2": 2, "keep_middle2": 2, "keep_low2": 2, "stack_high2": 2,
    "stack_middle2": 2, "stack_low2": 2, "store": 3,
}
STEPS = {"pe": PE_STEPS, "act": ACT_STEPS, "dve": DVE_STEPS, "pool": POOL_STEPS, "sp": SP_STEPS}
ENGINE = {step: engine for engine, steps in STEPS.items() for step in steps}
BEHIND = {step: n for steps in STEPS.values() for step, n in steps.items()}
LAST = max(BEHIND.values())
HEAD_START = LAST + 2

N_WIDE, N_NARROW = 3, 2
SLOTS = {
    "mx1_2": 0, "mx1_1": 2, "mx1_4": 1, "mx1_3": 0, "mx1_0": 2, "out2": 4, "mt1": 2, "v1": 3, "st1_2": 0,
    "st1_3": 2, "st1_0": 1, "st1_1": 0, "mx2_3": 2, "mx2_4": 1, "av1": 0, "mx2_2": 2, "mx2_0": 1, "pooled": 3,
    "v2": 4, "gram": 3, "mx2_1": 1, "mx2_5": 2, "var": 3, "out1": 4, "spread": 3, "mt2": 4, "qk1": 0, "xt": 3,
    "st2_0": 1, "st2_2": 2, "route": 4, "st2_1": 1, "st2_3": 2, "st2_5": 1, "st2_4": 0, "hwt": 3, "av2": 2,
    "qk2": 1,
}

READERS = {
    "pooled": ["pooled_rows"], "gram": ["prod"], "var": ["variance"], "spread": ["scaled"],
    "qk1": ["high1", "rest1"], "v1": ["values1"], "qk2": ["high2", "rest2"], "v2": ["values2"],
    "xt": ["xt_low", "xt_high"], "route": ["weighted"], "hwt": ["hwt_rows", "weight_rows"],
    "mt1": ["shift1_0", "shift1_1"], "mt2": ["shift2_0", "shift2_1"], "av1": ["heads1"], "av2": ["heads2"],
    "out1": ["hidden"], "out2": ["result"],
}
for _s in PE_STEPS:
    if _s[:2] == "mx":
        READERS[_s] = ["max" + _s[2:]]
    if _s[:2] == "st":
        READERS[_s] = ["probs" + _s[2:]]

N_DMAS = {"store": 2, "load0": 1, "load1": 1, "load2": 1}
for _n in "12":
    for _p, _c in (("high", 5), ("middle", 3), ("low", 2)):
        N_DMAS[f"keep_{_p}{_n}"] = 1
        N_DMAS[f"stack_{_p}{_n}"] = _c


def count(it, step, back):
    steps = list(STEPS[ENGINE[step]])
    return it * len(steps) + (len(steps) * (HEAD_START - back) + steps.index(step) + 1)


def latest(user, steps, before):
    backs = [(BEHIND[user] - BEHIND[s], s) for s in steps] + [(BEHIND[user] + 1 - BEHIND[s], s) for s in before]
    back, step = min(backs, key=lambda x: (x[0], -list(STEPS[ENGINE[x[1]]]).index(x[1])))
    return step, back


def at(it, user, *steps, before=()):
    return count(it, *latest(user, steps, before))


def landed_at(it, user, step, age=0):
    back = BEHIND[user] + age - BEHIND[step]
    return it * (16 * N_DMAS[step]) + 16 * N_DMAS[step] * (HEAD_START + 1 - back)


def build(nc, x, cls_tok, cw, w_attn, b_attn, w_proj, b_proj, Wg, bg, Wqkv, bqkv, Wproj, bproj,
          A, ba, Bm, bb, out):
    B, C, IMG, _ = x.shape
    D = cw.shape[1]
    H = 12
    DH = D // H
    P = 16
    NP = IMG // P
    T = NP * NP + 1
    TP = 256
    T0, T1 = 128, T - 128
    E, RANK = A.shape[0], A.shape[1]
    G = 6
    GR = G * DH
    KR = GR + 2 * G
    SL = 256
    NQ = C + 2
    CT = 4
    XP = CT * NP * 2
    XT = C // CT
    XF = (P // 2) * IMG
    EPS = 1e-5
    N_IT = B + LAST
    SCALING = 2.0
    SC1 = float(D) ** -0.5
    SC2 = float(DH) ** -0.5
    NEG = -1e30

    with ExitStack() as ctx:
        def sb(name, shape, dt=F32):
            return ctx.enter_context(nc.sbuf_tensor(name, shape, dt))

        def sem(name):
            return ctx.enter_context(nc.semaphore(name))

        wide = [ctx.enter_context(nc.psum_tensor(f"wide{i}", [128, 4 * SL], F32)) for i in range(N_WIDE)]
        narrow = [ctx.enter_context(nc.psum_tensor(f"narrow{i}", [128, 2 * SL], F32)) for i in range(N_NARROW)]
        slots = [narrow[0]] + wide
        slot = {s: (wide + narrow)[i] for s, i in SLOTS.items()}

        def tiles(step, parts=128):
            return slot[step][0:parts, :].rearrange("p (t c) -> p t c", c=SL)

        ident = sb("ident", [128, 128])
        ident_b = sb("ident_b", [128, 128], BF16)
        causal = sb("causal", [128, 128], BF16)
        minus_half = sb("minus_half", [128, 1])
        causal_t = sb("causal_t", [128, 128], BF16)
        patch_c = sb("patch_c", [XP, CT, NP])
        patch_mask = sb("patch_mask", [XP, NP])
        chan_sel = sb("chan_sel", [XP, XT, NQ])
        row_sel = sb("row_sel", [2, NQ], BF16)
        row_val = sb("row_val", [2, T], BF16)
        var_ones = sb("var_ones", [128, 1])
        iota_i = sb("iota_i", [128, E], I32)
        iota_f = sb("iota_f", [128, E])
        h0_w = sb("h0_w", [128, D])
        cen = sb("cen", [C + 1, D])
        cen_sum = sb("cen_sum", [C + 1, 1])
        cen_t = sb("cen_t", [128, 2, NQ])
        gram_w = sb("gram_w", [128, C + 1])
        wa = sb("wa", [128, 2, 3 * D])
        w1 = sb("w1", [128, 3 * D])
        wp1 = sb("wp1", [128, 3, D])
        wp2 = sb("wp2", [128, 3, D])
        nat_q = sb("nat_q", [GR, 6, D])
        nat_b = sb("nat_b", [GR, 6, E * RANK])
        nat_p = sb("nat_p", [GR, 2, 3, 4, 32])
        nat_a = sb("nat_a", [128, D])
        nat_g = sb("nat_g", [E, D])
        wx = sb("wx", [128, 3 * D])
        wb = sb("wb", [128, 3 * D])
        wh = sb("wh", [128, 3 * D])
        rx = sb("rx", [128, 128 + E])
        rb = sb("rb", [128, 128 + E])
        xs = sb("xs", [XP, XT, XF])
        part = sb("part", [XP, XT, NP])
        xa = sb("xa", [XP, XT, XF // 2])
        big = sb("big", [XP, XT, NP * NP])
        pt = sb("pt", [128, TP])
        ptk = sb("ptk", [128, TP])
        prod = sb("prod", [128, TP])
        tok_var = sb("tok_var", [128, 2])
        rstd_tok = sb("rstd_tok", [128, 2, NQ])
        ptn = sb("ptn", [128, TP])
        pieces = [sb(f"pieces{n}", [GR, 3, 4, T], BF16) for n in (1, 2)]
        rest = [sb(f"rest{n}", [GR, 4, T]) for n in (1, 2)]
        stack = [sb(f"stack{n}", [128, G, 4, T], BF16) for n in (1, 2)]
        kept = [nc.dram_tensor(f"kept{n}", (3, GR, 4 * T), BF16, kind="Internal").ap() for n in (1, 2)]
        mxp = [sb(f"mxp{n}", [128, 2, 2, 2, G], BF16) for n in (1, 2)]
        va = [sb(f"va{n}", [128, 2, H, 32]) for n in (1, 2)]
        mx = [sb(f"mx{n}", [128, 2, H]) for n in (1, 2)]
        p0 = [sb(f"p0_{n}", [128, H, T]) for n in (1, 2)]
        p1 = [sb("p1_1", [128, H, T1]), sb("p1_2", [128, H, T])]
        den = [sb(f"den{n}", [128, 3, T]) for n in (1, 2)]
        lnd = [sb(f"lnd{n}", [128, 3, T]) for n in (1, 2)]
        inv = [sb(f"inv{n}", [128, 3, T]) for n in (1, 2)]
        o_t = [sb(f"o_t{n}", [128, 3, TP]) for n in (1, 2)]
        h1 = sb("h1", [128, 2, D])
        h1k = sb("h1k", [128, 2, D])
        bst = sb("bst", [128, 2, 6])
        bag = sb("bag", [128, 2, 2])
        rstd = sb("rstd", [128, 2, 1])
        xh = sb("xh", [128, 2, D])
        xt0 = sb("xt0", [128, TP])
        xtb = sb("xtb", [128, TP])
        hwt = sb("hwt", [128, TP])
        rm = sb("rm", [128, 2])
        rl = sb("rl", [128, 2, E])
        re = sb("re", [128, 2, E])
        rs = sb("rs", [128, 2])
        ri = sb("ri", [128, 2])
        rp = sb("rp", [128, 2, E])
        rt = sb("rt", [128, 2, 8])
        rx_u = sb("rx_u", [128, 2, 8], U32)
        rx_f = sb("rx_f", [128, 2, 8])
        picked = sb("picked", [128, 2, 2, E])
        c2 = sb("c2", [128, 2, E])
        hw = sb("hw", [128, 2, E, RANK])
        y = sb("y", [128, 2, D])

        pe_done, act_done, dve_done, pool_done = (sem(s) for s in ("pe_done", "act_done", "dve_done", "pool_done"))
        done = {"pe": pe_done, "act": act_done, "dve": dve_done, "pool": pool_done}
        cleared = sem("cleared")
        loaded = sem("loaded")
        landed = {s: sem(f"{s}_landed") for s in SP_STEPS}
        first_kept = sem("first_kept")
        const_ready = sem("const_ready")
        prep_dve = sem("prep_dve")
        prep_pe = sem("prep_pe")
        prep_act = sem("prep_act")
        prep_pool = sem("prep_pool")
        ready = sem("ready")

        loads = []

        def load(dst, src):
            loads.append((dst, src))

        load(h0_w[0:C, :], cw)
        load(h0_w[C:C + 1, :], cls_tok.rearrange("a b d -> (a b) d"))
        load(h0_w[C + 1:C + 2, :], b_proj.rearrange("(a d) -> a d", a=1))
        load(cen[0:C, :], cw)
        load(cen[C:C + 1, :], cls_tok.rearrange("a b d -> (a b) d"))
        load(wa[:, 0, :], w_attn[0:128, :])
        load(wa[0:D - 128, 1, :], w_attn[128:D, :])
        load(w1[C + 1:C + 2, :], b_attn.rearrange("(a d) -> a d", a=1))
        wp_src = w_proj.rearrange("(t j d) n -> j d t n", j=4, d=DH)
        for j in range(4):
            load(wp1[32 * j:32 * j + DH, :, :], wp_src[j])
        load(nat_q[:, :, :], Wqkv.rearrange("(m p) d -> p m d", p=GR))
        bm_src = Bm.rearrange("e (m p) r -> m p e r", p=GR)
        pr_src = Wproj.rearrange("(m p) (t j d) -> m p t j d", p=GR, j=4, d=DH)
        for m in range(6):
            load(nat_b[:, m, :].rearrange("p (e r) -> p e r", e=E), bm_src[m])
        for m in range(2):
            for t in range(3):
                load(nat_p[:, m, t, :, 0:DH], pr_src[m, :, t])
            load(nat_p[:, m, 0, 0, DH:DH + 1], bproj.rearrange("(m p a) -> m p a", p=GR, a=1)[m])
        load(nat_a[:, :], A.rearrange("e r d -> (e r) d"))
        load(nat_g[:, :], Wg)
        load(wb[64:65, :], bqkv.rearrange("(a d) -> a d", a=1))
        load(wb[96:96 + E, :], bb)
        load(rb[64:65, 0:128], ba.rearrange("(a e) r -> a (e r)", a=1))
        load(rb[64:65, 128:128 + E], bg.rearrange("(a e) -> a e", a=1))

        clears = [(t, 0.0) for t in (h1, h1k, xh, o_t[0], o_t[1], xt0, hwt, y, part, big, xs, xa, mx[0], mx[1], mxp[0],
                                     mxp[1], rm, rl, rp, rt, rx_f, picked, c2, hw, bag, rx_u, p1[0], p1[1])]
        clears += [(t, 1.0) for t in (p0[0], p0[1], den[0], den[1], lnd[0], lnd[1], inv[0], inv[1],
                                      rs, ri, re, tok_var, rstd, bst, *wide, *narrow)]

        def x_tile(image, t):
            return x[bass.ds(image, 1), CT * t:CT * (t + 1)].rearrange(
                "b c (i h r) w -> (b c i h) (r w)", h=2, r=P // 2)

        N_READY = 5
        PREP_DVE = 7 + len(clears)
        paused = {n: sem(f"{n}_paused") for n in ("pool", "pe", "dve", "sp")}

        def hold(e, name):
            e.sem_inc(paused[name], 1)

        block = ctx.enter_context(nc.Block())

        @block.sync
        def _(sp):
            sp.wait_ge(cleared, 1)
            for dst, src in loads:
                sp.dma_start(dst, src).then_inc(loaded, 16)
            sp.wait_ge(const_ready, 1)
            for n in range(2):
                for piece in range(3):
                    sp.dma_start(kept[n][piece],
                                 pieces[n][:, piece].rearrange("p m t -> p (m t)")).then_inc(first_kept, 16)
            sp.wait_ge(first_kept, 6 * 16)
            for s in SP_STEPS:
                sp.sem_inc(landed[s], 16 * N_DMAS[s] * HEAD_START)
            sp.sem_inc(ready, 1)
            sp.wait_ge(ready, N_READY)

            places = (((0, 0, 4), (2, 0, 2), (3, 2, 4), (4, 0, 2), (5, 2, 4)),
                      ((1, 0, 4), (2, 2, 4), (3, 0, 2)),
                      ((4, 2, 4), (5, 0, 2)))

            def stack_piece(n, piece, signal):
                for block, m0, m1 in places[piece]:
                    sp.dma_start(stack[n][DH * block:DH * block + DH, :, m0:m1, :].rearrange("d j m t -> d j (m t)"),
                                 kept[n][piece, :, m0 * T:m1 * T].rearrange("(j d) x -> d j x", d=DH)
                                 ).then_inc(signal, 16)

            with sp.Fori(0, N_IT) as it:
                loading = sp.snap((it + (B - BEHIND["load0"])) % B)
                storing = sp.snap((it + (B - BEHIND["store"])) % B)
                sp.wait_ge(pool_done, at(it, "load1", before=("halves1",)))
                hold(sp, "sp")
                sp.dma_start(xs[:, 1, :], x_tile(loading, 1)).then_inc(landed["load1"], 16)
                sp.wait_ge(act_done, at(it, "keep_high1", "high1"))
                hold(sp, "sp")
                sp.wait_ge(landed["stack_high1"], landed_at(it, "keep_high1", "stack_high1", age=1))
                hold(sp, "sp")
                sp.dma_start(kept[0][0],
                             pieces[0][:, 0].rearrange("p m t -> p (m t)")).then_inc(landed["keep_high1"], 16)
                sp.wait_ge(pool_done, at(it, "keep_low1", "low1"))
                hold(sp, "sp")
                sp.wait_ge(landed["stack_low1"], landed_at(it, "keep_low1", "stack_low1", age=1))
                hold(sp, "sp")
                sp.dma_start(kept[0][2],
                             pieces[0][:, 2].rearrange("p m t -> p (m t)")).then_inc(landed["keep_low1"], 16)
                sp.wait_ge(pool_done, at(it, "load2", before=("halves2",)))
                hold(sp, "sp")
                sp.dma_start(xs[:, 2, :], x_tile(loading, 2)).then_inc(landed["load2"], 16)
                sp.wait_ge(pe_done, at(it, "stack_high1",
                        before=("mx1_0", "mx1_1", "mx1_2", "mx1_3", "mx1_4", "st1_0", "st1_1", "st1_2",
                        "st1_3")))
                hold(sp, "sp")
                sp.wait_ge(landed["keep_high1"], landed_at(it, "stack_high1", "keep_high1"))
                hold(sp, "sp")
                stack_piece(0, 0, landed["stack_high1"])
                sp.wait_ge(act_done, at(it, "keep_middle1", "middle1"))
                hold(sp, "sp")
                sp.wait_ge(landed["stack_middle1"], landed_at(it, "keep_middle1", "stack_middle1", age=1))
                hold(sp, "sp")
                sp.dma_start(kept[0][1],
                             pieces[0][:, 1].rearrange("p m t -> p (m t)")).then_inc(landed["keep_middle1"], 16)
                sp.wait_ge(pool_done, at(it, "load0", before=("halves0",)))
                hold(sp, "sp")
                sp.dma_start(xs[:, 0, :], x_tile(loading, 0)).then_inc(landed["load0"], 16)
                sp.wait_ge(landed["keep_low1"], landed_at(it, "stack_low1", "keep_low1"))
                hold(sp, "sp")
                stack_piece(0, 2, landed["stack_low1"])
                sp.wait_ge(landed["keep_middle1"], landed_at(it, "stack_middle1", "keep_middle1"))
                hold(sp, "sp")
                stack_piece(0, 1, landed["stack_middle1"])
                sp.wait_ge(act_done, at(it, "keep_high2", "high2"))
                hold(sp, "sp")
                sp.wait_ge(landed["stack_high2"], landed_at(it, "keep_high2", "stack_high2", age=1))
                hold(sp, "sp")
                sp.dma_start(kept[1][0],
                             pieces[1][:, 0].rearrange("p m t -> p (m t)")).then_inc(landed["keep_high2"], 16)
                sp.wait_ge(act_done, at(it, "keep_middle2", "middle2"))
                hold(sp, "sp")
                sp.wait_ge(landed["stack_middle2"], landed_at(it, "keep_middle2", "stack_middle2", age=1))
                hold(sp, "sp")
                sp.dma_start(kept[1][1],
                             pieces[1][:, 1].rearrange("p m t -> p (m t)")).then_inc(landed["keep_middle2"], 16)
                sp.wait_ge(pool_done, at(it, "keep_low2", "low2"))
                hold(sp, "sp")
                sp.wait_ge(landed["stack_low2"], landed_at(it, "keep_low2", "stack_low2", age=1))
                hold(sp, "sp")
                sp.dma_start(kept[1][2],
                             pieces[1][:, 2].rearrange("p m t -> p (m t)")).then_inc(landed["keep_low2"], 16)
                sp.wait_ge(pe_done, at(it, "stack_high2",
                        before=("mx2_0", "mx2_1", "mx2_2", "mx2_3", "mx2_4", "mx2_5", "st2_0", "st2_1", "st2_2",
                        "st2_3", "st2_4", "st2_5")))
                hold(sp, "sp")
                sp.wait_ge(landed["keep_high2"], landed_at(it, "stack_high2", "keep_high2"))
                hold(sp, "sp")
                stack_piece(1, 0, landed["stack_high2"])
                sp.wait_ge(landed["keep_middle2"], landed_at(it, "stack_middle2", "keep_middle2"))
                hold(sp, "sp")
                stack_piece(1, 1, landed["stack_middle2"])
                sp.wait_ge(landed["keep_low2"], landed_at(it, "stack_low2", "keep_low2"))
                hold(sp, "sp")
                stack_piece(1, 2, landed["stack_low2"])
                sp.wait_ge(dve_done, at(it, "store", "result"))
                hold(sp, "sp")
                sp.dma_start(out[bass.ds(storing, 1), 0:T0].rearrange("b t d -> (b t) d"),
                             y[:, 0, :]).then_inc(landed["store"], 16)
                sp.dma_start(out[bass.ds(storing, 1), T0:T].rearrange("b t d -> (b t) d"),
                             y[0:T1, 1, :]).then_inc(landed["store"], 16)
            for s in SP_STEPS:
                sp.wait_ge(landed[s], 16 * N_DMAS[s] * (HEAD_START + N_IT))

        @block.gpsimd
        def _(pool):
            n = [0]

            def step(ins):
                n[0] += 1
                ins.then_inc(prep_pool, 1)
                pool.wait_ge(prep_pool, n[0])

            for tile in (wp1, nat_p, wb, w1, h0_w, rb, gram_w):
                pool.memset(tile[:], 0.0).then_inc(prep_pool, 1)
            n[0] += 7
            pool.wait_ge(prep_pool, 7)
            pool.sem_inc(cleared, 1)
            for tile, v in ((ident, 0.0), (causal, 0.0), (causal_t, 0.0), (minus_half, -0.5), (patch_c, 1.0),
                            (chan_sel, 1.0), (row_sel, 0.0), (row_val, 1.0), (var_ones, 1.0), (rstd_tok, 1.0),
                            (prod, 0.0), (pt, 0.0), (ptk, 0.0), (ptn, 0.0), (va[0], 1.0), (va[1], 1.0),
                            (stack[0], 0.0), (stack[1], 0.0), (pieces[0], 0.0), (pieces[1], 0.0),
                            (rest[0], 0.0), (rest[1], 0.0), (xtb, 0.0)):
                pool.memset(tile[:], v).then_inc(prep_pool, 1)
                n[0] += 1
            pool.iota(iota_i[:], pattern=[[1, E]], base=0, channel_multiplier=0).then_inc(prep_pool, 1)
            n[0] += 1
            pool.wait_ge(prep_pool, n[0])

            def select(tile, op, fill, base, pattern, cm):
                step(pool.affine_select(out=tile, in_=tile, compare_op=op, fill=fill, base=base,
                                        pattern=pattern, channel_multiplier=cm))

            select(ident[:], ALU.not_equal, 1.0, 0, [[-1, 128]], 1)
            select(causal[:], ALU.is_ge, NEG, 0, [[-1, 128]], 1)
            select(causal_t[:], ALU.is_ge, NEG, 0, [[1, 128]], -1)
            select(patch_c[:], ALU.is_ge, 0.0, 0, [[-2 * NP, CT], [-2, NP]], 1)
            select(patch_c[:], ALU.is_ge, 0.0, 1, [[2 * NP, CT], [2, NP]], -1)
            select(chan_sel[:], ALU.is_ge, 0.0, 0, [[XP, XT], [-2 * NP, NQ]], 1)
            select(chan_sel[:], ALU.is_ge, 0.0, 2 * NP - 1, [[-XP, XT], [2 * NP, NQ]], -1)
            select(row_sel[:], ALU.not_equal, 1.0, C, [[-1, NQ]], 1)
            select(row_val[:], ALU.is_ge, 0.0, 0, [[-1, T]], 1000)
            for i in range(2):
                for piece in range(2):
                    select(stack[i][GR:KR, :, 2:4, :], ALU.not_equal, 1.0, -G * piece, [[-1, G], [0, 2], [0, T]], 1)
            step(pool.memset(xtb[64:65, :], 1.0))
            step(pool.tensor_copy(ident_b[:], ident[:]))
            step(pool.tensor_copy(iota_f[:], iota_i[:]))
            pool.sem_inc(const_ready, 1)
            pool.wait_ge(prep_dve, PREP_DVE)
            pool.sem_inc(pool_done, HEAD_START * len(POOL_STEPS))
            pool.sem_inc(ready, 1)
            pool.wait_ge(ready, N_READY)

            with pool.Fori(0, N_IT) as it:
                pool.wait_ge(dve_done, at(it, "halves1", before=("pooling1",)))
                pool.wait_ge(landed["load1"], landed_at(it, "halves1", "load1"))
                pool.tensor_tensor(xa[:, 1, :], xs[:, 1, 0:XF // 2], xs[:, 1, XF // 2:XF],
                                   ALU.add).then_inc(pool_done, 1)
                pool.wait_ge(act_done, at(it, "low1", "middle1"))
                pool.wait_ge(landed["keep_low1"], landed_at(it, "low1", "keep_low1", age=1))
                pool.tensor_tensor(pieces[0][:, 2], rest[0][:], pieces[0][:, 1], ALU.subtract
                    ).then_inc(pool_done, 1)
                pool.wait_ge(act_done, at(it, "low2", "middle2"))
                pool.wait_ge(landed["keep_low2"], landed_at(it, "low2", "keep_low2", age=1))
                pool.tensor_tensor(pieces[1][:, 2], rest[1][:], pieces[1][:, 1], ALU.subtract
                    ).then_inc(pool_done, 1)
                pool.wait_ge(dve_done, at(it, "halves2", before=("pooling2",)))
                pool.wait_ge(landed["load2"], landed_at(it, "halves2", "load2"))
                pool.tensor_tensor(xa[:, 2, :], xs[:, 2, 0:XF // 2], xs[:, 2, XF // 2:XF],
                                   ALU.add).then_inc(pool_done, 1)
                pool.wait_ge(dve_done, at(it, "halves0", before=("pooling0",)))
                pool.wait_ge(landed["load0"], landed_at(it, "halves0", "load0"))
                pool.tensor_tensor(xa[:, 0, :], xs[:, 0, 0:XF // 2], xs[:, 0, XF // 2:XF],
                                   ALU.add).then_inc(pool_done, 1)
                pool.wait_ge(act_done, at(it, "hidden_kept", "hidden"))
                pool.wait_ge(dve_done, at(it, "hidden_kept", before=("result",)))
                hold(pool, "pool")
                pool.tensor_copy(h1k[:], h1[:]).then_inc(pool_done, 1)
                pool.wait_ge(dve_done, at(it, "rows2", "pooling2"))
                pool.wait_ge(pe_done, at(it, "rows2", before=("pooled",)))
                pool.tensor_tensor(
                    big[:, 2, :].rearrange("p (i j) -> p i j", i=NP),
                    part[:, 2, :].unsqueeze(1).broadcast_to([XP, NP, NP]),
                    patch_mask[:, :].unsqueeze(2).broadcast_to([XP, NP, NP]), ALU.mult).then_inc(pool_done, 1)
                pool.wait_ge(dve_done, at(it, "rows1", "pooling1"))
                pool.tensor_tensor(
                    big[:, 1, :].rearrange("p (i j) -> p i j", i=NP),
                    part[:, 1, :].unsqueeze(1).broadcast_to([XP, NP, NP]),
                    patch_mask[:, :].unsqueeze(2).broadcast_to([XP, NP, NP]), ALU.mult).then_inc(pool_done, 1)
                pool.wait_ge(act_done, at(it, "pooled_kept", "pooled_rows"))
                pool.wait_ge(pe_done, at(it, "pooled_kept", before=("out1",)))
                hold(pool, "pool")
                pool.tensor_copy(ptk[0:NQ, 0:T], pt[0:NQ, 0:T]).then_inc(pool_done, 1)
                pool.wait_ge(dve_done, at(it, "rows0", "pooling0"))
                pool.tensor_tensor(
                    big[:, 0, :].rearrange("p (i j) -> p i j", i=NP),
                    part[:, 0, :].unsqueeze(1).broadcast_to([XP, NP, NP]),
                    patch_mask[:, :].unsqueeze(2).broadcast_to([XP, NP, NP]), ALU.mult).then_inc(pool_done, 1)
                pool.wait_ge(dve_done, at(it, "deviation1", "variance"))
                hold(pool, "pool")
                pool.tensor_tensor(tok_var[:], tok_var[:], minus_half[:, :].broadcast_to([128, 2]), ALU.pow
                    ).then_inc(pool_done, 1)
                pool.wait_ge(dve_done, at(it, "deviation2", "token_var"))
                hold(pool, "pool")
                pool.tensor_tensor(rstd[:], rstd[:], minus_half[:, :].unsqueeze(1).broadcast_to([128, 2, 1]), ALU.pow
                    ).then_inc(pool_done, 1)

        @block.tensor
        def _(pe):
            pe.wait_ge(const_ready, 1)
            pe.wait_ge(loaded, 16 * len(loads))
            pe.wait_ge(prep_dve, PREP_DVE - 3)
            for c, (a, b) in enumerate(((0, 128), (128, D))):
                ins = pe.transpose(slots[0][0:b - a, SL * c:SL * c + C + 1], cen[:, a:b], ident[0:C + 1, 0:C + 1])
            ins.then_inc(prep_pe, 1)
            for m in range(6):
                if m >= 1:
                    pe.wait_ge(prep_act, 3 * m)
                pe.transpose(slots[1][:, 0:GR], nat_q[:, m, 0:128], ident[0:GR, 0:GR])
                pe.transpose(slots[2][0:D - 128, 0:GR], nat_q[:, m, 128:D], ident[0:GR, 0:GR])
                pe.transpose(slots[3][:, 0:GR], nat_b[:, m, :], ident[0:GR, 0:GR]).then_inc(prep_pe, 1)
            for m in range(2):
                for t in range(3):
                    pe.wait_ge(prep_act, 18 + 3 * m + t)
                    pe.transpose(slots[1][:, 0:GR], nat_p[:, m, t].rearrange("p j d -> p (j d)"),
                                 ident[0:GR, 0:GR]).then_inc(prep_pe, 1)
            pe.wait_ge(prep_act, 24)
            pe.transpose(slots[1][:, 0:128], nat_a[:, 0:128], ident[:])
            pe.transpose(slots[1][:, 128:128 + E], nat_g[:, 0:128], ident[0:E, 0:E])
            pe.transpose(slots[2][0:D - 128, 0:128], nat_a[:, 128:D], ident[:])
            pe.transpose(slots[2][0:D - 128, 128:128 + E], nat_g[:, 128:D], ident[0:E, 0:E]).then_inc(prep_pe, 1)
            pe.wait_ge(prep_dve, PREP_DVE - 1)
            pe.wait_ge(prep_act, 26)
            for half in range(2):
                cols = slice(3 * D // 2 * half, 3 * D // 2 * (half + 1))
                for c, n in enumerate((128, D - 128)):
                    pe.matmul(slots[3][0:C + 1, 2 * SL * half:2 * SL * half + 3 * D // 2],
                              cen_t[0:n, c, 0:C + 1], wa[0:n, c, cols], start=(c == 0), stop=(c == 1))
            for c, n in enumerate((128, D - 128)):
                ins = pe.matmul(slots[1][0:C + 1, 0:C + 1], cen_t[0:n, c, 0:C + 1], cen_t[0:n, c, 0:C + 1],
                                start=(c == 0), stop=(c == 1))
            ins.then_inc(prep_pe, 1)
            pe.sem_inc(pe_done, HEAD_START * len(PE_STEPS))
            pe.sem_inc(ready, 1)
            pe.wait_ge(ready, N_READY)

            with pe.Fori(0, N_IT) as it:
                def claim(step, after=()):
                    users = [s for s in PE_STEPS if SLOTS[s] == SLOTS[step]]
                    i = users.index(step)
                    previous = users[i - 1]
                    backs = [(int(i == 0) + BEHIND[previous] - BEHIND[r], r) for r in READERS[previous]]
                    backs += [(BEHIND[step] - BEHIND[r], r) for r in after]
                    for engine in done:
                        mine = [(-back, list(STEPS[engine]).index(r), r) for back, r in backs if ENGINE[r] == engine]
                        if mine:
                            back, _, last = max(mine)
                            pe.wait_ge(done[engine], count(it, last, -back))

                def shifted(n, step, heads, keys, queries):
                    k0, k1 = keys
                    w = k1 - k0
                    for i, h in enumerate(heads):
                        if n == 0 and k0:
                            dst = slot[step][0:w, 512 * (i // G) + 80 * (i % G):512 * (i // G) + 80 * (i % G) + T - queries]
                        else:
                            dst = slot[step][0:w, SL * i:SL * i + T]
                        ins = pe.matmul(dst, stack[n][:, h % G, 2 + h // G, k0:k1], stack[n][:, h % G, h // G, queries:T],
                                        start=True, stop=(n == 1))
                        if n == 0:
                            ins = pe.matmul(dst[:, 0:w], ident_b[0:w, 0:w], causal_t[0:w, 0:w], start=False, stop=True)
                    ins.then_inc(pe_done, 1)

                def raw(n, step, tile, heads):
                    q0, q1 = (0, T0) if tile == 0 else (T0, T)
                    rows = q1 - q0
                    nk, pitch = (T0, T0) if n == 0 and tile == 0 else (T, SL)
                    masked = n == 0
                    per_bank = 2 * SL // pitch
                    for b in range(len(heads) // per_bank):
                        bank = slot[step][0:rows, 2 * SL * b:2 * SL * b + 2 * SL].rearrange("p (h k) -> p h k", k=pitch)
                        first = masked and tile == 0
                        if first:
                            pe.matmul(bank, ident_b[:], causal[:].unsqueeze(1).broadcast_to([128, per_bank, 128]),
                                      start=True, stop=False)
                        for k in range(per_bank):
                            h = heads[per_bank * b + k]
                            ins = pe.matmul(bank[:, k, 0:nk], stack[n][0:GR, h % G, h // G, q0:q1],
                                            stack[n][0:GR, h % G, 2 + h // G, 0:nk],
                                            start=not first, stop=(not masked or (first and k == per_bank - 1)))
                            if masked and not first:
                                ins = pe.matmul(bank[:, k, T0:T], ident_b[0:rows, 0:rows], causal[0:rows, 0:T1],
                                                start=False, stop=True)
                    ins.then_inc(pe_done, 1)

                def turn_maxima(n, step):
                    for g in range(2):
                        for t, (a, b) in enumerate(((0, T0), (T0, T))):
                            ins = pe.matmul(slot[step][0:KR - GR, SL * g + a:SL * g + b],
                                            mxp[n][0:b - a, t, g].rearrange("p c j -> p (c j)"), ident_b[0:b - a, 0:b - a],
                                            start=True, stop=True)
                    ins.then_inc(pe_done, 1)

                def values(n, step):
                    q1 = T0 if n == 0 else 0
                    for t in range(3):
                        for j in range(4):
                            pe.matmul(slot[step][32 * j:32 * j + 32, SL * t:SL * t + T], va[n][:, 0, 4 * t + j, :],
                                      p0[n][:, 4 * t + j, :], start=True, stop=False)
                        for j in range(4):
                            ins = pe.matmul(slot[step][32 * j:32 * j + 32, SL * t + q1:SL * t + T],
                                            va[n][:, 1, 4 * t + j, :], p1[n][:, 4 * t + j, :], start=False, stop=True)
                    ins.then_inc(pe_done, 1)

                chunks = ((xt0, wx), (xtb, wb), (hwt, wh))
                claim("mx1_2")
                pe.wait_ge(landed["stack_high1"], landed_at(it, "mx1_2", "stack_high1"))
                pe.wait_ge(landed["stack_middle1"], landed_at(it, "mx1_2", "stack_middle1"))
                pe.wait_ge(landed["stack_low1"], landed_at(it, "mx1_2", "stack_low1"))
                raw(0, "mx1_2", 1, range(0, 4))
                claim("mx1_1")
                raw(0, "mx1_1", 0, range(8, 12))
                claim("mx1_4")
                raw(0, "mx1_4", 1, range(8, 12))
                claim("mx1_3")
                raw(0, "mx1_3", 1, range(4, 8))
                claim("mx1_0")
                raw(0, "mx1_0", 0, range(0, 8))
                claim("out2", after=("heads2",))
                for tt in range(2):
                    for t in range(3):
                        ins = pe.matmul(slot["out2"][:, SL * tt:SL * tt + D], o_t[1][:, t, 128 * tt:128 * tt + 128],
                                        wp2[:, t, :], start=(t == 0), stop=(t == 2))
                ins.then_inc(pe_done, 1)
                claim("mt1", after=("max_low1",))
                hold(pe, "pe")
                turn_maxima(0, "mt1")
                claim("v1", after=("scaled",))
                hold(pe, "pe")
                for t in range(2):
                    ins = pe.matmul(slot["v1"][:, SL * t:SL * t + D], ptn[:, 128 * t:128 * t + 128], w1[:, 2 * D:3 * D],
                                    start=True, stop=True)
                ins.then_inc(pe_done, 1)
                claim("st1_2", after=("shift1_1",))
                shifted(0, "st1_2", range(8, 12), (0, T0), 0)
                claim("st1_3", after=("shift1_0", "shift1_1"))
                shifted(0, "st1_3", range(H), (T0, T), T0)
                claim("st1_0", after=("shift1_0",))
                shifted(0, "st1_0", range(0, 4), (0, T0), 0)
                claim("st1_1")
                shifted(0, "st1_1", range(4, 8), (0, T0), 0)
                claim("mx2_3")
                pe.wait_ge(landed["stack_high2"], landed_at(it, "mx2_3", "stack_high2"))
                pe.wait_ge(landed["stack_middle2"], landed_at(it, "mx2_3", "stack_middle2"))
                pe.wait_ge(landed["stack_low2"], landed_at(it, "mx2_3", "stack_low2"))
                raw(1, "mx2_3", 1, range(0, 4))
                claim("mx2_4")
                raw(1, "mx2_4", 1, range(4, 8))
                claim("av1", after=("probs1_0", "probs1_1", "probs1_2", "probs1_3", "values1"))
                hold(pe, "pe")
                values(0, "av1")
                claim("mx2_2")
                raw(1, "mx2_2", 0, range(8, 12))
                claim("mx2_0")
                raw(1, "mx2_0", 0, range(0, 4))
                claim("pooled", after=("rows0", "rows1", "rows2"))
                hold(pe, "pe")
                pe.matmul(slot["pooled"][0:NQ, 0:T], row_sel[:], row_val[:], start=True, stop=False)
                for t in range(XT):
                    ins = pe.matmul(slot["pooled"][0:NQ, 1:T], chan_sel[:, t, :], big[:, t, :],
                                    start=False, stop=(t == XT - 1))
                ins.then_inc(pe_done, 1)
                claim("v2", after=("xt_low", "xt_high", "hwt_rows", "weight_rows"))
                for tt in range(2):
                    for c, (act_rows, w) in enumerate(chunks):
                        ins = pe.matmul(slot["v2"][:, SL * tt:SL * tt + D], act_rows[:, 128 * tt:128 * tt + 128],
                                        w[:, 2 * D:3 * D], start=(c == 0), stop=(c == 2))
                ins.then_inc(pe_done, 1)
                claim("gram", after=("pooled_rows",))
                hold(pe, "pe")
                pe.matmul(slot["gram"][0:C + 1, 0:T], gram_w[:], pt[:, 0:T], start=True, stop=True
                    ).then_inc(pe_done, 1)
                claim("mx2_1")
                raw(1, "mx2_1", 0, range(4, 8))
                claim("mx2_5")
                raw(1, "mx2_5", 1, range(8, 12))
                claim("var", after=("prod",))
                hold(pe, "pe")
                for t in range(2):
                    ins = pe.matmul(slot["var"][:, t:t + 1], prod[:, 128 * t:128 * t + 128], var_ones[:], start=True, stop=True)
                ins.then_inc(pe_done, 1)
                claim("out1", after=("pooled_kept", "heads1"))
                hold(pe, "pe")
                for tt in range(2):
                    tok = slice(128 * tt, 128 * tt + 128)
                    pe.matmul(slot["out1"][:, SL * tt:SL * tt + D], ptk[:, tok], h0_w[:], start=True, stop=False)
                    for t in range(3):
                        ins = pe.matmul(slot["out1"][:, SL * tt:SL * tt + D], o_t[0][:, t, tok], wp1[:, t, :],
                                        start=False, stop=(t == 2))
                ins.then_inc(pe_done, 1)
                claim("spread", after=("deviation_cols",))
                for t, (a, b) in enumerate(((0, T0), (T0, T))):
                    ins = pe.matmul(slot["spread"][0:NQ, a:b], rstd_tok[0:b - a, t, :], ident[0:b - a, 0:b - a],
                                    start=True, stop=True)
                ins.then_inc(pe_done, 1)
                claim("mt2", after=("max_low2",))
                hold(pe, "pe")
                turn_maxima(1, "mt2")
                claim("qk1", after=("scaled",))
                hold(pe, "pe")
                for m in range(4):
                    ins = pe.matmul(slot["qk1"][0:GR, SL * m:SL * m + T], w1[:, GR * m:GR * m + GR], ptn[:, 0:T],
                                    start=True, stop=True)
                ins.then_inc(pe_done, 1)
                claim("xt", after=("normal",))
                for t in range(2):
                    pe.transpose(slot["xt"][:, 128 * t:128 * t + 128], xh[:, t, 0:128], ident[:])
                for t in range(2):
                    ins = pe.transpose(slot["xt"][0:D - 128, SL + 128 * t:SL + 128 * t + 128], xh[:, t, 128:D], ident[:])
                ins.then_inc(pe_done, 1)
                claim("st2_0", after=("shift2_0",))
                shifted(1, "st2_0", range(0, 4), (0, T0), 0)
                claim("st2_2", after=("shift2_1",))
                shifted(1, "st2_2", range(8, 12), (0, T0), 0)
                claim("route", after=("xt_low", "xt_high"))
                for tt in range(2):
                    tok = slice(128 * tt, 128 * tt + 128)
                    pe.matmul(slot["route"][:, SL * tt:SL * tt + 128 + E], xt0[:, tok], rx[:], start=True, stop=False)
                    ins = pe.matmul(slot["route"][:, SL * tt:SL * tt + 128 + E], xtb[:, tok], rb[:], start=False, stop=True)
                ins.then_inc(pe_done, 1)
                claim("st2_1", after=("shift2_0", "shift2_1"))
                shifted(1, "st2_1", range(4, 8), (0, T0), 0)
                claim("st2_3")
                shifted(1, "st2_3", range(0, 4), (T0, T), 0)
                claim("st2_5")
                shifted(1, "st2_5", range(8, 12), (T0, T), 0)
                claim("st2_4")
                shifted(1, "st2_4", range(4, 8), (T0, T), 0)
                claim("hwt", after=("weighted",))
                for tt in range(2):
                    pe.transpose(slot["hwt"][:, 128 * tt:128 * tt + 128], hw[:, tt].rearrange("p e r -> p (e r)"), ident[:])
                for tt in range(2):
                    ins = pe.transpose(slot["hwt"][0:E, SL + 128 * tt:SL + 128 * tt + 128], c2[:, tt, :], ident[:])
                ins.then_inc(pe_done, 1)
                claim("av2",
                        after=("probs2_0", "probs2_1", "probs2_2", "probs2_3", "probs2_4", "probs2_5",
                        "values2"))
                hold(pe, "pe")
                values(1, "av2")
                claim("qk2", after=("xt_low", "xt_high", "hwt_rows", "weight_rows"))
                for m in range(4):
                    for c, (act_rows, w) in enumerate(chunks):
                        ins = pe.matmul(slot["qk2"][0:GR, SL * m:SL * m + T], w[:, GR * m:GR * m + GR], act_rows[:, 0:T],
                                        start=(c == 0), stop=(c == 2))
                ins.then_inc(pe_done, 1)

        @block.scalar
        def _(act):
            for m in range(6):
                cols = slice(GR * m, GR * m + GR)
                act.wait_ge(prep_pe, m + 2)
                act.activation(wx[:, cols], slots[1][:, 0:GR], ACT.Copy).then_inc(prep_act, 1)
                act.activation(wb[0:D - 128, cols], slots[2][0:D - 128, 0:GR], ACT.Copy).then_inc(prep_act, 1)
                act.activation(wh[:, cols], slots[3][:, 0:GR], ACT.Copy, scale=SCALING).then_inc(prep_act, 1)
            for m in range(2):
                for t in range(3):
                    act.wait_ge(prep_pe, 8 + 3 * m + t)
                    act.activation(wp2[:, t, GR * m:GR * m + GR], slots[1][:, 0:GR], ACT.Copy).then_inc(prep_act, 1)
            act.wait_ge(prep_pe, 14)
            act.activation(rx[:], slots[1][:, 0:128 + E], ACT.Copy).then_inc(prep_act, 1)
            act.activation(rb[0:D - 128, :], slots[2][0:D - 128, 0:128 + E], ACT.Copy).then_inc(prep_act, 1)
            act.wait_ge(prep_pe, 15)
            act.activation(w1[0:C + 1, :].rearrange("p (h n) -> p h n", h=2),
                           slots[3][0:C + 1, :].rearrange("p (h n) -> p h n", h=2)[:, :, 0:3 * D // 2],
                           ACT.Copy).then_inc(prep_act, 1)
            act.activation(gram_w[0:C + 1, :], slots[1][0:C + 1, 0:C + 1], ACT.Copy, scale=1.0 / D).then_inc(prep_act, 1)
            act.wait_ge(prep_act, 28)
            act.sem_inc(act_done, HEAD_START * len(ACT_STEPS))
            act.sem_inc(ready, 1)
            act.wait_ge(ready, N_READY)

            act.preload_act_table_set("natural_log_exp_and_others")
            with act.Fori(0, N_IT) as it:
                def copy(dst, src, scale=1.0):
                    act.activation(dst, src, ACT.Copy, scale=scale).then_inc(act_done, 1)

                act.wait_ge(pe_done, at(it, "shift1_1", "mt1", before=("st1_1", "st1_2", "st1_3")))
                copy(stack[0][GR:KR, :, 1, :],
                     tiles("mt1", KR - GR)[:, 1, 0:T].unsqueeze(1).broadcast_to([KR - GR, G, T]))
                act.wait_ge(pe_done, at(it, "shift1_0", before=("st1_0", "st1_1", "st1_3")))
                copy(stack[0][GR:KR, :, 0, :],
                     tiles("mt1", KR - GR)[:, 0, 0:T].unsqueeze(1).broadcast_to([KR - GR, G, T]))
                act.wait_ge(pe_done, at(it, "probs1_2", "st1_2", before=("av1",)))
                act.activation(p0[0][:, 8:12, :], tiles("st1_2")[:, :, 0:T], ACT.Exp, scale=SC1
                    ).then_inc(act_done, 1)
                act.wait_ge(pe_done, at(it, "values1", "v1"))
                copy(va[0][:, :, :, 0:DH], tiles("v1")[:, 0:2, 0:D].rearrange("p t (h d) -> p t h d", h=H))
                act.wait_ge(pe_done, at(it, "probs1_3", "st1_3"))
                act.activation(
                    p1[0][0:T1].rearrange("p (b h) q -> p b h q", b=2),
                    slot["st1_3"][0:T1, :].rearrange("p (b n) -> p b n", b=2)[:, :, 0:80 * G].rearrange(
                        "p b (h n) -> p b h n", h=G)[:, :, :, 0:T1],
                    ACT.Exp, scale=SC1).then_inc(act_done, 1)
                act.wait_ge(pe_done, at(it, "probs1_0", "st1_0"))
                act.activation(p0[0][:, 0:4, :], tiles("st1_0")[:, :, 0:T], ACT.Exp, scale=SC1
                    ).then_inc(act_done, 1)
                act.wait_ge(pe_done, at(it, "probs1_1", "st1_1"))
                act.activation(p0[0][:, 4:8, :], tiles("st1_1")[:, :, 0:T], ACT.Exp, scale=SC1
                    ).then_inc(act_done, 1)
                act.wait_ge(dve_done, at(it, "log1", "den1"))
                act.activation(lnd[0][:], den[0][:], ACT.Ln).then_inc(act_done, 1)
                act.wait_ge(act_done, at(it, "inverse1", "log1"))
                act.activation(inv[0][:], lnd[0][:], ACT.Exp, scale=-1.0).then_inc(act_done, 1)
                act.wait_ge(pe_done, at(it, "pooled_rows", "pooled"))
                act.wait_ge(dve_done, at(it, "pooled_rows", before=("prod", "scaled")))
                act.wait_ge(pool_done, at(it, "pooled_rows", before=("pooled_kept",)))
                copy(pt[0:NQ, 0:T], slot["pooled"][0:NQ, 0:T])
                act.wait_ge(pe_done, at(it, "values2", "v2", before=("av2",)))
                copy(va[1][:, :, :, 0:DH], tiles("v2")[:, 0:2, 0:D].rearrange("p t (h d) -> p t h d", h=H))
                act.wait_ge(pe_done, at(it, "hidden", "out1"))
                act.wait_ge(pool_done, at(it, "hidden", before=("hidden_kept",)))
                act.wait_ge(dve_done, at(it, "hidden", before=("stats", "normal")))
                copy(h1[:], tiles("out1")[:, 0:2, 0:D])
                act.wait_ge(pe_done, at(it, "shift2_0", "mt2", before=("st2_0", "st2_1", "st2_3", "st2_4")))
                copy(stack[1][GR:KR, :, 0, :],
                     tiles("mt2", KR - GR)[:, 0, 0:T].unsqueeze(1).broadcast_to([KR - GR, G, T]))
                act.wait_ge(pe_done, at(it, "shift2_1", before=("st2_1", "st2_2", "st2_4", "st2_5")))
                copy(stack[1][GR:KR, :, 1, :],
                     tiles("mt2", KR - GR)[:, 1, 0:T].unsqueeze(1).broadcast_to([KR - GR, G, T]))
                act.wait_ge(pe_done, at(it, "high1", "qk1"))
                act.wait_ge(dve_done, at(it, "high1", before=("rest1",)))
                act.wait_ge(landed["keep_high1"], landed_at(it, "high1", "keep_high1", age=1))
                copy(pieces[0][:, 0], tiles("qk1", GR)[:, :, 0:T])
                act.wait_ge(pe_done, at(it, "xt_high", "xt", before=("route", "qk2", "v2")))
                copy(xtb[0:D - 128, :], slot["xt"][0:D - 128, SL:2 * SL])
                copy(xt0[:], slot["xt"][:, 0:SL])
                act.wait_ge(dve_done, at(it, "middle1", "rest1"))
                act.wait_ge(pool_done, at(it, "middle1", before=("low1",)))
                act.wait_ge(landed["keep_middle1"], landed_at(it, "middle1", "keep_middle1", age=1))
                copy(pieces[0][:, 1], rest[0][:])
                act.wait_ge(pe_done, at(it, "probs2_0", "st2_0"))
                act.activation(p0[1][:, 0:4, :], tiles("st2_0")[:, :, 0:T], ACT.Exp, scale=SC2
                    ).then_inc(act_done, 1)
                act.wait_ge(dve_done, at(it, "rexp", "rsub", before=("rsum", "rprob")))
                act.activation(re[:], rl[:], ACT.Exp).then_inc(act_done, 1)
                act.wait_ge(pe_done, at(it, "probs2_2", "st2_2"))
                act.activation(p0[1][:, 8:12, :], tiles("st2_2")[:, :, 0:T], ACT.Exp, scale=SC2
                    ).then_inc(act_done, 1)
                act.wait_ge(pe_done, at(it, "probs2_1", "st2_1"))
                act.activation(p0[1][:, 4:8, :], tiles("st2_1")[:, :, 0:T], ACT.Exp, scale=SC2
                    ).then_inc(act_done, 1)
                act.wait_ge(pe_done, at(it, "probs2_3", "st2_3"))
                act.activation(p1[1][0:T1, 0:4, :], tiles("st2_3", T1)[:, :, 0:T], ACT.Exp, scale=SC2
                    ).then_inc(act_done, 1)
                act.wait_ge(pe_done, at(it, "probs2_5", "st2_5"))
                act.activation(p1[1][0:T1, 8:12, :], tiles("st2_5", T1)[:, :, 0:T], ACT.Exp, scale=SC2
                    ).then_inc(act_done, 1)
                act.wait_ge(pe_done, at(it, "probs2_4", "st2_4"))
                act.activation(p1[1][0:T1, 4:8, :], tiles("st2_4", T1)[:, :, 0:T], ACT.Exp, scale=SC2
                    ).then_inc(act_done, 1)
                act.wait_ge(pe_done, at(it, "hwt_rows", "hwt", before=("qk2", "v2")))
                copy(hwt[:], slot["hwt"][:, 0:SL])
                copy(xtb[96:96 + E, :], slot["hwt"][0:E, SL:2 * SL])
                act.wait_ge(dve_done, at(it, "log2", "den2"))
                act.activation(lnd[1][:], den[1][:], ACT.Ln).then_inc(act_done, 1)
                act.wait_ge(act_done, at(it, "inverse2", "log2"))
                act.activation(inv[1][:], lnd[1][:], ACT.Exp, scale=-1.0).then_inc(act_done, 1)
                act.wait_ge(pe_done, at(it, "high2", "qk2"))
                act.wait_ge(dve_done, at(it, "high2", before=("rest2",)))
                act.wait_ge(landed["keep_high2"], landed_at(it, "high2", "keep_high2", age=1))
                copy(pieces[1][:, 0], tiles("qk2", GR)[:, :, 0:T])
                act.wait_ge(dve_done, at(it, "middle2", "rest2"))
                act.wait_ge(pool_done, at(it, "middle2", before=("low2",)))
                act.wait_ge(landed["keep_middle2"], landed_at(it, "middle2", "keep_middle2", age=1))
                copy(pieces[1][:, 1], rest[1][:])

        @block.vector
        def _(dve):
            def pooling(t):
                return dve.tensor_reduce(part[:, t, :], xa[:, t, :].rearrange("p (r j w) -> p j r w", r=P // 4, w=P),
                                         AX.XY, ALU.add)

            for tile, v in clears:
                dve.memset(tile[:], v).then_inc(prep_dve, 1)
            dve.wait_ge(const_ready, 1)
            dve.tensor_reduce(patch_mask[:], patch_c[:].rearrange("p c i -> p i c"), AX.X, ALU.add).then_inc(prep_dve, 1)
            dve.wait_ge(loaded, 16 * len(loads))
            dve.tensor_reduce(cen_sum[:], cen[:], AX.X, ALU.add).then_inc(prep_dve, 1)
            dve.wait_ge(prep_dve, PREP_DVE - 5)
            dve.tensor_scalar(cen_sum[:], cen_sum[:], 1.0 / D, None, ALU.mult).then_inc(prep_dve, 1)
            dve.wait_ge(prep_dve, PREP_DVE - 4)
            dve.tensor_scalar(cen[:], cen[:], cen_sum[:, 0:1], None, ALU.subtract).then_inc(prep_dve, 1)
            dve.wait_ge(prep_pe, 1)
            dve.tensor_copy(cen_t[:, 0, 0:C + 1], slots[0][:, 0:C + 1]).then_inc(prep_dve, 1)
            dve.tensor_copy(cen_t[0:D - 128, 1, 0:C + 1], slots[0][0:D - 128, SL:SL + C + 1]).then_inc(prep_dve, 1)
            dve.tensor_scalar(wb[96:96 + E, :], wb[96:96 + E, :], SCALING, None, ALU.mult).then_inc(prep_dve, 1)
            dve.wait_ge(prep_dve, PREP_DVE)
            dve.sem_inc(dve_done, HEAD_START * len(DVE_STEPS))
            dve.sem_inc(ready, 1)
            dve.wait_ge(ready, N_READY)

            with dve.Fori(0, N_IT) as it:
                dve.wait_ge(pe_done, at(it, "max1_2", "mx1_2"))
                dve.tensor_reduce(mx[0][0:T1, 1, 0:4], tiles("mx1_2", T1)[:, :, 0:T], AX.X, ALU.max
                    ).then_inc(dve_done, 1)
                dve.wait_ge(pe_done, at(it, "max1_1", "mx1_1"))
                dve.tensor_reduce(mx[0][:, 0, 8:12], slot["mx1_1"][:, 0:4 * T0].rearrange("p (h k) -> p h k", h=4),
                                  AX.X, ALU.max).then_inc(dve_done, 1)
                dve.wait_ge(pe_done, at(it, "max1_4", "mx1_4"))
                dve.tensor_reduce(mx[0][0:T1, 1, 8:12], tiles("mx1_4", T1)[:, :, 0:T], AX.X, ALU.max
                    ).then_inc(dve_done, 1)
                dve.wait_ge(pe_done, at(it, "max1_3", "mx1_3"))
                dve.tensor_reduce(mx[0][0:T1, 1, 4:8], tiles("mx1_3", T1)[:, :, 0:T], AX.X, ALU.max
                    ).then_inc(dve_done, 1)
                dve.wait_ge(pe_done, at(it, "max1_0", "mx1_0"))
                dve.tensor_reduce(mx[0][:, 0, 0:8], slot["mx1_0"][:, 0:8 * T0].rearrange("p (h k) -> p h k", h=8),
                                  AX.X, ALU.max).then_inc(dve_done, 1)
                dve.wait_ge(dve_done, at(it, "max_high1", "max1_0", "max1_1", "max1_2", "max1_3", "max1_4"))
                dve.wait_ge(pe_done, at(it, "max_high1", before=("mt1",)))
                hold(dve, "dve")
                dve.tensor_scalar(mxp[0][:, :, :, 0], mx[0][:].rearrange("p t (g j) -> p t g j", g=2), -1.0, None, ALU.mult
                    ).then_inc(dve_done, 1)
                dve.wait_ge(dve_done, at(it, "max_low1", "max_high1"))
                dve.scalar_tensor_tensor(mxp[0][:, :, :, 1], mx[0][:].rearrange("p t (g j) -> p t g j", g=2), -1.0,
                                         mxp[0][:, :, :, 0], ALU.mult, ALU.subtract).then_inc(dve_done, 1)
                dve.wait_ge(pe_done, at(it, "result", "out2"))
                dve.wait_ge(pool_done, at(it, "result", "hidden_kept"))
                dve.wait_ge(landed["store"], landed_at(it, "result", "store", age=1))
                dve.tensor_tensor(y[:], tiles("out2")[:, 0:2, 0:D], h1k[:], ALU.add).then_inc(dve_done, 1)
                dve.wait_ge(pool_done, at(it, "pooling1", "halves1", before=("rows1",)))
                pooling(1).then_inc(dve_done, 1)
                dve.wait_ge(pool_done, at(it, "pooling0", "halves0", before=("rows0",)))
                pooling(0).then_inc(dve_done, 1)
                dve.wait_ge(pool_done, at(it, "pooling2", "halves2", before=("rows2",)))
                pooling(2).then_inc(dve_done, 1)
                dve.wait_ge(pe_done, at(it, "max2_3", "mx2_3"))
                dve.tensor_reduce(mx[1][0:T1, 1, 0:4], tiles("mx2_3", T1)[:, :, 0:T], AX.X, ALU.max
                    ).then_inc(dve_done, 1)
                dve.wait_ge(pe_done, at(it, "max2_4", "mx2_4"))
                dve.tensor_reduce(mx[1][0:T1, 1, 4:8], tiles("mx2_4", T1)[:, :, 0:T], AX.X, ALU.max
                    ).then_inc(dve_done, 1)
                dve.wait_ge(pe_done, at(it, "den1", "av1"))
                hold(dve, "dve")
                dve.stream_shuffle(den[0][:], tiles("av1")[:, 0:3, 0:T], [DH + i % DH for i in range(32)]
                    ).then_inc(dve_done, 1)
                dve.wait_ge(pe_done, at(it, "max2_2", "mx2_2"))
                dve.tensor_reduce(mx[1][:, 0, 8:12], tiles("mx2_2")[:, :, 0:T], AX.X, ALU.max).then_inc(dve_done, 1)
                dve.wait_ge(pe_done, at(it, "max2_0", "mx2_0"))
                dve.tensor_reduce(mx[1][:, 0, 0:4], tiles("mx2_0")[:, :, 0:T], AX.X, ALU.max).then_inc(dve_done, 1)
                dve.wait_ge(act_done, at(it, "newton_a1", "inverse1"))
                dve.tensor_tensor(den[0][:], den[0][:], inv[0][:], ALU.mult).then_inc(dve_done, 1)
                dve.wait_ge(dve_done, at(it, "newton_b1", "newton_a1"))
                dve.scalar_tensor_tensor(inv[0][:], den[0][:], 2.0, inv[0][:], ALU.subtract, ALU.mult
                    ).then_inc(dve_done, 1)
                dve.wait_ge(pe_done, at(it, "prod", "gram", before=("var",)))
                dve.wait_ge(act_done, at(it, "prod", "pooled_rows"))
                dve.tensor_tensor(prod[0:C + 1, 0:T], slot["gram"][0:C + 1, 0:T], pt[0:C + 1, 0:T], ALU.mult
                    ).then_inc(dve_done, 1)
                dve.wait_ge(dve_done, at(it, "heads1", "newton_b1"))
                dve.wait_ge(pe_done, at(it, "heads1", before=("out1",)))
                dve.scalar_tensor_tensor(o_t[0][:, :, 0:T], tiles("av1")[:, 0:3, 0:T], -1.0, inv[0][:],
                                         ALU.mult, ALU.mult).then_inc(dve_done, 1)
                dve.wait_ge(pe_done, at(it, "variance", "var"))
                dve.wait_ge(pool_done, at(it, "variance", before=("deviation1",)))
                dve.tensor_scalar(tok_var[:], slot["var"][:, 0:2], EPS, None, ALU.add).then_inc(dve_done, 1)
                dve.wait_ge(pe_done, at(it, "max2_5", "mx2_5"))
                dve.tensor_reduce(mx[1][0:T1, 1, 8:12], tiles("mx2_5", T1)[:, :, 0:T], AX.X, ALU.max
                    ).then_inc(dve_done, 1)
                dve.wait_ge(pool_done, at(it, "deviation_cols", "deviation1"))
                dve.wait_ge(pe_done, at(it, "deviation_cols", before=("spread",)))
                dve.tensor_copy(rstd_tok[:, :, 0:C + 1], tok_var[:, :].unsqueeze(2).broadcast_to([128, 2, C + 1])
                    ).then_inc(dve_done, 1)
                dve.wait_ge(pe_done, at(it, "max2_1", "mx2_1"))
                dve.tensor_reduce(mx[1][:, 0, 4:8], tiles("mx2_1")[:, :, 0:T], AX.X, ALU.max).then_inc(dve_done, 1)
                dve.wait_ge(dve_done, at(it, "max_high2", "max2_0", "max2_1", "max2_2", "max2_3", "max2_4", "max2_5"))
                dve.wait_ge(pe_done, at(it, "max_high2", before=("mt2",)))
                hold(dve, "dve")
                dve.tensor_scalar(mxp[1][:, :, :, 0], mx[1][:].rearrange("p t (g j) -> p t g j", g=2), -1.0, None, ALU.mult
                    ).then_inc(dve_done, 1)
                dve.wait_ge(dve_done, at(it, "max_low2", "max_high2"))
                dve.scalar_tensor_tensor(mxp[1][:, :, :, 1], mx[1][:].rearrange("p t (g j) -> p t g j", g=2), -1.0,
                                         mxp[1][:, :, :, 0], ALU.mult, ALU.subtract).then_inc(dve_done, 1)
                dve.wait_ge(pe_done, at(it, "scaled", "spread", before=("qk1", "v1")))
                dve.tensor_tensor(ptn[0:NQ, 0:T], pt[0:NQ, 0:T], slot["spread"][0:NQ, 0:T], ALU.mult
                    ).then_inc(dve_done, 1)
                dve.wait_ge(act_done, at(it, "stats", "hidden"))
                for tt in range(2):
                    ins = dve.bn_stats(bst[:, tt, :], h1[:, tt, :])
                ins.then_inc(dve_done, 1)
                dve.wait_ge(dve_done, at(it, "moments", "stats"))
                hold(dve, "dve")
                for tt in range(2):
                    ins = dve.bn_aggr(bag[:, tt, :], bst[:, tt, :])
                ins.then_inc(dve_done, 1)
                dve.wait_ge(dve_done, at(it, "token_var", "moments"))
                dve.tensor_scalar(rstd[:], bag[:, :, 1:2], EPS, None, ALU.add).then_inc(dve_done, 1)
                dve.wait_ge(pool_done, at(it, "normal", "deviation2"))
                dve.wait_ge(pe_done, at(it, "normal", before=("xt",)))
                for tt in range(2):
                    ins = dve.tensor_scalar(xh[:, tt, :], h1[:, tt, :], bag[:, tt, 0:1], rstd[:, tt, :], ALU.subtract, ALU.mult)
                ins.then_inc(dve_done, 1)
                dve.wait_ge(act_done, at(it, "rest1", "high1", before=("middle1",)))
                dve.wait_ge(pool_done, at(it, "rest1", before=("low1",)))
                dve.tensor_tensor(rest[0][:], tiles("qk1", GR)[:, :, 0:T], pieces[0][:, 0], ALU.subtract
                    ).then_inc(dve_done, 1)
                dve.wait_ge(pe_done, at(it, "rmax", "route"))
                dve.tensor_reduce(rm[:], tiles("route")[:, 0:2, 128:128 + E], AX.X, ALU.max).then_inc(dve_done, 1)
                dve.wait_ge(dve_done, at(it, "rsub", "rmax"))
                dve.wait_ge(act_done, at(it, "rsub", before=("rexp",)))
                dve.tensor_tensor(rl[:], tiles("route")[:, 0:2, 128:128 + E], rm[:, :].unsqueeze(2).broadcast_to([128, 2, E]),
                                  ALU.subtract).then_inc(dve_done, 1)
                dve.wait_ge(act_done, at(it, "rsum", "rexp"))
                dve.tensor_reduce(rs[:], re[:], AX.X, ALU.add).then_inc(dve_done, 1)
                dve.wait_ge(dve_done, at(it, "rinv", "rsum"))
                dve.reciprocal(ri[:], rs[:]).then_inc(dve_done, 1)
                dve.wait_ge(dve_done, at(it, "rprob", "rinv"))
                dve.tensor_tensor(rp[:], re[:], ri[:, :].unsqueeze(2).broadcast_to([128, 2, E]), ALU.mult
                    ).then_inc(dve_done, 1)
                dve.wait_ge(dve_done, at(it, "rtop", "rprob"))
                hold(dve, "dve")
                for tt in range(2):
                    ins = dve.max(rt[:, tt, :], rp[:, tt, :])
                ins.then_inc(dve_done, 1)
                dve.wait_ge(dve_done, at(it, "ridx", "rtop"))
                hold(dve, "dve")
                for tt in range(2):
                    ins = dve.max_index(rx_u[:, tt, :], rt[:, tt, :], rp[:, tt, :])
                ins.then_inc(dve_done, 1)
                dve.wait_ge(dve_done, at(it, "ridxf", "ridx"))
                dve.tensor_copy(rx_f[:], rx_u[:]).then_inc(dve_done, 1)
                dve.wait_ge(dve_done, at(it, "rpick", "ridxf"))
                for k in range(2):
                    for tt in range(2):
                        ins = dve.tensor_scalar(picked[:, k, tt, :], iota_f[:], rx_f[:, tt, k:k + 1], rt[:, tt, k:k + 1],
                                                ALU.is_equal, ALU.mult)
                ins.then_inc(dve_done, 1)
                dve.wait_ge(dve_done, at(it, "rcomb", "rpick"))
                dve.wait_ge(pe_done, at(it, "rcomb", before=("hwt",)))
                dve.tensor_tensor(c2[:], picked[:, 0], picked[:, 1], ALU.add).then_inc(dve_done, 1)
                dve.wait_ge(dve_done, at(it, "weighted", "rcomb"))
                dve.tensor_tensor(hw[:], tiles("route")[:, 0:2, 0:128].rearrange("p t (e r) -> p t e r", e=E),
                                  c2[:, :, :].unsqueeze(3).broadcast_to([128, 2, E, RANK]), ALU.mult
                                      ).then_inc(dve_done, 1)
                dve.wait_ge(pe_done, at(it, "den2", "av2"))
                hold(dve, "dve")
                dve.stream_shuffle(den[1][:], tiles("av2")[:, 0:3, 0:T], [DH + i % DH for i in range(32)]
                    ).then_inc(dve_done, 1)
                dve.wait_ge(act_done, at(it, "newton_a2", "inverse2"))
                dve.tensor_tensor(den[1][:], den[1][:], inv[1][:], ALU.mult).then_inc(dve_done, 1)
                dve.wait_ge(dve_done, at(it, "newton_b2", "newton_a2"))
                dve.scalar_tensor_tensor(inv[1][:], den[1][:], 2.0, inv[1][:], ALU.subtract, ALU.mult
                    ).then_inc(dve_done, 1)
                dve.wait_ge(dve_done, at(it, "heads2", "newton_b2"))
                dve.wait_ge(pe_done, at(it, "heads2", before=("out2",)))
                dve.scalar_tensor_tensor(o_t[1][:, :, 0:T], tiles("av2")[:, 0:3, 0:T], -1.0, inv[1][:],
                                         ALU.mult, ALU.mult).then_inc(dve_done, 1)
                dve.wait_ge(act_done, at(it, "rest2", "high2", before=("middle2",)))
                dve.wait_ge(pool_done, at(it, "rest2", before=("low2",)))
                dve.tensor_tensor(rest[1][:], tiles("qk2", GR)[:, :, 0:T], pieces[1][:, 0], ALU.subtract
                    ).then_inc(dve_done, 1)


_INS = ['x', 'cls_tok', 'L0_tok_channel_weights', 'L0_attn_w_attn', 'L0_attn_b_attn', 'L0_attn_w_proj',
        'L0_attn_b_proj', 'L0_ffn_Wg', 'L0_ffn_bg', 'L0_ffn_Wqkv', 'L0_ffn_bqkv', 'L0_ffn_Wproj',
        'L0_ffn_bproj', 'L0_ffn_A', 'L0_ffn_ba', 'L0_ffn_Bm', 'L0_ffn_bb']
_OUTS = [((64, 197, 192), 'float32')]


def kernel(**inputs):
    import numpy as _np
    import concourse.bacc as _bacc
    from concourse import mybir as _mybir
    from concourse.bass_utils import run_bass_kernel_spmd as _run

    nc = _bacc.Bacc("TRN2", target_bir_lowering=False, num_devices=1)
    arrays, args = {}, []
    for name in _INS:
        a = _np.ascontiguousarray(inputs[name])
        arrays[f"in_{name}_dram"] = a
        args.append(nc.dram_tensor(f"in_{name}_dram", a.shape, _mybir.dt.from_np(a.dtype), kind="ExternalInput").ap())
    for i, (shape, dtype) in enumerate(_OUTS):
        dt = _mybir.dt.from_np(_np.dtype(dtype))
        args.append(nc.dram_tensor(f"out_{i}_dram", shape, dt, kind="ExternalOutput").ap())
    build(nc, *args)
    r = _run(nc, [arrays], core_ids=[0])
    got = tuple(r.results[0][f"out_{i}_dram"] for i in range(len(_OUTS)))
    return got[0]
```
